# Optimizing a Trainium2 kernel written in Bass

```python
import numpy as np
import jax
import jax.numpy as jnp

def _softmax(x, axis=-1):
    return jax.nn.softmax(x, axis=axis)

def _gelu(x):
    return jax.nn.gelu(x, approximate=True)

def _silu(x):
    return jax.nn.silu(x)

def _sigmoid(x):
    return jax.nn.sigmoid(x)

def _layernorm(x, axis=-1, eps=1e-05):
    m = jnp.mean(x, axis=axis, keepdims=True)
    v = jnp.var(x, axis=axis, keepdims=True)
    return (x - m) / jnp.sqrt(v + eps)

def _scatter_add(tgt, idx, src, axis=0):
    return tgt.at[idx].add(src)

def _segment_sum(src, seg, n):
    return jax.ops.segment_sum(src, seg, n)
kernel_name = 'mk_adaln_ffn_d4_seqx_r8_d1aebe'

def setup_inputs(seed: int=0):
    np.random.seed(seed)
    _w = jnp.asarray

    def _rec_inputs():
        import jax
        import jax.numpy as jnp
        _rk = jax.random.key(seed)
        x = -0.0003929 + 0.9999 * jax.random.normal(jax.random.fold_in(_rk, 1), (64, 32, 256), jnp.float32)
        _lenS = 32 - jax.random.randint(jax.random.fold_in(_rk, 7), (64,), 0, max(1, 32 // 4) + 1, jnp.int32)
        _lenS2 = 32 - jax.random.randint(jax.random.fold_in(_rk, 8), (64,), 0, max(1, 32 // 4) + 1, jnp.int32)
        cond_1 = jax.random.uniform(jax.random.fold_in(_rk, 11), (64, 1), jnp.float32, 0.0, 1.37214)
        itok_B_0_15 = jax.random.randint(jax.random.fold_in(_rk, 12), (64,), 0, 16, jnp.int32)
        itok_B_0_6 = jax.random.randint(jax.random.fold_in(_rk, 13), (64,), 0, 7, jnp.int32)
        itok_B_1_198 = jax.random.randint(jax.random.fold_in(_rk, 14), (64,), 1, 199, jnp.int32)
        return (x, cond_1, itok_B_0_15, itok_B_0_6, itok_B_1_198)
    x, cond_1, itok_B_0_15, itok_B_0_6, itok_B_1_198 = _rec_inputs()

    def _L0_cond_setup():
        import jax, jax.numpy as jnp
        import numpy as np
        B, S, D_MODEL, NHEAD = (4, 256, 256, 16)
        HEAD_DIM = D_MODEL // NHEAD
        key = jax.random.key(seed)
        ks = jax.random.split(key, 6)
        scale = 1.0 / np.sqrt(D_MODEL)
        return {'hidden_states': jax.random.normal(ks[0], (B, S, D_MODEL), dtype=jnp.float32), 'attention_precision': jax.random.uniform(ks[1], (B, 1, 1), dtype=jnp.float32, minval=0.5, maxval=2.0), 'Wq': jax.random.normal(ks[2], (D_MODEL, D_MODEL), dtype=jnp.float32) * scale, 'Wk': jax.random.normal(ks[3], (D_MODEL, D_MODEL), dtype=jnp.float32) * scale, 'Wv': jax.random.normal(ks[4], (D_MODEL, D_MODEL), dtype=jnp.float32) * scale, 'Wo': jax.random.normal(ks[5], (D_MODEL, D_MODEL), dtype=jnp.float32) * scale}
    _L0_cond_all = _L0_cond_setup()
    _L0_cond_in = {k: v for k, v in _L0_cond_all.items() if k in ('Wq', 'Wk', 'Wv', 'Wo')}
    del _L0_cond_all

    def _L0_ffn_setup():
        import math
        import jax, jax.numpy as jnp
        import numpy as np
        NUM_EXPERTS = 8
        TOP_K = 2
        CAP_FACTOR = 1.25
        D_MODEL = 256
        D_HIDDEN = 1024
        B, S = (4, 256)
        key = jax.random.key(seed)
        ks = jax.random.split(key, 6)
        x = jax.random.normal(ks[0], (B, S, D_MODEL), dtype=jnp.float32)
        gating_w = jax.random.normal(ks[1], (D_MODEL, NUM_EXPERTS), dtype=jnp.float32) * (1.0 / math.sqrt(D_MODEL))
        w1 = jax.random.normal(ks[2], (NUM_EXPERTS, D_MODEL, D_HIDDEN), dtype=jnp.float32) * (1.0 / math.sqrt(D_MODEL))
        b1 = jnp.zeros((NUM_EXPERTS, D_HIDDEN), dtype=jnp.float32)
        w2 = jax.random.normal(ks[3], (NUM_EXPERTS, D_HIDDEN, D_MODEL), dtype=jnp.float32) * (1.0 / math.sqrt(D_HIDDEN))
        b2 = jnp.zeros((NUM_EXPERTS, D_MODEL), dtype=jnp.float32)
        return {'x': x, 'gating_w': gating_w, 'w1': w1, 'b1': b1, 'w2': w2, 'b2': b2}
    _L0_ffn_all = _L0_ffn_setup()
    _L0_ffn_in = {k: v for k, v in _L0_ffn_all.items() if k in ('gating_w', 'w1', 'b1', 'w2', 'b2')}
    del _L0_ffn_all

    def _L1_cond_setup():
        import jax, jax.numpy as jnp
        import numpy as np
        key = jax.random.key(seed)
        k1, k2, k3, k4 = jax.random.split(key, 4)
        B, S, IN, OUT, E = (64, 32, 256, 256, 16)
        bound = 1.0 / np.sqrt(IN)
        x = jax.random.normal(k1, (B, S, IN), dtype=jnp.float32)
        idx = jax.random.randint(k2, (B,), 0, E, dtype=jnp.int64)
        W = jax.random.uniform(k3, (E, IN, OUT), dtype=jnp.float32, minval=-bound, maxval=bound)
        b = jnp.full((E, OUT), 0.1, dtype=jnp.float32)
        return {'x': x, 'id': idx, 'W': W, 'b': b}
    _L1_cond_all = _L1_cond_setup()
    _L1_cond_in = {k: v for k, v in _L1_cond_all.items() if k in ('W', 'b')}
    del _L1_cond_all

    def _L1_ffn_setup():
        import jax, jax.numpy as jnp
        import numpy as np
        NUM_EXPERTS = 32
        TOP_K = 8
        SELECT_TOP_K = 4
        THRESHOLD = 0.5
        HIDDEN = 256
        D_FF = 96

        def _moe_forward(hidden_states, gate_weight, gate_up_proj, down_proj, similarity):
            B, S_len, H = hidden_states.shape
            E, K, Ssel = (NUM_EXPERTS, TOP_K, SELECT_TOP_K)
            x = hidden_states.reshape(-1, H)
            router_logits = x @ gate_weight.T
            router_probs = jax.nn.softmax(router_logits.astype(jnp.float32), axis=-1).astype(router_logits.dtype)
            router_top_value, router_indices = jax.lax.top_k(router_probs, K)
            routing_weights = router_top_value / jnp.clip(jnp.sum(router_top_value, axis=-1, keepdims=True), 1e-12, None)
            sim = similarity.astype(jnp.float32)
            sim = sim.at[jnp.arange(E), jnp.arange(E)].set(1.0)
            prim = router_indices[:, :Ssel]
            sec = router_indices[:, Ssel:]
            sim_cand = sim[sec[:, :, None], prim[:, None, :]]
            best_sim = jnp.max(sim_cand, axis=-1)
            best_i = jnp.argmax(sim_cand, axis=-1)
            prim_rep = jnp.broadcast_to(prim[:, None, :], sim_cand.shape)
            best_primary = jnp.take_along_axis(prim_rep, best_i[..., None], axis=-1)[..., 0]
            new_sec = jnp.where(best_sim < THRESHOLD, sec, best_primary) if THRESHOLD > 0.0 else best_primary
            rerouted_indices = jnp.concatenate([prim, new_sec], axis=1)
            combine = jnp.sum(jax.nn.one_hot(rerouted_indices, E, dtype=routing_weights.dtype) * routing_weights[..., None], axis=1)

            def expert_step(y, params):
                wgu, wd, cw = params
                gu = x @ wgu.T
                g, u = jnp.split(gu, 2, axis=-1)
                h = jax.nn.silu(g) * u
                y = y + h @ wd.T * cw[:, None]
                return (y, None)
            y0 = jnp.zeros_like(x)
            y, _ = jax.lax.scan(expert_step, y0, (gate_up_proj, down_proj, combine.T))
            return y.reshape(B, S_len, H)
        key = jax.random.key(seed)
        ks = jax.random.split(key, 5)
        hidden_states = jax.random.normal(ks[0], (4, 256, HIDDEN), dtype=jnp.float32)
        gate_weight = jax.random.normal(ks[1], (NUM_EXPERTS, HIDDEN), dtype=jnp.float32) * 0.02
        gate_up_proj = jax.random.normal(ks[2], (NUM_EXPERTS, 2 * D_FF, HIDDEN), dtype=jnp.float32) * 0.02
        down_proj = jax.random.normal(ks[3], (NUM_EXPERTS, HIDDEN, D_FF), dtype=jnp.float32) * 0.02
        similarity = jax.random.uniform(ks[4], (NUM_EXPERTS, NUM_EXPERTS), dtype=jnp.float32)
        return {'hidden_states': hidden_states, 'gate_weight': gate_weight, 'gate_up_proj': gate_up_proj, 'down_proj': down_proj, 'similarity': similarity}
    _L1_ffn_all = _L1_ffn_setup()
    _L1_ffn_in = {k: v for k, v in _L1_ffn_all.items() if k in ('gate_weight', 'gate_up_proj', 'down_proj', 'similarity')}
    del _L1_ffn_all

    def _L2_cond_setup():
        import jax, jax.numpy as jnp
        import numpy as np
        B, T, D_IN, D_OUT = (16, 256, 256, 256)
        N_ADAPTERS, RANK = (8, 16)
        key = jax.random.key(seed)
        k_x, k_w, k_a, k_b, k_s, k_idx = jax.random.split(key, 6)
        x = jax.random.normal(k_x, (B, T, D_IN), dtype=jnp.float32)
        W = jax.random.normal(k_w, (D_OUT, D_IN), dtype=jnp.float32) * (1.0 / np.sqrt(D_IN))
        A = jax.random.normal(k_a, (N_ADAPTERS, RANK, D_IN), dtype=jnp.float32) * 0.02
        Bm = jax.random.normal(k_b, (N_ADAPTERS, D_OUT, RANK), dtype=jnp.float32) * 0.02
        scalings = jnp.ones((N_ADAPTERS,), dtype=jnp.float32)
        adapter_idx = jax.random.randint(k_idx, (B,), 0, N_ADAPTERS, dtype=jnp.int32)
        return {'x': x, 'W': W, 'A': A, 'Bm': Bm, 'scalings': scalings, 'adapter_idx': adapter_idx}
    _L2_cond_all = _L2_cond_setup()
    _L2_cond_in = {k: v for k, v in _L2_cond_all.items() if k in ('W', 'A', 'Bm', 'scalings')}
    del _L2_cond_all

    def _L2_ffn_setup():
        import jax, jax.numpy as jnp
        import numpy as np
        EPS_NORM = 1e-06
        EPS_SCALE = 1e-05

        def _rmsnorm(x, g):
            rms = jnp.sqrt(jnp.mean(x * x, axis=-1, keepdims=True) + EPS_NORM)
            return x / rms * g

        def _activation_quant(x):
            scale = 127.0 / jnp.clip(jnp.max(jnp.abs(x), axis=-1, keepdims=True), EPS_SCALE)
            return jnp.clip(jnp.round(x * scale), -128, 127) / scale

        def _weight_quant(w):
            scale = 1.0 / jnp.clip(jnp.mean(jnp.abs(w)), EPS_SCALE)
            return jnp.clip(jnp.round(w * scale), -1, 1) / scale

        def _bitlinear(x, w, g):
            x_norm = _rmsnorm(x, g)
            x_q = x_norm + jax.lax.stop_gradient(_activation_quant(x_norm) - x_norm)
            w_q = w + jax.lax.stop_gradient(_weight_quant(w) - w)
            return jnp.einsum('bsi,oi->bso', x_q, w_q)
        key = jax.random.key(seed)
        k_x, k_w1, k_w2 = jax.random.split(key, 3)
        d_model, d_ff = (256, 1024)
        B, S = (4, 256)
        x = jax.random.normal(k_x, (B, S, d_model), dtype=jnp.float32)
        w1 = jax.random.normal(k_w1, (d_ff, d_model), dtype=jnp.float32) * (1.0 / np.sqrt(d_model))
        w2 = jax.random.normal(k_w2, (d_model, d_ff), dtype=jnp.float32) * (1.0 / np.sqrt(d_ff))
        g1 = jnp.ones((d_model,), dtype=jnp.float32)
        g2 = jnp.ones((d_ff,), dtype=jnp.float32)
        return {'x': x, 'w1': w1, 'g1': g1, 'w2': w2, 'g2': g2}
    _L2_ffn_all = _L2_ffn_setup()
    _L2_ffn_in = {k: v for k, v in _L2_ffn_all.items() if k in ('w1', 'g1', 'w2', 'g2')}
    del _L2_ffn_all

    def _L3_cond_setup():
        import jax, jax.numpy as jnp
        import numpy as np
        B, C, T = (128, 32, 256)
        S, D = (200, 32)
        key = jax.random.key(seed)
        k1, k2, k3 = jax.random.split(key, 3)
        x = jax.random.normal(k1, (B, C, T), dtype=jnp.float32)
        conditions = jax.random.randint(k2, (B,), 0, S, dtype=jnp.int64)
        weights = jax.random.normal(k3, (S, C, D), dtype=jnp.float32) / jnp.sqrt(jnp.float32(C))
        return {'x': x, 'conditions': conditions, 'weights': weights}
    _L3_cond_all = _L3_cond_setup()
    _L3_cond_in = {k: v for k, v in _L3_cond_all.items() if k in ('weights',)}
    del _L3_cond_all

    def _L3_ffn_setup():
        import jax, jax.numpy as jnp
        import numpy as np
        NUM_ROUTED = 7
        TOP_K = 3
        D = 256
        H = 256
        B, S = (4, 256)

        def _expert_ffn(x, w1, wg, w2):
            return jax.nn.silu(x @ w1) * (x @ wg) @ w2
        key = jax.random.key(seed)
        ks = jax.random.split(key, 8)
        s = 0.02
        return {'x': jax.random.normal(ks[0], (B, S, D), jnp.float32), 'W1': jax.random.normal(ks[1], (NUM_ROUTED, D, H), jnp.float32) * s, 'Wg': jax.random.normal(ks[2], (NUM_ROUTED, D, H), jnp.float32) * s, 'W2': jax.random.normal(ks[3], (NUM_ROUTED, H, D), jnp.float32) * s, 'Ws1': jax.random.normal(ks[4], (D, H), jnp.float32) * s, 'Wsg': jax.random.normal(ks[5], (D, H), jnp.float32) * s, 'Ws2': jax.random.normal(ks[6], (H, D), jnp.float32) * s, 'gate_w': jax.random.normal(ks[7], (D, NUM_ROUTED), jnp.float32) * s, 'gate_b': jnp.zeros((NUM_ROUTED,), jnp.float32), 'biases': jnp.zeros((NUM_ROUTED,), jnp.float32)}
    _L3_ffn_all = _L3_ffn_setup()
    _L3_ffn_in = {k: v for k, v in _L3_ffn_all.items() if k in ('W1', 'Wg', 'W2', 'Ws1', 'Wsg', 'Ws2', 'gate_w', 'gate_b', 'biases')}
    del _L3_ffn_all
    return {'x': x, 'cond_1': cond_1, 'itok_B_0_15': itok_B_0_15, 'itok_B_0_6': itok_B_0_6, 'itok_B_1_198': itok_B_1_198, 'L0_cond_Wq': _L0_cond_in['Wq'], 'L0_cond_Wk': _L0_cond_in['Wk'], 'L0_cond_Wv': _L0_cond_in['Wv'], 'L0_cond_Wo': _L0_cond_in['Wo'], 'L0_ffn_gating_w': _L0_ffn_in['gating_w'], 'L0_ffn_w1': _L0_ffn_in['w1'], 'L0_ffn_b1': _L0_ffn_in['b1'], 'L0_ffn_w2': _L0_ffn_in['w2'], 'L0_ffn_b2': _L0_ffn_in['b2'], 'L1_cond_W': _L1_cond_in['W'], 'L1_cond_b': _L1_cond_in['b'], 'L1_ffn_gate_weight': _L1_ffn_in['gate_weight'], 'L1_ffn_gate_up_proj': _L1_ffn_in['gate_up_proj'], 'L1_ffn_down_proj': _L1_ffn_in['down_proj'], 'L1_ffn_similarity': _L1_ffn_in['similarity'], 'L2_cond_W': _L2_cond_in['W'], 'L2_cond_A': _L2_cond_in['A'], 'L2_cond_Bm': _L2_cond_in['Bm'], 'L2_cond_scalings': _L2_cond_in['scalings'], 'L2_ffn_w1': _L2_ffn_in['w1'], 'L2_ffn_g1': _L2_ffn_in['g1'], 'L2_ffn_w2': _L2_ffn_in['w2'], 'L2_ffn_g2': _L2_ffn_in['g2'], 'L3_cond_weights': _L3_cond_in['weights'], 'L3_ffn_W1': _L3_ffn_in['W1'], 'L3_ffn_Wg': _L3_ffn_in['Wg'], 'L3_ffn_W2': _L3_ffn_in['W2'], 'L3_ffn_Ws1': _L3_ffn_in['Ws1'], 'L3_ffn_Wsg': _L3_ffn_in['Wsg'], 'L3_ffn_Ws2': _L3_ffn_in['Ws2'], 'L3_ffn_gate_w': _L3_ffn_in['gate_w'], 'L3_ffn_gate_b': _L3_ffn_in['gate_b'], 'L3_ffn_biases': _L3_ffn_in['biases']}

def reference(x, cond_1, itok_B_0_15, itok_B_0_6, itok_B_1_198, L0_cond_Wq, L0_cond_Wk, L0_cond_Wv, L0_cond_Wo, L0_ffn_gating_w, L0_ffn_w1, L0_ffn_b1, L0_ffn_w2, L0_ffn_b2, L1_cond_W, L1_cond_b, L1_ffn_gate_weight, L1_ffn_gate_up_proj, L1_ffn_down_proj, L1_ffn_similarity, L2_cond_W, L2_cond_A, L2_cond_Bm, L2_cond_scalings, L2_ffn_w1, L2_ffn_g1, L2_ffn_w2, L2_ffn_g2, L3_cond_weights, L3_ffn_W1, L3_ffn_Wg, L3_ffn_W2, L3_ffn_Ws1, L3_ffn_Wsg, L3_ffn_Ws2, L3_ffn_gate_w, L3_ffn_gate_b, L3_ffn_biases):
    import jax
    import jax.numpy as jnp

    def _L0_cond_ref(hidden_states, attention_precision, Wq, Wk, Wv, Wo):
        import jax, jax.numpy as jnp
        import numpy as np
        B, S, D_MODEL, NHEAD = (4, 256, 256, 16)
        HEAD_DIM = D_MODEL // NHEAD
        b, s, _ = hidden_states.shape

        def proj(x, W):
            y = jnp.einsum('bsd,ed->bse', x, W)
            return y.reshape(b, s, NHEAD, HEAD_DIM).transpose(0, 2, 1, 3)
        q = proj(hidden_states, Wq)
        k = proj(hidden_states, Wk)
        v = proj(hidden_states, Wv)
        beta = jnp.minimum(attention_precision, 4.0)[:, None]
        q = q * beta
        scores = jnp.einsum('bhqd,bhkd->bhqk', q, k) / np.sqrt(HEAD_DIM)
        causal = jnp.tril(jnp.ones((s, s), dtype=bool))
        scores = jnp.where(causal, scores, jnp.finfo(scores.dtype).min)
        attn = jax.nn.softmax(scores, axis=-1)
        out = jnp.einsum('bhqk,bhkd->bhqd', attn, v)
        out = out.transpose(0, 2, 1, 3).reshape(b, s, D_MODEL)
        return jnp.einsum('bsd,ed->bse', out, Wo)

    def _L0_ffn_ref(x, gating_w, w1, b1, w2, b2):
        import math
        import jax, jax.numpy as jnp
        import numpy as np
        NUM_EXPERTS = 8
        TOP_K = 2
        CAP_FACTOR = 1.25
        D_MODEL = 256
        D_HIDDEN = 1024
        B, S = (4, 256)
        b, s, d = x.shape
        x_flat = x.reshape(-1, d)
        T = x_flat.shape[0]
        num_items = T * TOP_K
        capacity = int(math.ceil(num_items / NUM_EXPERTS * CAP_FACTOR))
        gates = jax.nn.softmax(x_flat @ gating_w, axis=-1)
        topk_w, topk_idx = jax.lax.top_k(gates, TOP_K)
        norm_w = topk_w / (jnp.sum(topk_w, axis=-1, keepdims=True) + 1e-08)
        flat_e = topk_idx.reshape(-1)
        flat_t = jnp.repeat(jnp.arange(T, dtype=jnp.int32), TOP_K)
        flat_w = norm_w.reshape(-1)
        onehot = (flat_e[:, None] == jnp.arange(NUM_EXPERTS)[None, :]).astype(jnp.int32)
        pos_all = jnp.cumsum(onehot, axis=0) - 1
        position = jnp.take_along_axis(pos_all, flat_e[:, None].astype(jnp.int32), axis=1)[:, 0]
        valid = position < capacity
        pos_scatter = jnp.where(valid, position, capacity)
        buf = jnp.zeros((NUM_EXPERTS, capacity, d), dtype=x.dtype)
        buf = buf.at[flat_e, pos_scatter].set(x_flat[flat_t], mode='drop')
        h = jnp.maximum(jnp.einsum('ecd,edh->ech', buf, w1) + b1[:, None, :], 0.0)
        out_e = jnp.einsum('ech,ehd->ecd', h, w2) + b2[:, None, :]
        pos_gather = jnp.minimum(position, capacity - 1)
        gathered = out_e[flat_e, pos_gather]
        w_eff = jnp.where(valid, flat_w, 0.0)
        out_flat = jnp.zeros_like(x_flat).at[flat_t].add(gathered * w_eff[:, None])
        return out_flat.reshape(b, s, d)

    def _L1_cond_ref(x, id, W, b):
        import jax, jax.numpy as jnp
        import numpy as np
        Wg = W[id]
        bg = b[id]
        out = jnp.einsum('bsi,bio->bso', x, Wg) + bg[:, None, :]
        return out

    def _L1_ffn_ref(hidden_states, gate_weight, gate_up_proj, down_proj, similarity):
        import jax, jax.numpy as jnp
        import numpy as np
        NUM_EXPERTS = 32
        TOP_K = 8
        SELECT_TOP_K = 4
        THRESHOLD = 0.5
        HIDDEN = 256
        D_FF = 96

        def _moe_forward(hidden_states, gate_weight, gate_up_proj, down_proj, similarity):
            B, S_len, H = hidden_states.shape
            E, K, Ssel = (NUM_EXPERTS, TOP_K, SELECT_TOP_K)
            x = hidden_states.reshape(-1, H)
            router_logits = x @ gate_weight.T
            router_probs = jax.nn.softmax(router_logits.astype(jnp.float32), axis=-1).astype(router_logits.dtype)
            router_top_value, router_indices = jax.lax.top_k(router_probs, K)
            routing_weights = router_top_value / jnp.clip(jnp.sum(router_top_value, axis=-1, keepdims=True), 1e-12, None)
            sim = similarity.astype(jnp.float32)
            sim = sim.at[jnp.arange(E), jnp.arange(E)].set(1.0)
            prim = router_indices[:, :Ssel]
            sec = router_indices[:, Ssel:]
            sim_cand = sim[sec[:, :, None], prim[:, None, :]]
            best_sim = jnp.max(sim_cand, axis=-1)
            best_i = jnp.argmax(sim_cand, axis=-1)
            prim_rep = jnp.broadcast_to(prim[:, None, :], sim_cand.shape)
            best_primary = jnp.take_along_axis(prim_rep, best_i[..., None], axis=-1)[..., 0]
            new_sec = jnp.where(best_sim < THRESHOLD, sec, best_primary) if THRESHOLD > 0.0 else best_primary
            rerouted_indices = jnp.concatenate([prim, new_sec], axis=1)
            combine = jnp.sum(jax.nn.one_hot(rerouted_indices, E, dtype=routing_weights.dtype) * routing_weights[..., None], axis=1)

            def expert_step(y, params):
                wgu, wd, cw = params
                gu = x @ wgu.T
                g, u = jnp.split(gu, 2, axis=-1)
                h = jax.nn.silu(g) * u
                y = y + h @ wd.T * cw[:, None]
                return (y, None)
            y0 = jnp.zeros_like(x)
            y, _ = jax.lax.scan(expert_step, y0, (gate_up_proj, down_proj, combine.T))
            return y.reshape(B, S_len, H)
        return _moe_forward(hidden_states, gate_weight, gate_up_proj, down_proj, similarity)

    def _L2_cond_ref(x, W, A, Bm, scalings, adapter_idx):
        import jax, jax.numpy as jnp
        import numpy as np
        B, T, D_IN, D_OUT = (16, 256, 256, 256)
        N_ADAPTERS, RANK = (8, 16)
        H = jnp.einsum('btd,od->bto', x, W)
        A_b = A[adapter_idx]
        B_b = Bm[adapter_idx]
        s_b = scalings[adapter_idx]
        xa = jnp.einsum('btd,brd->btr', x, A_b)
        delta = jnp.einsum('btr,bor->bto', xa, B_b)
        delta = jax.lax.stop_gradient(delta * s_b[:, None, None])
        return H + delta

    def _L2_ffn_ref(x, w1, g1, w2, g2):
        import jax, jax.numpy as jnp
        import numpy as np
        EPS_NORM = 1e-06
        EPS_SCALE = 1e-05

        def _rmsnorm(x, g):
            rms = jnp.sqrt(jnp.mean(x * x, axis=-1, keepdims=True) + EPS_NORM)
            return x / rms * g

        def _activation_quant(x):
            scale = 127.0 / jnp.clip(jnp.max(jnp.abs(x), axis=-1, keepdims=True), EPS_SCALE)
            return jnp.clip(jnp.round(x * scale), -128, 127) / scale

        def _weight_quant(w):
            scale = 1.0 / jnp.clip(jnp.mean(jnp.abs(w)), EPS_SCALE)
            return jnp.clip(jnp.round(w * scale), -1, 1) / scale

        def _bitlinear(x, w, g):
            x_norm = _rmsnorm(x, g)
            x_q = x_norm + jax.lax.stop_gradient(_activation_quant(x_norm) - x_norm)
            w_q = w + jax.lax.stop_gradient(_weight_quant(w) - w)
            return jnp.einsum('bsi,oi->bso', x_q, w_q)
        h = _bitlinear(x, w1, g1)
        h = jnp.square(jax.nn.relu(h))
        return _bitlinear(h, w2, g2)

    def _L3_cond_ref(x, conditions, weights):
        import jax, jax.numpy as jnp
        import numpy as np
        B, C, T = (128, 32, 256)
        S, D = (200, 32)
        w = weights[conditions]
        return jnp.einsum('bct,bcd->bdt', x, w)

    def _L3_ffn_ref(x, W1, Wg, W2, Ws1, Wsg, Ws2, gate_w, gate_b, biases):
        import jax, jax.numpy as jnp
        import numpy as np
        NUM_ROUTED = 7
        TOP_K = 3
        D = 256
        H = 256
        B, S = (4, 256)

        def _expert_ffn(x, w1, wg, w2):
            return jax.nn.silu(x @ w1) * (x @ wg) @ w2
        output = _expert_ffn(x, Ws1, Wsg, Ws2)
        gate_logits = x @ gate_w + gate_b
        gate_probas = jax.nn.softmax(gate_logits, axis=-1)
        biased_probas = gate_probas + biases
        _, topk_idxs = jax.lax.top_k(biased_probas, TOP_K)
        topk_probas = jnp.take_along_axis(gate_probas, topk_idxs, axis=-1)
        topk_probas = topk_probas / jnp.sum(topk_probas, axis=-1, keepdims=True)
        for e in range(NUM_ROUTED):
            w_e = jnp.sum(topk_probas * (topk_idxs == e), axis=-1)
            output = output + _expert_ffn(x, W1[e], Wg[e], W2[e]) * w_e[..., None]
        return output
    x = x + _L0_ffn_ref(_L0_cond_ref(x, cond_1[:, None, :], L0_cond_Wq, L0_cond_Wk, L0_cond_Wv, L0_cond_Wo), L0_ffn_gating_w, L0_ffn_w1, L0_ffn_b1, L0_ffn_w2, L0_ffn_b2)
    x = x + _L1_ffn_ref(_L1_cond_ref(x, itok_B_0_15, L1_cond_W, L1_cond_b), L1_ffn_gate_weight, L1_ffn_gate_up_proj, L1_ffn_down_proj, L1_ffn_similarity)
    x = x + _L2_ffn_ref(_L2_cond_ref(x, L2_cond_W, L2_cond_A, L2_cond_Bm, L2_cond_scalings, itok_B_0_6), L2_ffn_w1, L2_ffn_g1, L2_ffn_w2, L2_ffn_g2)
    x = x + _L3_ffn_ref(_L3_cond_ref(x, itok_B_1_198, L3_cond_weights), L3_ffn_W1, L3_ffn_Wg, L3_ffn_W2, L3_ffn_Ws1, L3_ffn_Wsg, L3_ffn_Ws2, L3_ffn_gate_w, L3_ffn_gate_b, L3_ffn_biases)
    return x

_drawn_inputs = setup_inputs


def setup_inputs(seed=0):
    import zlib

    import numpy as np

    out = dict(_drawn_inputs(seed))
    spreads = {'L0_ffn_b1': (0.0, 0.1),
     'L0_ffn_b2': (0.0, 0.1),
     'L1_cond_b': (0.10000000149011612, 0.2),
     'L2_cond_scalings': (1.0, 0.2),
     'L2_ffn_g1': (1.0, 0.2),
     'L2_ffn_g2': (1.0, 0.2),
     'L3_ffn_gate_b': (0.0, 0.1),
     'L3_ffn_biases': (0.0, 0.1)}
    factors = {}
    for name, (base, spread) in spreads.items():
        noise = np.random.default_rng([zlib.crc32(name.encode()), seed]).standard_normal(out[name].shape)
        drawn = base * np.exp(spread * noise) if base else spread * noise
        out[name] = jnp.asarray(drawn.astype(out[name].dtype))
    for name, factor in factors.items():
        out[name] = (out[name] * factor).astype(out[name].dtype)
    return out
```

```python
from contextlib import ExitStack

import numpy as np

import concourse.bass as bass
from concourse import mybir

F32 = mybir.dt.float32
F32R = mybir.dt.float32r
BF16 = mybir.dt.bfloat16
U32 = mybir.dt.uint32
I32 = mybir.dt.int32
ALU = mybir.AluOpType
ACT = mybir.ActivationFunctionType
AX = mybir.AxisListType.X

P = 128
D = 256
DC = D // P
SEQS, SEQ = 64, 32
T = SEQS * SEQ
TILES = T // P
TSEQ = P // SEQ
BLOCK = 512
BLOCKS = T // BLOCK
BTILES = BLOCK // P
BSEQ = BLOCK // SEQ
HEADS, HD = 16, 16
CHEADS = P // HD
E0, F0 = 8, 1024
CAP = (2 * T * 5 // 4 + E0 - 1) // E0
E1, F1, K1, PRIM1 = 32, 96, 8, 4
W1TAB = 16
A2, R2, F2 = 8, 16, 1024
S3, E3, F3, K3 = 200, 7, 256, 3
MAGIC = 1.5 * 2.0 ** 23

CONST = {}


def constants():
    p = np.arange(P)
    parts = {
        "ident": np.eye(P),
        "before": p[:, None] < p[None, :],
        "ones": np.ones((P, P)),
        "causal": np.where(np.arange(SEQ)[None, :] <= (p % SEQ)[:, None], 0.0, -1e30),
        "head": (p // HD)[:, None] == np.arange(CHEADS)[None, :],
        "quad": (p // SEQ)[:, None] == np.arange(TSEQ)[None, :],
        "count": np.broadcast_to(np.arange(32), (P, 32)),
        "adapter": (p // R2)[:, None],
        "position": (p % SEQ)[:, None],
    }
    at = 0
    for name, part in parts.items():
        CONST[name] = (at, at + part.shape[1])
        at += part.shape[1]
    return np.ascontiguousarray(np.concatenate([np.asarray(x, np.float32) for x in parts.values()], axis=1))


CONSTANTS = constants()


class Signal:

    def __init__(self, sem, per=1, free=0):
        self.sem, self.per, self.free = sem, per, free

    def at(self, i, n):
        value = i * self.per + (n + self.free)
        assert not isinstance(value, int) or value > 0
        return value

    def grant(self, eng):
        eng.sem_inc(self.sem, self.free)


class Semaphores:

    def __init__(self, nc):
        self.nc, self.taken = nc, []

    def new(self, name):
        self.taken.append(self.nc.alloc_semaphore(name))
        return self.taken[-1]

    def clear(self):
        self.nc.clear_and_free_semaphores(self.taken)
        self.nc.all_engine_barrier()
        self.taken = []


class Chain:

    def __init__(self, eng, sem, per):
        self.eng, self.sem, self.per = eng, sem, per
        self.i, self.n = 0, 0

    def start(self, i):
        self.i, self.n = i, 0

    def next(self):
        self.n += 1
        return self.sem

    def count(self):
        return self.i * self.per + self.n

    def end(self):
        assert self.n == self.per, f"steps in a pass: {self.n}, not {self.per}"


def spread(ap, axis, n):
    ap = ap.unsqueeze(axis)
    shape = list(ap.shape)
    shape[axis] = n
    return ap.broadcast_to(shape)


def const(consts, name):
    a, b = CONST[name]
    return consts[:, a:b]


class Split:

    def __init__(self, new, name, shape):
        self.high, self.low = new(name + "_high", shape, F32R), new(name + "_low", shape, F32R)

    @property
    def high_read(self):
        return self.high[:].bitcast(F32)

    def passes(self, other):
        return ((self.high, other.high), (self.high, other.low), (self.low, other.high))


def product(pe, out, stationary, moving, ks, pick_s, pick_m, start=True, stop=True):
    last = None
    n, count = 0, 3 * len(ks)
    for k in ks:
        for s, m in stationary.passes(moving):
            last = pe.matmul(out, pick_s(s, k), pick_m(m, k), start=start and n == 0, stop=stop and n == count - 1,
                             skip_group_check=True)
            n += 1
    return last


def attention_phase(nc, sems, io, psum, consts, slots, weights_eff, mixes, rows):
    with ExitStack() as ctx:
        def sb(name, shape, dt=F32):
            return ctx.enter_context(nc.sbuf_tensor("a_" + name, shape, dt))

        def sig(name, per=1, free=0):
            return Signal(sems.new("a_" + name), per, free)

        xT = sb("xT", [P, DC, T])
        xs = Split(sb, "x", [P, DC, BLOCK])
        w_raw = sb("w_raw", [P, 4, DC, D])
        ws = Split(sb, "w", [P, 4, DC, D])
        gate_w = sb("gate_w", [P, DC, E0])
        beta = sb("beta", [P, SEQS])
        q = sb("q", [P, DC, BLOCK])
        k = sb("k", [P, DC, BLOCK])
        k_heads = sb("k_heads", [P, BSEQ, DC, CHEADS, SEQ])
        v_heads = sb("v_heads", [P, BSEQ, 4, 4, HD])
        score = sb("score", [P, 2, HEADS, SEQ])
        peak = sb("peak", [P, 2, HEADS])
        total = sb("total", [P, 2, HEADS])
        prob = sb("prob", [P, 2, HEADS, SEQ])
        probT = sb("probT", [P, 2, 4, P])
        os_ = Split(sb, "o", [P, 2, DC, P])
        y = sb("y", [P, BTILES, D])
        yT = sb("yT", [P, 2, DC, P])
        zeros = sb("zeros", [P, 2560])
        g_peak = sb("g_peak", [P, BTILES])
        g_exp = sb("g_exp", [P, BTILES, E0])
        g_sum = sb("g_sum", [P, BTILES])
        gates = sb("gates", [P, BTILES, E0])
        top = sb("top", [P, BTILES, 8])
        top_at = sb("top_at", [P, BTILES, 8], U32)
        top_e = sb("top_e", [P, BTILES, 2])
        w_sum = sb("w_sum", [P, BTILES])
        w_norm = sb("w_norm", [P, BTILES, 2])
        chosen = sb("chosen", [P, BTILES, 2, E0])
        taken = sb("taken", [P, BTILES, E0])
        before = sb("before", [P, BTILES + 1, E0])
        place_of = sb("place_of", [P, BTILES, 2, E0])
        place = sb("place", [P, BTILES, 2])
        valid = sb("valid", [P, BTILES, 2])
        lost = sb("lost", [P, BTILES, 2])
        slot = sb("slot", [P, BTILES, 2])
        target = sb("target", [P, BTILES, 2])
        scatter_at = sb("scatter_at", [P, BTILES, 2], U32)

        mix_id = sb("mix_id", [P, SEQS], I32)
        mix_own = sb("mix_own", [P, TILES, TSEQ])
        mix_row_f = sb("mix_row_f", [P, TILES])
        mix_row = sb("mix_row", [P, TILES], U32)

        mix_ids_loaded = sig("mix_ids_loaded")
        mix_rows_ready = sig("mix_rows_ready")
        mixes_loaded = sig("mixes_loaded")
        loaded = sig("loaded")
        weights_loaded = sig("weights_loaded")
        rows_cleared = sig("rows_cleared")
        zeros_set = sig("zeros_set")
        beta_ready = sig("beta_ready")
        weights_split = sig("weights_split")
        x_high = sig("x_high")
        x_low = sig("x_low")
        q_made = sig("q_made", 2)
        k_made = sig("k_made", 2)
        v_made = sig("v_made", 1, 1)
        v_cleared = sig("v_cleared")
        q_ready = sig("q_ready", 2)
        k_copied = sig("k_copied", 2)
        k_heads_dve = sig("k_heads_dve")
        k_heads_act = sig("k_heads_act")
        v_ready_act = sig("v_ready_act")
        v_ready_dve = sig("v_ready_dve")
        s_made = sig("s_made", BTILES, 2)
        s_masked = sig("s_masked", BTILES, 2)
        s_shifted = sig("s_shifted", BTILES)
        s_exp = sig("s_exp", BTILES)
        p_ready = sig("p_ready", BTILES, 2)
        pT_made = sig("pT_made", BTILES, 2)
        pT_ready = sig("pT_ready", BTILES, 2)
        o_made = sig("o_made", BTILES, 2)
        o_high = sig("o_high", BTILES)
        o_low = sig("o_low", BTILES, 2)
        y_made = sig("y_made", BTILES, 2)
        y_ready = sig("y_ready", BTILES, 2)
        yT_made = sig("yT_made", BTILES)
        yT_ready = sig("yT_ready", BTILES, 2)
        logits_made = sig("logits_made")
        g_shifted = sig("g_shifted")
        g_exped = sig("g_exped")
        taken_ready = sig("taken_ready")
        places_made = sig("places_made")
        targets_ready = sig("targets_ready")
        scattered = sig("scattered", 2 * BTILES * 16)
        y_left = sig("y_left", 1, 1)
        steps = sig("steps")
        pool_passed = sig("pool_passed")
        dve_passed = sig("dve_passed")
        block = ctx.enter_context(nc.Block())

        ident = const(consts, "ident")
        banks = [psum[:, n, :] for n in range(8)]
        v_psum = psum[:, 4:6, :].rearrange("p n (j g h d) -> p (n j) g h d", g=4, h=4, d=HD)

        def place_values(engine, i, quads):
            engine.wait_ge(v_made.sem, v_made.at(i, 1))
            engine.wait_ge(o_made.sem, o_made.at(i, 0))
            for b in quads:
                for h in range(4):
                    src = v_psum[b * SEQ:(b + 1) * SEQ, :, :, h, :]
                    dst = v_heads[h * SEQ:(h + 1) * SEQ, b:BSEQ:TSEQ, :, h, :]
                    if engine is nc.scalar:
                        last = engine.activation(dst, src, ACT.Copy)
                    else:
                        last = engine.tensor_copy(dst, src)
            return last
        b_q, b_k = banks[0:2], banks[2:4]
        b_s, b_pT, b_y, b_yT, b_o, b_g = banks[0:2], banks[2:4], banks[4], banks[5], banks[6], banks[7]

        def stages(tile_steps):
            for s in range(BTILES + max(lag for lag, _ in tile_steps)):
                for lag, work in tile_steps:
                    if 0 <= s - lag < BTILES:
                        work(s - lag)

        @block.sync
        def _(sp):
            sp.dma_start(consts[:], io["constants"]).then_inc(loaded.sem, 16)
            sp.dma_start(xT[:], io["xT"].rearrange("(c p) t -> p c t", p=P)).then_inc(loaded.sem, 16)
            sp.dma_start(w_raw[:], io["w_attention"].rearrange("w (c p) e -> p w c e", p=P)).then_inc(weights_loaded.sem, 16)
            sp.dma_start(gate_w[:], io["L0_ffn_gating_w"].rearrange("(c p) e -> p c e", p=P)).then_inc(weights_loaded.sem, 16)
            sp.dma_start(beta[:], io["cond_1"].rearrange("b o -> (b o)").partition_broadcast(P)).then_inc(loaded.sem, 16)
            sp.dma_start(mix_id[:], io["itok_B_1_198"].partition_broadcast(P)).then_inc(mix_ids_loaded.sem, 16)
            sp.wait_ge(zeros_set.sem, zeros_set.at(0, 1))
            clear = rows.rearrange("(n p r) d -> n p (r d)", p=P, r=10)
            for n in range(clear.shape[0]):
                sp.dma_start(clear[n], zeros[:]).then_inc(rows_cleared.sem, 16)

        @block.gpsimd
        def _(pool):
            y_left.grant(pool)
            pool.memset(v_heads[:], 0.0).then_inc(v_cleared.sem, 1)
            pool.wait_ge(mix_rows_ready.sem, mix_rows_ready.at(0, 5))
            for n in range(TILES):
                pool.indirect_dma_start(mixes[:, n, :], None, io["mix_rows"],
                                        bass.IndirectOffsetOnAxis(ap=mix_row[:, n:n + 1], axis=0)).then_inc(mixes_loaded.sem, 16)
            pool.wait_ge(rows_cleared.sem, rows_cleared.at(0, 16 * (E0 * CAP // (10 * P))))

            def scatter(i):
                pool.wait_ge(targets_ready.sem, targets_ready.at(i, 1))
                pool.sem_inc(pool_passed.sem, 1)
                for j in range(BTILES):
                    for c in range(2):
                        pool.indirect_dma_start(
                            rows, bass.IndirectOffsetOnAxis(ap=scatter_at[:, j, c:c + 1], axis=0), y[:, j, :], None,
                            bounds_check=E0 * CAP - 1, oob_is_err=False).then_inc(scattered.sem, 16)
                pool.wait_ge(scattered.sem, scattered.at(i, 2 * BTILES * 16))
                pool.sem_inc(y_left.sem, 1)

            with pool.Fori(0, BLOCKS) as i:
                scatter(i)
            pool.wait_ge(mixes_loaded.sem, mixes_loaded.at(0, 16 * TILES))

        @block.scalar
        def _(act):
            act.wait_ge(v_cleared.sem, v_cleared.at(0, 1))
            act.wait_ge(weights_loaded.sem, weights_loaded.at(0, 32))
            act.activation(ws.high[:], w_raw[:], ACT.Copy).then_inc(weights_split.sem, 1)
            act.wait_ge(loaded.sem, loaded.at(0, 48))
            head = const(consts, "head")

            def project(i):
                act.wait_ge(v_made.sem, v_made.at(i, 0))
                act.activation(xs.high[:], xT[:, :, bass.ds(i * BLOCK, BLOCK)], ACT.Copy).then_inc(x_high.sem, 1)
                for c in range(DC):
                    act.wait_ge(k_made.sem, k_made.at(i, c + 1))
                    act.activation(k[:, c, :], b_k[c], ACT.Copy).then_inc(k_copied.sem, 1)
                act.wait_ge(k_copied.sem, k_copied.at(i, 2))
                act.wait_ge(s_made.sem, s_made.at(i, 0))
                for h in range(CHEADS):
                    last = act.activation(k_heads[:, :, 1, h, :], k[:, 1, :].rearrange("p (b t) -> p b t", t=SEQ),
                                          ACT.Copy, scale=head[:, h:h + 1])
                last.then_inc(k_heads_act.sem, 1)
                place_values(act, i, (0, 1)).then_inc(v_ready_act.sem, 1)

            def tiles(i):
                def exp(j):
                    act.wait_ge(s_shifted.sem, s_shifted.at(i, j + 1))
                    act.activation(score[:, j % 2], score[:, j % 2], ACT.Exp).then_inc(s_exp.sem, 1)

                def turn(j):
                    act.wait_ge(pT_made.sem, pT_made.at(i, j + 1))
                    act.wait_ge(o_made.sem, o_made.at(i, j - 1))
                    act.activation(probT[:, j % 2], b_pT[j % 2], ACT.Copy).then_inc(pT_ready.sem, 1)

                def o(j):
                    act.wait_ge(o_made.sem, o_made.at(i, j + 1))
                    act.wait_ge(y_made.sem, y_made.at(i, j - 1))
                    act.activation(os_.high[:, j % 2], b_o[:, 0:D], ACT.Copy).then_inc(o_high.sem, 1)

                def y_out(j):
                    act.wait_ge(y_made.sem, y_made.at(i, j + 1))
                    if j == 0:
                        act.wait_ge(y_left.sem, y_left.at(i, 0))
                    act.activation(y[:, j, :], b_y[:, 0:D], ACT.Copy).then_inc(y_ready.sem, 1)

                def yT_out(j):
                    act.wait_ge(yT_made.sem, yT_made.at(i, j + 1))
                    act.activation(yT[:, j % 2], b_yT[:, 0:D], ACT.Copy).then_inc(yT_ready.sem, 1)

                stages([(0, exp), (2, turn), (3, o), (4, y_out), (5, yT_out)])
                act.wait_ge(g_shifted.sem, g_shifted.at(i, 1))
                act.activation(g_exp[:], g_exp[:], ACT.Exp).then_inc(g_exped.sem, 1)

            for made in (pT_ready, y_ready, yT_ready):
                made.grant(act)
            with act.Fori(0, BLOCKS) as i:
                project(i)
                tiles(i)

        @block.vector
        def _(dve):
            chain = Chain(dve, steps.sem, 34)
            s_masked.grant(dve)
            o_low.grant(dve)
            p_ready.grant(dve)
            dve.memset(zeros[:], 0.0).then_inc(zeros_set.sem, 1)
            dve.wait_ge(v_cleared.sem, v_cleared.at(0, 1))
            dve.wait_ge(weights_split.sem, weights_split.at(0, 1))
            dve.tensor_tensor(ws.low[:], w_raw[:], ws.high_read, ALU.subtract).then_inc(weights_split.sem, 1)
            dve.wait_ge(loaded.sem, loaded.at(0, 48))
            dve.tensor_scalar(beta[:], beta[:], 4.0, 0.25, ALU.min, ALU.mult).then_inc(beta_ready.sem, 1)
            dve.memset(before[:, 0, :], 0.0).then_inc(beta_ready.sem, 1)
            dve.wait_ge(beta_ready.sem, beta_ready.at(0, 2))
            dve.wait_ge(mix_ids_loaded.sem, mix_ids_loaded.at(0, 16))
            dve.tensor_copy(mix_own[:].rearrange("p n b -> p (n b)"), mix_id[:]).then_inc(mix_rows_ready.sem, 1)
            dve.wait_ge(mix_rows_ready.sem, mix_rows_ready.at(0, 1))
            dve.tensor_tensor(mix_own[:], mix_own[:], spread(const(consts, "quad"), 1, TILES), ALU.mult).then_inc(mix_rows_ready.sem, 1)
            dve.wait_ge(mix_rows_ready.sem, mix_rows_ready.at(0, 2))
            dve.tensor_reduce(mix_row_f[:], mix_own[:], AX, ALU.add).then_inc(mix_rows_ready.sem, 1)
            dve.wait_ge(mix_rows_ready.sem, mix_rows_ready.at(0, 3))
            dve.tensor_scalar(mix_row_f[:], mix_row_f[:], float(SEQ), const(consts, "position"), ALU.mult, ALU.add).then_inc(mix_rows_ready.sem, 1)
            dve.wait_ge(mix_rows_ready.sem, mix_rows_ready.at(0, 4))
            dve.tensor_copy(mix_row[:], mix_row_f[:]).then_inc(mix_rows_ready.sem, 1)
            head, causal, count = (const(consts, n) for n in ("head", "causal", "count"))

            def project(i):
                dve.wait_ge(x_high.sem, x_high.at(i, 1))
                dve.tensor_tensor(xs.low[:], xT[:, :, bass.ds(i * BLOCK, BLOCK)], xs.high_read, ALU.subtract).then_inc(x_low.sem, 1)
                for c in range(DC):
                    dve.wait_ge(q_made.sem, q_made.at(i, c + 1))
                    dve.tensor_tensor(q[:, c, :].rearrange("p (b t) -> p b t", t=SEQ),
                                      b_q[c].rearrange("p (b t) -> p b t", t=SEQ),
                                      spread(beta[:, bass.ds(i * BSEQ, BSEQ)], 2, SEQ), ALU.mult).then_inc(q_ready.sem, 1)
                dve.wait_ge(k_copied.sem, k_copied.at(i, 1))
                for h in range(CHEADS):
                    last = dve.tensor_scalar(k_heads[:, :, 0, h, :], k[:, 0, :].rearrange("p (b t) -> p b t", t=SEQ),
                                             head[:, h:h + 1], None, ALU.mult)
                last.then_inc(k_heads_dve.sem, 1)
                place_values(dve, i, (2, 3)).then_inc(v_ready_dve.sem, 1)

            def tiles(i):
                def shift(j):
                    sc = score[:, j % 2]
                    dve.wait_ge(s_made.sem, s_made.at(i, j + 1))
                    dve.wait_ge(p_ready.sem, p_ready.at(i, j - 1))
                    dve.tensor_tensor(sc, b_s[j % 2].rearrange("p (h t) -> p h t", t=SEQ), spread(causal, 1, HEADS),
                                      ALU.add).then_inc(s_masked.sem, 1)
                    dve.wait_ge(s_masked.sem, s_masked.at(i, j + 1))
                    dve.tensor_reduce(peak[:, j % 2], sc, AX, ALU.max).then_inc(chain.next(), 1)
                    dve.wait_ge(chain.sem, chain.count())
                    dve.tensor_tensor(sc, sc, spread(peak[:, j % 2], 2, SEQ), ALU.subtract).then_inc(s_shifted.sem, 1)

                def normalise(j):
                    sc, tot = score[:, j % 2], total[:, j % 2]
                    dve.wait_ge(s_exp.sem, s_exp.at(i, j + 1))
                    dve.tensor_reduce(tot, sc, AX, ALU.add).then_inc(chain.next(), 1)
                    dve.wait_ge(chain.sem, chain.count())
                    dve.reciprocal(tot, tot).then_inc(chain.next(), 1)
                    dve.wait_ge(chain.sem, chain.count())
                    dve.wait_ge(pT_made.sem, pT_made.at(i, j - 1))
                    dve.tensor_tensor(prob[:, j % 2], sc, spread(tot, 2, SEQ), ALU.mult).then_inc(p_ready.sem, 1)

                def o(j):
                    dve.wait_ge(o_high.sem, o_high.at(i, j + 1))
                    dve.tensor_tensor(os_.low[:, j % 2], b_o[:, 0:D].rearrange("p (c t) -> p c t", t=P),
                                      os_.high[:, j % 2].bitcast(F32), ALU.subtract).then_inc(o_low.sem, 1)

                stages([(0, shift), (1, normalise), (3, o)])

            def route(i):
                logits = b_g[:, 0:BTILES * E0].rearrange("p (j e) -> p j e", e=E0)
                dve.wait_ge(logits_made.sem, logits_made.at(i, 1))
                dve.tensor_reduce(g_peak[:], logits, AX, ALU.max).then_inc(chain.next(), 1)
                dve.wait_ge(chain.sem, chain.count())
                dve.tensor_tensor(g_exp[:], logits, spread(g_peak[:], 2, E0), ALU.subtract).then_inc(g_shifted.sem, 1)
                dve.wait_ge(g_exped.sem, g_exped.at(i, 1))
                dve.tensor_reduce(g_sum[:], g_exp[:], AX, ALU.add).then_inc(chain.next(), 1)
                dve.wait_ge(chain.sem, chain.count())
                dve.reciprocal(g_sum[:], g_sum[:]).then_inc(chain.next(), 1)
                dve.wait_ge(chain.sem, chain.count())
                dve.tensor_tensor(gates[:], g_exp[:], spread(g_sum[:], 2, E0), ALU.mult).then_inc(chain.next(), 1)
                dve.wait_ge(chain.sem, chain.count())
                dve.sem_inc(dve_passed.sem, 1)
                for j in range(BTILES):
                    last = dve.max(top[:, j, :], gates[:, j, :])
                last.then_inc(chain.next(), 1)
                dve.wait_ge(chain.sem, chain.count())
                dve.sem_inc(dve_passed.sem, 1)
                for j in range(BTILES):
                    last = dve.max_index(top_at[:, j, :], top[:, j, :], gates[:, j, :])
                last.then_inc(chain.next(), 1)
                dve.wait_ge(chain.sem, chain.count())
                dve.tensor_tensor(w_sum[:], top[:, :, 0], top[:, :, 1], ALU.add)
                dve.tensor_copy(top_e[:], top_at[:, :, 0:2]).then_inc(chain.next(), 1)
                dve.wait_ge(chain.sem, chain.count())
                dve.tensor_scalar(w_sum[:], w_sum[:], 1e-8, None, ALU.add).then_inc(chain.next(), 1)
                dve.tensor_tensor(chosen[:], spread(spread(count[:, 0:E0], 1, 2), 1, BTILES),
                                            spread(top_e[:], 3, E0), ALU.is_equal).then_inc(chain.next(), 1)
                dve.wait_ge(chain.sem, chain.count())
                dve.reciprocal(w_sum[:], w_sum[:]).then_inc(chain.next(), 1)
                dve.tensor_tensor(taken[:], chosen[:, :, 0, :], chosen[:, :, 1, :], ALU.add).then_inc(chain.next(), 1)
                dve.wait_ge(chain.sem, chain.count())
                dve.tensor_tensor(w_norm[:], top[:, :, 0:2], spread(w_sum[:], 2, 2), ALU.mult).then_inc(chain.next(), 1)
                for j in range(BTILES):
                    last = dve.tensor_tensor(before[:, j + 1, :], before[:, j, :], taken[:, j, :], ALU.add)
                    if j < BTILES - 1:
                        last.then_inc(chain.next(), 1)
                        dve.wait_ge(chain.sem, chain.count())
                last.then_inc(taken_ready.sem, 1)

            def assign(i):
                dve.wait_ge(taken_ready.sem, taken_ready.at(i, 1))
                dve.wait_ge(places_made.sem, places_made.at(i, 1))
                counts = b_g[:, 64:64 + BTILES * E0].rearrange("p (j e) -> p j e", e=E0)
                for c in range(2):
                    last = dve.tensor_tensor(place_of[:, :, c, :], chosen[:, :, c, :], counts, ALU.mult)
                last.then_inc(chain.next(), 1)
                dve.tensor_copy(before[:, 0, :], before[:, BTILES, :]).then_inc(chain.next(), 1)
                dve.wait_ge(chain.sem, chain.count())
                dve.tensor_reduce(place[:], place_of[:], AX, ALU.add).then_inc(chain.next(), 1)
                dve.wait_ge(chain.sem, chain.count())
                dve.tensor_scalar(valid[:], place[:], float(CAP), None, ALU.is_lt).then_inc(chain.next(), 1)
                dve.tensor_scalar(place[:], place[:], float(CAP - 1), None, ALU.min).then_inc(chain.next(), 1)
                dve.wait_ge(chain.sem, chain.count())
                dve.tensor_scalar(lost[:], valid[:], -1e6, 1e6, ALU.mult, ALU.add)
                dve.scalar_tensor_tensor(slot[:], top_e[:], float(CAP), place[:], ALU.mult, ALU.add).then_inc(chain.next(), 1)
                dve.wait_ge(chain.sem, chain.count())
                dve.tensor_tensor(target[:], slot[:], lost[:], ALU.add).then_inc(chain.next(), 1)
                dve.tensor_copy(slots[:, bass.ds(i * BTILES, BTILES), :], slot[:])
                dve.tensor_tensor(weights_eff[:, bass.ds(i * BTILES, BTILES), :], w_norm[:], valid[:], ALU.mult)
                dve.wait_ge(chain.sem, chain.count())
                dve.wait_ge(y_left.sem, y_left.at(i, 0))
                dve.tensor_copy(scatter_at[:], target[:]).then_inc(targets_ready.sem, 1)

            with dve.Fori(0, BLOCKS) as i:
                chain.start(i)
                project(i)
                tiles(i)
                route(i)
                assign(i)
                chain.end()

        @block.tensor
        def _(pe):
            pe.wait_ge(weights_split.sem, weights_split.at(0, 2))
            pe.wait_ge(loaded.sem, loaded.at(0, 48))
            for made in (v_made, s_made, pT_made, o_made, y_made):
                made.grant(pe)

            def project(i):
                pe.wait_ge(x_high.sem, x_high.at(i, 1))
                pe.wait_ge(x_low.sem, x_low.at(i, 1))
                for w, made, out in ((0, q_made, b_q), (1, k_made, b_k)):
                    for c in range(DC):
                        if w == 0:
                            pe.wait_ge(s_masked.sem, s_masked.at(i, 0))
                        else:
                            pe.wait_ge(pT_ready.sem, pT_ready.at(i, 0))
                        product(pe, out[c], ws, xs, range(DC), lambda a, kk: a[:, w, kk, c * P:(c + 1) * P],
                                lambda a, kk: a[:, kk, :]).then_inc(made.sem, 1)
                pe.wait_ge(y_ready.sem, y_ready.at(i, 0))
                pe.wait_ge(yT_ready.sem, yT_ready.at(i, 0))
                for j in range(BTILES):
                    last = product(pe, banks[4 + j // 2][:, (j % 2) * D:(j % 2 + 1) * D], xs, ws, range(DC),
                                   lambda a, kk: a[:, kk, j * P:(j + 1) * P], lambda a, kk: a[:, 2, kk, :])
                last.then_inc(v_made.sem, 1)

            def tiles(i):
                def scores(j):
                    if j == 0:
                        pe.wait_ge(q_ready.sem, q_ready.at(i, 2))
                        pe.wait_ge(k_heads_dve.sem, k_heads_dve.at(i, 1))
                        pe.wait_ge(k_heads_act.sem, k_heads_act.at(i, 1))
                    if j < 2:
                        pass
                    else:
                        pe.wait_ge(s_masked.sem, s_masked.at(i, j - 1))
                    for c in range(DC):
                        for b in range(TSEQ):
                            at = j * TSEQ + b
                            last = pe.matmul(b_s[j % 2][b * SEQ:(b + 1) * SEQ, c * D:(c + 1) * D],
                                             q[:, c, at * SEQ:(at + 1) * SEQ],
                                             k_heads[:, at, c].rearrange("p h t -> p (h t)"), start=True, stop=True,
                                             skip_group_check=True)
                    last.then_inc(s_made.sem, 1)

                def turn(j):
                    pe.wait_ge(p_ready.sem, p_ready.at(i, j + 1))
                    if j == 0:
                        pe.wait_ge(k_copied.sem, k_copied.at(i, 2))
                    pe.wait_ge(pT_ready.sem, pT_ready.at(i, j - 1))
                    for g in range(4):
                        last = pe.transpose(b_pT[j % 2][:, g * P:(g + 1) * P],
                                            prob[:, j % 2, 4 * g:4 * g + 4, :].rearrange("p h t -> p (h t)"), ident)
                    last.then_inc(pT_made.sem, 1)

                def mix(j):
                    pe.wait_ge(pT_ready.sem, pT_ready.at(i, j + 1))
                    if j == 0:
                        pe.wait_ge(v_ready_act.sem, v_ready_act.at(i, 1))
                        pe.wait_ge(v_ready_dve.sem, v_ready_dve.at(i, 1))
                    pe.wait_ge(o_low.sem, o_low.at(i, j))
                    for g in range(4):
                        for b in range(TSEQ):
                            out = b_o[64 * (g % 2):64 * (g % 2) + 64, (g // 2) * P + b * SEQ:(g // 2) * P + (b + 1) * SEQ]
                            last = pe.matmul(out, v_heads[:, j * TSEQ + b, g].rearrange("p h d -> p (h d)"),
                                             probT[:, j % 2, g, b * SEQ:(b + 1) * SEQ], start=True, stop=True,
                                             skip_group_check=True)
                    last.then_inc(o_made.sem, 1)

                def out(j):
                    pe.wait_ge(o_high.sem, o_high.at(i, j + 1))
                    pe.wait_ge(o_low.sem, o_low.at(i, j + 1))
                    pe.wait_ge(y_ready.sem, y_ready.at(i, j))
                    product(pe, b_y[:, 0:D], os_, ws, range(DC), lambda a, kk: a[:, j % 2, kk, :],
                            lambda a, kk: a[:, 3, kk, :]).then_inc(y_made.sem, 1)

                def turn_y(j):
                    pe.wait_ge(y_ready.sem, y_ready.at(i, j + 1))
                    pe.wait_ge(yT_ready.sem, yT_ready.at(i, j))
                    for c in range(DC):
                        last = pe.transpose(b_yT[:, c * P:(c + 1) * P], y[:, j, c * P:(c + 1) * P], ident)
                    last.then_inc(yT_made.sem, 1)

                def gate(j):
                    pe.wait_ge(yT_ready.sem, yT_ready.at(i, j + 1))
                    for c in range(DC):
                        last = pe.matmul(b_g[:, j * E0:(j + 1) * E0], yT[:, j % 2, c, :], gate_w[:, c, :],
                                         start=(c == 0), stop=(c == DC - 1), skip_group_check=True)
                    if j == BTILES - 1:
                        last.then_inc(logits_made.sem, 1)

                stages([(0, scores), (2, turn), (3, mix), (4, out), (5, turn_y), (6, gate)])

            def places(i):
                pe.wait_ge(taken_ready.sem, taken_ready.at(i, 1))
                pe.matmul(b_g[:, 64:64 + BTILES * E0], const(consts, "before"), taken[:].rearrange("p j e -> p (j e)"),
                          start=True, stop=False, skip_group_check=True)
                pe.matmul(b_g[:, 64:64 + BTILES * E0], const(consts, "ones"),
                          before[:, 0:BTILES, :].rearrange("p j e -> p (j e)"), start=False, stop=True,
                          skip_group_check=True).then_inc(places_made.sem, 1)

            with pe.Fori(0, BLOCKS) as i:
                project(i)
                tiles(i)
                places(i)


def capacity_experts_phase(nc, sems, io, psum, consts, rows, rows_out):
    CT, HALF, FC = CAP // P, CAP // 2, F0 // P
    STEPS = 2 * FC
    with ExitStack() as ctx:
        def sb(name, shape, dt=F32):
            return ctx.enter_context(nc.sbuf_tensor("e_" + name, shape, dt))

        def sig(name, per=1, free=0):
            return Signal(sems.new("e_" + name), per, free)

        w1_raw, w1 = sb("w1_raw", [P, DC, F0]), Split(sb, "w1", [P, DC, F0])
        w2_raw, w2 = sb("w2_raw", [P, FC, D]), Split(sb, "w2", [P, FC, D])
        row = sb("row", [P, CT, D])
        rT = Split(sb, "rT", [P, DC, CAP])
        relu = sb("relu", [P, 4, HALF])
        h = Split(sb, "h", [P, FC, CAP])
        y = sb("y", [P, CT, D])
        b1 = sb("b1", [P, E0 * FC])
        b1_now = sb("b1_now", [P, FC])
        b2 = sb("b2", [P, E0 * D])

        biases_loaded = sig("biases_loaded")
        rows_loaded = sig("rows_loaded", 16)
        w1_loaded = sig("w1_loaded", 16)
        w2_loaded = sig("w2_loaded", 16)
        w1_high, w1_low = sig("w1_high"), sig("w1_low")
        w2_high, w2_low = sig("w2_high"), sig("w2_low")
        rT_made = sig("rT_made", CT)
        rT_high = sig("rT_high", CT)
        rT_low = sig("rT_low", CT)
        h_made = sig("h_made", STEPS)
        h_relu = sig("h_relu", STEPS, 4)
        h_high = sig("h_high", STEPS)
        h_ready = sig("h_ready", STEPS, 4)
        b1_ready = sig("b1_ready")
        sp_passed = sig("sp_passed")
        y_made = sig("y_made", CT, 2)
        y_ready = sig("y_ready", CT, 2)
        y_stored = sig("y_stored", 16, 16)
        block = ctx.enter_context(nc.Block())
        ident = const(consts, "ident")
        banks = [psum[:, n, :] for n in range(8)]
        b_h, b_t, b_y = banks[0:4], banks[4:6], banks[6:8]

        def experts(engine, one):
            with engine.Fori(0, E0 - 1) as e:
                one(e, True)
            one(E0 - 1, False)

        @block.sync
        def _(sp):
            sp.dma_start(b1[:], io["b1"]).then_inc(biases_loaded.sem, 16)
            sp.dma_start(b2[:], io["L0_ffn_b2"].rearrange("e d -> (e d)").partition_broadcast(P)).then_inc(biases_loaded.sem, 16)
            sp.sem_inc(y_stored.sem, 16)

            def load_first(e):
                sp.dma_start(row[:], rows[bass.ds(e * CAP, CAP), :].rearrange("(r p) d -> p r d", p=P)).then_inc(rows_loaded.sem, 16)
                sp.dma_start(w1_raw[:], io["L0_ffn_w1"][bass.ds(e, 1)].rearrange("o (c p) f -> p (o c) f", p=P)).then_inc(w1_loaded.sem, 16)

            def load_second(e):
                sp.dma_start(w2_raw[:], io["L0_ffn_w2"][bass.ds(e, 1)].rearrange("o (f p) d -> p (o f) d", p=P)).then_inc(w2_loaded.sem, 16)

            load_first(0)
            load_second(0)

            def one(e, more):
                if more:
                    sp.wait_ge(rT_made.sem, rT_made.at(e, CT))
                    sp.sem_inc(sp_passed.sem, 1)
                    sp.wait_ge(w1_low.sem, w1_low.at(e, 1))
                    sp.sem_inc(sp_passed.sem, 1)
                    load_first(e + 1)
                    sp.wait_ge(w2_low.sem, w2_low.at(e, 1))
                    sp.sem_inc(sp_passed.sem, 1)
                    load_second(e + 1)
                sp.wait_ge(y_ready.sem, y_ready.at(e, CT))
                sp.sem_inc(sp_passed.sem, 1)
                sp.dma_start(rows_out[bass.ds(e * CAP, CAP), :].rearrange("(r p) d -> p r d", p=P), y[:]).then_inc(y_stored.sem, 16)

            experts(sp, one)
            sp.wait_ge(y_stored.sem, y_stored.at(E0, 0))

        @block.scalar
        def _(act):
            h_relu.grant(act)
            act.wait_ge(biases_loaded.sem, biases_loaded.at(0, 32))

            def prepare(e):
                for r in range(CT):
                    act.wait_ge(rT_made.sem, rT_made.at(e, r + 1))
                    act.activation(rT.high[:, :, r * P:(r + 1) * P], b_t[r % 2][:, 0:D].rearrange("p (c t) -> p c t", t=P),
                                   ACT.Copy).then_inc(rT_high.sem, 1)
                act.wait_ge(w1_loaded.sem, w1_loaded.at(e, 16))
                act.activation(w1.high[:], w1_raw[:], ACT.Copy).then_inc(w1_high.sem, 1)

            def one(e, more):
                act.wait_ge(b1_ready.sem, b1_ready.at(e, 1))
                for m in range(STEPS):
                    if m == 2:
                        act.wait_ge(w2_loaded.sem, w2_loaded.at(e, 16))
                        act.wait_ge(y_made.sem, y_made.at(e, 0))
                        act.activation(w2.high[:], w2_raw[:], ACT.Copy).then_inc(w2_high.sem, 1)
                    act.wait_ge(h_made.sem, h_made.at(e, m + 1))
                    act.wait_ge(h_ready.sem, h_ready.at(e, m - 3))
                    act.activation(relu[:, m % 4], b_h[m % 4][:, 0:HALF], ACT.Relu,
                                   bias=b1_now[:, m // 2:m // 2 + 1]).then_inc(h_relu.sem, 1)
                if more:
                    prepare(e + 1)

            prepare(0)
            experts(act, one)

        @block.vector
        def _(dve):
            h_ready.grant(dve)
            y_ready.grant(dve)
            dve.wait_ge(biases_loaded.sem, biases_loaded.at(0, 32))

            def prepare(e):
                for r in range(CT):
                    dve.wait_ge(rT_high.sem, rT_high.at(e, r + 1))
                    dve.tensor_tensor(rT.low[:, :, r * P:(r + 1) * P], b_t[r % 2][:, 0:D].rearrange("p (c t) -> p c t", t=P),
                                      rT.high[:, :, r * P:(r + 1) * P].bitcast(F32), ALU.subtract).then_inc(rT_low.sem, 1)
                dve.wait_ge(w1_high.sem, w1_high.at(e, 1))
                dve.tensor_tensor(w1.low[:], w1_raw[:], w1.high_read, ALU.subtract).then_inc(w1_low.sem, 1)

            def one(e, more):
                dve.wait_ge(h_relu.sem, h_relu.at(e, 0))
                dve.tensor_scalar(b1_now[:], b1[:, bass.ds(e * FC, FC)], 1.0, None, ALU.mult).then_inc(b1_ready.sem, 1)
                for m in range(STEPS):
                    if m == 3:
                        dve.wait_ge(w2_high.sem, w2_high.at(e, 1))
                        dve.tensor_tensor(w2.low[:], w2_raw[:], w2.high_read, ALU.subtract).then_inc(w2_low.sem, 1)
                    f, part = m // 2, slice((m % 2) * HALF, (m % 2 + 1) * HALF)
                    dve.wait_ge(h_relu.sem, h_relu.at(e, m + 1))
                    if m == 0:
                        dve.wait_ge(y_made.sem, y_made.at(e, 0))
                    dve.tensor_copy(h.high[:, f, part], relu[:, m % 4]).then_inc(h_high.sem, 1)
                    dve.wait_ge(h_high.sem, h_high.at(e, m + 1))
                    dve.tensor_tensor(h.low[:, f, part], relu[:, m % 4], h.high[:, f, part].bitcast(F32),
                                      ALU.subtract).then_inc(h_ready.sem, 1)
                if more:
                    prepare(e + 1)
                dve.wait_ge(y_stored.sem, y_stored.at(e, 0))
                for r in range(CT):
                    dve.wait_ge(y_made.sem, y_made.at(e, r + 1))
                    dve.tensor_tensor(y[:, r, :], b_y[r % 2][:, 0:D], b2[:, bass.ds(e * D, D)], ALU.add).then_inc(y_ready.sem, 1)

            prepare(0)
            experts(dve, one)

        @block.tensor
        def _(pe):
            y_made.grant(pe)

            def prepare(e):
                pe.wait_ge(rows_loaded.sem, rows_loaded.at(e, 16))
                for r in range(CT):
                    if r >= 2:
                        pe.wait_ge(rT_low.sem, rT_low.at(e, r - 1))
                    for c in range(DC):
                        last = pe.transpose(b_t[r % 2][:, c * P:(c + 1) * P], row[:, r, c * P:(c + 1) * P], ident)
                    last.then_inc(rT_made.sem, 1)

            def one(e, more):
                pe.wait_ge(rT_low.sem, rT_low.at(e, CT))
                pe.wait_ge(w1_low.sem, w1_low.at(e, 1))
                for m in range(STEPS):
                    f, part = m // 2, slice((m % 2) * HALF, (m % 2 + 1) * HALF)
                    pe.wait_ge(h_relu.sem, h_relu.at(e, m - 3))
                    product(pe, b_h[m % 4][:, 0:HALF], w1, rT, range(DC), lambda a, k: a[:, k, f * P:(f + 1) * P],
                            lambda a, k: a[:, k, part]).then_inc(h_made.sem, 1)
                if more:
                    prepare(e + 1)
                pe.wait_ge(w2_low.sem, w2_low.at(e, 1))
                pe.wait_ge(h_ready.sem, h_ready.at(e, STEPS))
                for r in range(CT):
                    pe.wait_ge(y_ready.sem, y_ready.at(e, r - 1))
                    product(pe, b_y[r % 2][:, 0:D], h, w2, range(FC), lambda a, k: a[:, k, r * P:(r + 1) * P],
                            lambda a, k: a[:, k, :]).then_inc(y_made.sem, 1)

            prepare(0)
            experts(pe, one)


def chosen_layer_phase(nc, sems, io, psum, consts, slots, weights_eff, rows_out, x, xT, combineT):
    PAIRS, J = TILES // 2, 2
    with ExitStack() as ctx:
        def sb(name, shape, dt=F32):
            return ctx.enter_context(nc.sbuf_tensor("c_" + name, shape, dt))

        def sem(name):
            return sems.new("c_" + name)

        def sig(name, per=1, free=0):
            return Signal(sem(name), per, free)

        PIECE = 2
        PIECES = W1TAB // PIECE
        w_raw = sb("w_raw", [P, 2, PIECE, DC, D])
        w = Split(sb, "w", [P, W1TAB, DC, D])
        bias_raw, bias = sb("bias_raw", [W1TAB, D]), Split(sb, "bias", [W1TAB, D])
        gate_raw, gate = sb("gate_raw", [P, DC, E1]), Split(sb, "gate", [P, DC, E1])
        ids = sb("ids", [W1TAB, SEQS], I32)
        ids_f = sb("ids_f", [W1TAB, SEQS])
        is_id = sb("is_id", [W1TAB, J, TSEQ, SEQ], F32R)
        sim = sb("sim", [P, 4, E1])
        got = sb("got", [P, TILES, 2, D])
        w_now = sb("w_now", [P, J, 2])
        part = sb("part", [P, J, D])
        x_now = sb("x_now", [P, J, D])
        x_nowT = Split(sb, "x_nowT", [P, J, DC, P])
        c = sb("c", [P, J, D])
        cT = Split(sb, "cT", [P, J, DC, P])
        r_peak = sb("r_peak", [P, J])
        r_prob = sb("r_prob", [P, J, E1])
        r_sum = sb("r_sum", [P, J])
        top = sb("top", [P, J, K1])
        top_at = sb("top_at", [P, J, K1], U32)
        top_e = sb("top_e", [P, J, K1])
        t_sum = sb("t_sum", [P, J])
        route = sb("route", [P, J, K1])
        hot = sb("hot", [P, J, K1, E1])
        hotT = sb("hotT", [P, J, P])
        pairs = sb("pairs", [P, J, 4, PRIM1, E1])
        likeness = sb("likeness", [P, J, 4, PRIM1])
        best = sb("best", [P, J, 4])
        keep = sb("keep", [P, J, 4])
        stays = sb("stays", [P, J, 4])
        leaves = sb("leaves", [P, J, 4])
        first = sb("first", [P, J, 4, PRIM1])
        first_of = sb("first_of", [P, J, 4])
        more_w = sb("more_w", [P, J, PRIM1])
        spread_w = sb("spread_w", [P, J, K1, E1])
        comb = sb("comb", [P, 2 * J, E1])
        combT = sb("combT", [J * E1, P])

        x_loaded = sig("x_loaded")
        small_loaded = sig("small_loaded")
        sim_cleared = sig("sim_cleared")
        sim_loaded = sig("sim_loaded")
        sim_ready = sig("sim_ready")
        w_loaded = [sem(f"w_loaded{n}") for n in range(2)]
        w_high = sig("w_high")
        w_low = sig("w_low")
        got_pair = [sem(f"got_pair{n}") for n in range(PAIRS)]
        gathered = sig("gathered")
        w_taken = sig("w_taken")
        small_ready = sig("small_ready")
        part_ready = sig("part_ready")
        x_ready = sig("x_ready", 1, 1)
        x_kept = sig("x_kept", 1, 1)
        xT_made = sig("xT_made", 1, 1)
        xT_high = sig("xT_high")
        xT_low = sig("xT_low")
        is_id_ready = sig("is_id_ready")
        c_made = sig("c_made", J, 2)
        c_ready = sig("c_ready", J, 2)
        cT_made = sig("cT_made", 1, 1)
        cT_high = sig("cT_high")
        cT_low = sig("cT_low", 1, 1)
        cT_kept = sig("cT_kept", 1, 1)
        logits_made = sig("logits_made", 1, 1)
        r_shifted = sig("r_shifted")
        r_exp = sig("r_exp")
        hot_ready = sig("hot_ready")
        hotT_made = sig("hotT_made")
        hotT_ready = sig("hotT_ready")
        sim_made = sig("sim_made")
        sim_read = sig("sim_read", 1, 2)
        comb_ready = sig("comb_ready")
        combT_made = sig("combT_made")
        combT_ready = sig("combT_ready", 1, 1)
        combT_stored = sig("combT_stored", 2 * 16, 16)
        steps = sig("steps")
        dve_passed, sp_passed = sig("dve_passed"), sig("sp_passed")
        block = ctx.enter_context(nc.Block())
        ident, count = const(consts, "ident"), const(consts, "count")
        banks = [psum[:, n, :] for n in range(8)]
        b_xT, b_sim, b_cT, b_g, b_hotT, b_combT = banks[4], banks[4], banks[5], banks[6], banks[7], banks[7]

        def skewed(engine, front_back):
            front_back(0, True, False)
            with engine.Fori(1, PAIRS) as i:
                front_back(i, True, True)
            front_back(PAIRS, False, True)

        @block.sync
        def _(sp):
            sp.sem_inc(combT_stored.sem, 16)
            sp.dma_start(x[:], io["x"].rearrange("(n p) d -> p n d", p=P)).then_inc(x_loaded.sem, 16)
            sp.dma_start(ids[:], io["itok_B_0_15"].partition_broadcast(W1TAB)).then_inc(small_loaded.sem, 16)
            sp.dma_start(bias_raw[:], io["L1_cond_b"]).then_inc(small_loaded.sem, 16)
            sp.dma_start(gate_raw[:], io["gate1"].rearrange("(c p) e -> p c e", p=P)).then_inc(small_loaded.sem, 16)
            sp.wait_ge(sim_cleared.sem, sim_cleared.at(0, 1))
            for n in range(4):
                sp.dma_start(sim[n * E1:(n + 1) * E1, n, :], io["L1_ffn_similarity"]).then_inc(sim_loaded.sem, 16)
            for n in range(PIECES):
                if n >= 2:
                    sp.wait_ge(w_low.sem, w_low.at(0, n - 1))
                sp.dma_start(w_raw[:, n % 2], io["L1_cond_W"][n * PIECE:(n + 1) * PIECE].rearrange("w (c p) e -> p w c e", p=P))\
                    .then_inc(w_loaded[n % 2], 16)

            def one(i, front, back):
                if back:
                    sp.wait_ge(combT_ready.sem, combT_ready.at(i, 0))
                    sp.sem_inc(sp_passed.sem, 1)
                    for j in range(J):
                        at = (i - 1) * (J * P) + j * P
                        sp.dma_start(combineT[:, bass.ds(at, P)], combT[j * E1:(j + 1) * E1, :]).then_inc(combT_stored.sem, 16)

            skewed(sp, one)
            sp.wait_ge(combT_stored.sem, combT_stored.at(PAIRS, 0))

        @block.gpsimd
        def _(pool):
            pool.memset(sim[:], 0.0).then_inc(sim_cleared.sem, 1)

            def relay(m):
                pool.wait_ge(got_pair[m], 4 * 16)
                pool.sem_inc(gathered.sem, 1)

            for m in range(PAIRS):
                for n in (2 * m, 2 * m + 1):
                    for k in range(2):
                        pool.indirect_dma_start(got[:, n, k, :], None, rows_out,
                                                bass.IndirectOffsetOnAxis(ap=slots[:, n, k:k + 1], axis=0)).then_inc(got_pair[m], 16)
                if m == 0:
                    pool.wait_ge(sim_loaded.sem, sim_loaded.at(0, 64))
                    flat = sim[:].rearrange("p k e -> p (k e)")
                    pool.affine_select(out=flat, in_=flat, compare_op=ALU.not_equal, fill=1.0, base=0,
                                       pattern=[[-1, P]], channel_multiplier=1).then_inc(sim_ready.sem, 1)
                if m >= 2:
                    relay(m - 2)
            relay(PAIRS - 2)
            relay(PAIRS - 1)

        @block.scalar
        def _(act):
            for made in (x_kept, c_ready, cT_kept, combT_ready):
                made.grant(act)
            act.wait_ge(small_loaded.sem, small_loaded.at(0, 48))
            act.activation(bias.high[:], bias_raw[:], ACT.Copy).then_inc(small_ready.sem, 1)
            act.activation(gate.high[:], gate_raw[:], ACT.Copy).then_inc(small_ready.sem, 1)
            for n in range(PIECES):
                act.wait_ge(w_loaded[n % 2], 16 * (n // 2 + 1))
                act.activation(w.high[:, n * PIECE:(n + 1) * PIECE], w_raw[:, n % 2], ACT.Copy).then_inc(w_high.sem, 1)

            def one(i, front, back):
                if front:
                    act.wait_ge(xT_made.sem, xT_made.at(i, 1))
                    act.activation(x_nowT.high[:].rearrange("p j c t -> p (j c t)"), b_xT, ACT.Copy).then_inc(xT_high.sem, 1)
                    act.activation(x[:, bass.ds(i * J, J), :], x_now[:], ACT.Copy).then_inc(x_kept.sem, 1)
                if back:
                    act.wait_ge(r_shifted.sem, r_shifted.at(i - 1, 1))
                    act.activation(r_prob[:], r_prob[:], ACT.Exp).then_inc(r_exp.sem, 1)

                def take(j):
                    act.wait_ge(c_made.sem, c_made.at(i, j + 1))
                    act.wait_ge(cT_made.sem, cT_made.at(i, 0))
                    for b in range(TSEQ):
                        quad = slice(b * SEQ, (b + 1) * SEQ)
                        last = act.activation(c[quad, j, :], banks[2 * j + b // 2][quad, (b % 2) * D:(b % 2 + 1) * D], ACT.Copy)
                    last.then_inc(c_ready.sem, 1)

                if front:
                    take(0)
                if back:
                    act.wait_ge(hotT_made.sem, hotT_made.at(i - 1, 1))
                    act.activation(hotT[:].rearrange("p j t -> p (j t)"), b_hotT[:, 0:J * P], ACT.Copy).then_inc(hotT_ready.sem, 1)
                if front:
                    take(1)
                    act.wait_ge(cT_made.sem, cT_made.at(i, 1))
                    act.wait_ge(logits_made.sem, logits_made.at(i, 0))
                    act.wait_ge(cT_kept.sem, cT_kept.at(i, 0))
                    act.activation(cT.high[:].rearrange("p j c t -> p (j c t)"), b_cT, ACT.Copy).then_inc(cT_high.sem, 1)
                if back:
                    act.wait_ge(combT_made.sem, combT_made.at(i - 1, 1))
                    act.wait_ge(combT_stored.sem, combT_stored.at(i - 1, 0))
                    act.activation(combT[:], b_combT[0:J * E1, 0:P], ACT.Copy).then_inc(combT_ready.sem, 1)
                if front:
                    act.wait_ge(cT_low.sem, cT_low.at(i, 1))
                    for half in ("high", "low"):
                        src = (cT.high, cT.low)[half == "low"]
                        dst = (xT.high, xT.low)[half == "low"]
                        last = act.activation(dst[:, :, bass.ds(i * J * P, J * P)].rearrange("p c (j t) -> p j c t", j=J).bitcast(F32R),
                                              src[:].bitcast(F32), ACT.Copy)
                    last.then_inc(cT_kept.sem, 1)

            skewed(act, one)

        @block.vector
        def _(dve):
            chain = Chain(dve, steps.sem, 25)
            sim_read.grant(dve)
            cT_low.grant(dve)
            x_ready.grant(dve)
            dve.memset(comb[:], 0.0).then_inc(small_ready.sem, 1)
            dve.wait_ge(small_ready.sem, small_ready.at(0, 3))
            dve.tensor_tensor(bias.low[:], bias_raw[:], bias.high_read, ALU.subtract).then_inc(small_ready.sem, 1)
            dve.tensor_tensor(gate.low[:], gate_raw[:], gate.high_read, ALU.subtract).then_inc(small_ready.sem, 1)
            dve.tensor_copy(ids_f[:], ids[:]).then_inc(small_ready.sem, 1)
            for n in range(PIECES):
                dve.wait_ge(w_high.sem, w_high.at(0, n + 1))
                dve.tensor_tensor(w.low[:, n * PIECE:(n + 1) * PIECE], w_raw[:, n % 2],
                                  w.high[:, n * PIECE:(n + 1) * PIECE].bitcast(F32), ALU.subtract).then_inc(w_low.sem, 1)
            dve.wait_ge(x_loaded.sem, x_loaded.at(0, 16))
            dve.wait_ge(small_ready.sem, small_ready.at(0, 6))

            def combine(i):
                dve.wait_ge(x_ready.sem, x_ready.at(i, 0))
                dve.wait_ge(gathered.sem, gathered.at(i, 1))
                dve.wait_ge(xT_made.sem, xT_made.at(i, 0))
                dve.tensor_scalar(w_now[:], weights_eff[:, bass.ds(i * J, J), :], 1.0, None, ALU.mult).then_inc(w_taken.sem, 1)
                dve.wait_ge(c_made.sem, c_made.at(i, 0))
                dve.tensor_scalar(is_id[:], spread(ids_f[:, bass.ds(i * J * TSEQ, J * TSEQ)].rearrange("p (j b) -> p j b", j=J), 3, SEQ),
                                  consts[0:W1TAB, CONST["position"][0]:CONST["position"][1]], None, ALU.is_equal).then_inc(is_id_ready.sem, 1)
                dve.wait_ge(w_taken.sem, w_taken.at(i, 1))
                for j in range(J):
                    last = dve.scalar_tensor_tensor(part[:, j, :], got[:, bass.ds(i * J + j, 1), 0, :].rearrange("p o d -> p (o d)"),
                                                    w_now[:, j, 0:1], x[:, bass.ds(i * J + j, 1), :].rearrange("p o d -> p (o d)"),
                                                    ALU.mult, ALU.add)
                last.then_inc(part_ready.sem, 1)
                dve.wait_ge(part_ready.sem, part_ready.at(i, 1))
                dve.wait_ge(x_kept.sem, x_kept.at(i, 0))
                for j in range(J):
                    last = dve.scalar_tensor_tensor(x_now[:, j, :], got[:, bass.ds(i * J + j, 1), 1, :].rearrange("p o d -> p (o d)"),
                                                    w_now[:, j, 1:2], part[:, j, :], ALU.mult, ALU.add)
                last.then_inc(x_ready.sem, 1)

            def low(dst, bank, high, made):
                return dve.tensor_tensor(dst.low[:].rearrange("p j c t -> p (j c t)"), bank,
                                         dst.high[:].rearrange("p j c t -> p (j c t)").bitcast(F32), ALU.subtract)

            def choose(i):
                logits = b_g[:, 0:J * E1].rearrange("p (j e) -> p j e", e=E1)
                chain.start(i)
                dve.wait_ge(logits_made.sem, logits_made.at(i, 1))
                dve.tensor_reduce(r_peak[:], logits, AX, ALU.max).then_inc(chain.next(), 1)
                dve.wait_ge(chain.sem, chain.count())
                dve.tensor_tensor(r_prob[:], logits, spread(r_peak[:], 2, E1), ALU.subtract).then_inc(r_shifted.sem, 1)
                dve.wait_ge(r_exp.sem, r_exp.at(i, 1))
                dve.tensor_reduce(r_sum[:], r_prob[:], AX, ALU.add).then_inc(chain.next(), 1)
                dve.wait_ge(chain.sem, chain.count())
                dve.reciprocal(r_sum[:], r_sum[:]).then_inc(chain.next(), 1)
                dve.wait_ge(chain.sem, chain.count())
                dve.tensor_tensor(r_prob[:], r_prob[:], spread(r_sum[:], 2, E1), ALU.mult).then_inc(chain.next(), 1)
                dve.wait_ge(chain.sem, chain.count())
                dve.sem_inc(dve_passed.sem, 1)
                for j in range(J):
                    last = dve.max(top[:, j, :], r_prob[:, j, :])
                last.then_inc(chain.next(), 1)
                dve.wait_ge(chain.sem, chain.count())
                dve.sem_inc(dve_passed.sem, 1)
                for j in range(J):
                    last = dve.max_index(top_at[:, j, :], top[:, j, :], r_prob[:, j, :])
                last.then_inc(chain.next(), 1)
                dve.wait_ge(chain.sem, chain.count())
                dve.tensor_copy(top_e[:], top_at[:]).then_inc(chain.next(), 1)
                dve.tensor_reduce(t_sum[:], top[:], AX, ALU.add).then_inc(chain.next(), 1)
                dve.wait_ge(chain.sem, chain.count())
                dve.tensor_scalar(t_sum[:], t_sum[:], 1e-12, None, ALU.max).then_inc(chain.next(), 1)
                dve.tensor_tensor(hot[:].rearrange("p j k e -> p (j k) e"), spread(count, 1, J * K1),
                                  spread(top_e[:].rearrange("p j k -> p (j k)"), 2, E1), ALU.is_equal).then_inc(hot_ready.sem, 1)
                dve.wait_ge(chain.sem, chain.count())
                dve.reciprocal(t_sum[:], t_sum[:]).then_inc(chain.next(), 1)
                dve.wait_ge(chain.sem, chain.count())
                dve.tensor_tensor(route[:], top[:], spread(t_sum[:], 2, K1), ALU.mult).then_inc(chain.next(), 1)

            def reroute(i):
                dve.wait_ge(sim_made.sem, sim_made.at(i, 1))
                dve.wait_ge(hot_ready.sem, hot_ready.at(i, 1))
                for j in range(J):
                    last = dve.tensor_tensor(pairs[:, j], spread(b_sim[:, j * P:(j + 1) * P].rearrange("p (k e) -> p k e", e=E1), 2, PRIM1),
                                             spread(hot[:, j, 0:PRIM1, :], 1, 4), ALU.mult)
                last.then_inc(sim_read.sem, 1)
                dve.wait_ge(sim_read.sem, sim_read.at(i, 1))
                dve.tensor_reduce(likeness[:].rearrange("p j s m -> p (j s m)"),
                                            pairs[:].rearrange("p j s m e -> p (j s m) e"), AX, ALU.add).then_inc(chain.next(), 1)
                dve.wait_ge(chain.sem, chain.count())
                dve.tensor_reduce(best[:], likeness[:], AX, ALU.max).then_inc(chain.next(), 1)
                dve.wait_ge(chain.sem, chain.count())
                dve.tensor_scalar(keep[:], best[:], 0.5, None, ALU.is_lt).then_inc(chain.next(), 1)
                dve.tensor_tensor(first[:].rearrange("p j s m -> p (j s) m"), likeness[:].rearrange("p j s m -> p (j s) m"),
                                            spread(best[:].rearrange("p j s -> p (j s)"), 2, PRIM1), ALU.is_equal).then_inc(chain.next(), 1)
                dve.wait_ge(chain.sem, chain.count())
                dve.scalar_tensor_tensor(first[:].rearrange("p j s m -> p (j s) m"),
                                                   spread(count[:, 0:PRIM1], 1, J * 4), -8.0,
                                                   first[:].rearrange("p j s m -> p (j s) m"), ALU.add, ALU.mult).then_inc(chain.next(), 1)
                dve.tensor_tensor(stays[:], route[:, :, PRIM1:K1], keep[:], ALU.mult).then_inc(chain.next(), 1)
                dve.wait_ge(chain.sem, chain.count())
                dve.tensor_reduce(first_of[:], first[:], AX, ALU.min).then_inc(chain.next(), 1)
                dve.wait_ge(chain.sem, chain.count())
                dve.tensor_tensor(first[:].rearrange("p j s m -> p (j s) m"), first[:].rearrange("p j s m -> p (j s) m"),
                                            spread(first_of[:].rearrange("p j s -> p (j s)"), 2, PRIM1), ALU.is_equal).then_inc(chain.next(), 1)
                dve.tensor_tensor(leaves[:], route[:, :, PRIM1:K1], stays[:], ALU.subtract).then_inc(chain.next(), 1)
                dve.wait_ge(chain.sem, chain.count())
                dve.tensor_copy(route[:, :, PRIM1:K1], stays[:]).then_inc(chain.next(), 1)
                dve.tensor_tensor(first[:].rearrange("p j s m -> p (j s) m"), first[:].rearrange("p j s m -> p (j s) m"),
                                            spread(leaves[:].rearrange("p j s -> p (j s)"), 2, PRIM1), ALU.mult).then_inc(chain.next(), 1)
                dve.wait_ge(chain.sem, chain.count())
                dve.tensor_reduce(more_w[:], first[:].rearrange("p j s m -> p j m s"), AX, ALU.add).then_inc(chain.next(), 1)
                dve.wait_ge(chain.sem, chain.count())
                dve.tensor_tensor(route[:, :, 0:PRIM1], route[:, :, 0:PRIM1], more_w[:], ALU.add).then_inc(chain.next(), 1)
                dve.wait_ge(chain.sem, chain.count())
                dve.tensor_tensor(spread_w[:].rearrange("p j k e -> p (j k) e"), hot[:].rearrange("p j k e -> p (j k) e"),
                                            spread(route[:].rearrange("p j k -> p (j k)"), 2, E1), ALU.mult).then_inc(chain.next(), 1)
                dve.wait_ge(chain.sem, chain.count())
                dve.tensor_reduce(comb[:, 0:J, :], spread_w[:].rearrange("p j k e -> p j e k"), AX, ALU.add).then_inc(comb_ready.sem, 1)
                dve.wait_ge(comb_ready.sem, comb_ready.at(i, 1))
                chain.end()

            def one(i, front, back):
                if front:
                    combine(i)
                    dve.wait_ge(xT_high.sem, xT_high.at(i, 1))
                    low(x_nowT, b_xT, None, None).then_inc(xT_low.sem, 1)
                if back:
                    choose(i - 1)
                    reroute(i - 1)
                if front:
                    dve.wait_ge(cT_high.sem, cT_high.at(i, 1))
                    low(cT, b_cT, None, None).then_inc(cT_low.sem, 1)

            skewed(dve, one)

        @block.tensor
        def _(pe):
            for made in (xT_made, c_made, cT_made, logits_made):
                made.grant(pe)
            pe.wait_ge(small_ready.sem, small_ready.at(0, 6))
            pe.wait_ge(w_low.sem, w_low.at(0, PIECES))
            pe.wait_ge(sim_ready.sem, sim_ready.at(0, 1))

            def turn_x(i):
                pe.wait_ge(x_ready.sem, x_ready.at(i, 1))
                pe.wait_ge(sim_read.sem, sim_read.at(i - 1, 0))
                for j in range(J):
                    for k in range(DC):
                        last = pe.transpose(b_xT[:, (j * DC + k) * P:(j * DC + k + 1) * P], x_now[:, j, k * P:(k + 1) * P], ident)
                last.then_inc(xT_made.sem, 1)

            def layer(i, j):
                pe.wait_ge(xT_low.sem, xT_low.at(i, 1))
                pe.wait_ge(is_id_ready.sem, is_id_ready.at(i, 1))
                pe.wait_ge(c_ready.sem, c_ready.at(i, j - 1))
                for pair in range(2):
                    out = banks[2 * j + pair]
                    which = is_id[:, j].rearrange("p b t -> p (b t)")
                    for n, half in enumerate((bias.high, bias.low)):
                        pe.matmul(out, which, spread(half[:], 1, 2), start=(n == 0), stop=False, skip_group_check=True)
                    for b in (2 * pair, 2 * pair + 1):
                        own = pe.value_load(ids[0:1, bass.ds(i * J * TSEQ + j * TSEQ + b, 1)], min_val=0, max_val=W1TAB - 1)
                        last = product(pe, out[:, (b % 2) * D:(b % 2 + 1) * D], x_nowT, w, range(DC), lambda a, k: a[:, j, k, :],
                                       lambda a, k: a[:, bass.ds(own, 1), k, :].rearrange("p o e -> p (o e)"), start=False)
                last.then_inc(c_made.sem, 1)

            def one(i, front, back):
                if front:
                    turn_x(i)
                    layer(i, 0)
                if back:
                    pe.wait_ge(hot_ready.sem, hot_ready.at(i - 1, 1))
                    pe.wait_ge(combT_ready.sem, combT_ready.at(i - 1, 0))
                    for j in range(J):
                        last = pe.transpose(b_hotT[:, j * P:(j + 1) * P], hot[:, j, PRIM1:K1, :].rearrange("p k e -> p (k e)"), ident)
                    last.then_inc(hotT_made.sem, 1)
                if front:
                    layer(i, 1)
                if back:
                    pe.wait_ge(hotT_ready.sem, hotT_ready.at(i - 1, 1))
                    if front:
                        pe.wait_ge(xT_low.sem, xT_low.at(i, 1))
                    for j in range(J):
                        last = pe.matmul(b_sim[:, j * P:(j + 1) * P], hotT[:, j, :], sim[:].rearrange("p k e -> p (k e)"),
                                         start=True, stop=True, skip_group_check=True)
                    last.then_inc(sim_made.sem, 1)
                if front:
                    pe.wait_ge(c_ready.sem, c_ready.at(i, J))
                    pe.wait_ge(cT_low.sem, cT_low.at(i, 0))
                    for j in range(J):
                        for k in range(DC):
                            last = pe.transpose(b_cT[:, (j * DC + k) * P:(j * DC + k + 1) * P], c[:, j, k * P:(k + 1) * P], ident)
                    last.then_inc(cT_made.sem, 1)
                if back:
                    pe.wait_ge(comb_ready.sem, comb_ready.at(i - 1, 1))
                    pe.transpose(b_combT[:, 0:P], comb[:].rearrange("p j e -> p (j e)"), ident).then_inc(combT_made.sem, 1)
                if front:
                    pe.wait_ge(cT_low.sem, cT_low.at(i, 1))
                    for j in range(J):
                        last = product(pe, b_g[:, j * E1:(j + 1) * E1], cT, gate, range(DC), lambda a, k: a[:, j, k, :],
                                       lambda a, k: a[:, k, :])
                    last.then_inc(logits_made.sem, 1)

            skewed(pe, one)


def gated_experts_phase(nc, sems, name, psum, gate_w, up_w, down_w, combineT, width, experts, chunks, x, xT):
    group = chunks * P // width
    GROUPS = experts // group
    STEPS = BLOCKS * chunks
    with ExitStack() as ctx:
        def sb(n, shape, dt=F32):
            return ctx.enter_context(nc.sbuf_tensor(f"{name}_{n}", shape, dt))

        def sig(n, per=1, free=0):
            return Signal(sems.new(f"{name}_{n}"), per, free)

        gu_raw, gu = sb("gu_raw", [P, chunks, 2, DC, P]), Split(sb, "gu", [P, chunks, 2, DC, P])
        down_raw, down = sb("down_raw", [P, chunks, D]), Split(sb, "down", [P, chunks, D])
        weight = sb("weight", [P, chunks, T])
        silu = sb("silu", [P, 2, BLOCK])
        prod = sb("prod", [P, 2, BLOCK])
        hw = sb("hw", [P, 2, BLOCK])
        h = Split(sb, "h", [P, 2, chunks, BLOCK])

        gu_loaded = [sig(f"gu_loaded{c}", 32) for c in range(chunks)]
        down_loaded = sig("down_loaded", 16)
        weight_loaded = [sig(f"weight_loaded{c}", 16 * len(pieces(c, width))) for c in range(chunks)]
        gu_high, gu_low = sig("gu_high", chunks), sig("gu_low", chunks)
        down_high, down_low = sig("down_high"), sig("down_low")
        gu_made = sig("gu_made", STEPS)
        silu_ready = sig("silu_ready", STEPS)
        prod_ready = sig("prod_ready", STEPS, 2)
        hw_ready = sig("hw_ready", STEPS, 2)
        h_high = sig("h_high", STEPS)
        h_low = sig("h_low", STEPS, 2)
        y_made = sig("y_made", BLOCKS, 2)
        y_added = sig("y_added", BLOCKS, 2)
        sp_passed = sig("sp_passed")
        block = ctx.enter_context(nc.Block())
        banks = [psum[:, n, :] for n in range(8)]

        def groups(engine, one):
            with engine.Fori(0, GROUPS - 1) as g:
                one(g, True)
            one(GROUPS - 1, False)

        @block.sync
        def _(sp):
            def load_gu(g, c):
                for n, w in enumerate((gate_w, up_w)):
                    src = w[:, bass.ds((g * chunks + c) * P, P)].rearrange("(k p) f -> p k f", p=P)
                    sp.dma_start(gu_raw[:, c, n], src).then_inc(gu_loaded[c].sem, 16)

            def load_down(g):
                src = down_w[bass.ds(g * (chunks * P), chunks * P), :].rearrange("(c p) d -> p c d", p=P)
                sp.dma_start(down_raw[:], src).then_inc(down_loaded.sem, 16)

            def load_weight(g, c):
                for a, b, e in pieces(c, width):
                    src = combineT[bass.ds(g * group + e, 1), :].rearrange("o t -> (o t)").partition_broadcast(b - a)
                    sp.dma_start(weight[a:b, c, :], src).then_inc(weight_loaded[c].sem, 16)

            for c in range(chunks):
                load_gu(0, c)
            for c in range(chunks):
                load_weight(0, c)
            load_down(0)

            def one(g, more):
                if more:
                    for c in range(chunks):
                        sp.wait_ge(gu_low.sem, gu_low.at(g, c + 1))
                        sp.sem_inc(sp_passed.sem, 1)
                        load_gu(g + 1, c)
                    sp.wait_ge(down_low.sem, down_low.at(g, 1))
                    sp.sem_inc(sp_passed.sem, 1)
                    load_down(g + 1)
                    for c in range(chunks):
                        sp.wait_ge(hw_ready.sem, hw_ready.at(g, STEPS - chunks + c + 1))
                        sp.sem_inc(sp_passed.sem, 1)
                        load_weight(g + 1, c)

            groups(sp, one)

        @block.gpsimd
        def _(pool):
            hw_ready.grant(pool)

            def one(g, more):
                for m in range(STEPS):
                    b, c = divmod(m, chunks)
                    if b == 0:
                        pool.wait_ge(weight_loaded[c].sem, weight_loaded[c].at(g, weight_loaded[c].per))
                    pool.wait_ge(prod_ready.sem, prod_ready.at(g, m + 1))
                    pool.wait_ge(h_low.sem, h_low.at(g, m - 1))
                    pool.tensor_tensor(hw[:, m % 2], prod[:, m % 2], weight[:, c, b * BLOCK:(b + 1) * BLOCK],
                                       ALU.mult).then_inc(hw_ready.sem, 1)

            groups(pool, one)

        @block.scalar
        def _(act):
            def split_gu(g, c):
                act.wait_ge(gu_loaded[c].sem, gu_loaded[c].at(g, 32))
                act.activation(gu.high[:, c], gu_raw[:, c], ACT.Copy).then_inc(gu_high.sem, 1)

            for c in range(chunks):
                split_gu(0, c)

            def one(g, more):
                for m in range(STEPS):
                    b, c = divmod(m, chunks)
                    act.wait_ge(gu_made.sem, gu_made.at(g, m + 1))
                    act.wait_ge(prod_ready.sem, prod_ready.at(g, m - 1))
                    act.activation(silu[:, m % 2], banks[m % 2], ACT.Silu).then_inc(silu_ready.sem, 1)
                    if m == 0:
                        act.wait_ge(down_loaded.sem, down_loaded.at(g, 16))
                        act.wait_ge(y_made.sem, y_made.at(g, 0))
                        act.activation(down.high[:], down_raw[:], ACT.Copy).then_inc(down_high.sem, 1)
                    if more and b == BLOCKS - 1:
                        split_gu(g + 1, c)
                    act.wait_ge(hw_ready.sem, hw_ready.at(g, m + 1))
                    act.wait_ge(y_made.sem, y_made.at(g, b - 1))
                    act.activation(h.high[:, b % 2, c], hw[:, m % 2], ACT.Copy).then_inc(h_high.sem, 1)

            groups(act, one)

        @block.vector
        def _(dve):
            for made in (prod_ready, h_low, y_added):
                made.grant(dve)

            def split_gu(g, c):
                dve.wait_ge(gu_high.sem, gu_high.at(g, c + 1))
                dve.tensor_tensor(gu.low[:, c], gu_raw[:, c], gu.high[:, c].bitcast(F32), ALU.subtract).then_inc(gu_low.sem, 1)

            for c in range(chunks):
                split_gu(0, c)

            def add(g, b):
                dve.wait_ge(y_made.sem, y_made.at(g, b + 1))
                dve.wait_ge(y_added.sem, y_added.at(g, b))
                for half in range(2):
                    out = x[:, b * BTILES + 2 * half:b * BTILES + 2 * half + 2, :].rearrange("p n d -> p (n d)")
                    last = dve.tensor_tensor(out, banks[4 + 2 * (b % 2) + half], out, ALU.add)
                last.then_inc(y_added.sem, 1)

            def one(g, more):
                for m in range(STEPS):
                    b, c = divmod(m, chunks)
                    dve.wait_ge(silu_ready.sem, silu_ready.at(g, m + 1))
                    dve.wait_ge(hw_ready.sem, hw_ready.at(g, m - 1))
                    dve.tensor_tensor(prod[:, m % 2], banks[2 + m % 2], silu[:, m % 2], ALU.mult).then_inc(prod_ready.sem, 1)
                    if m == 0:
                        dve.wait_ge(down_high.sem, down_high.at(g, 1))
                        dve.tensor_tensor(down.low[:], down_raw[:], down.high_read, ALU.subtract).then_inc(down_low.sem, 1)
                    if more and b == BLOCKS - 1:
                        split_gu(g + 1, c)
                    dve.wait_ge(h_high.sem, h_high.at(g, m + 1))
                    dve.tensor_tensor(h.low[:, b % 2, c], hw[:, m % 2], h.high[:, b % 2, c].bitcast(F32),
                                      ALU.subtract).then_inc(h_low.sem, 1)
                    if c == chunks - 1 and b > 0:
                        add(g, b - 1)
                add(g, BLOCKS - 1)

            groups(dve, one)

        @block.tensor
        def _(pe):
            y_made.grant(pe)

            def hidden(g, b, c):
                m = b * chunks + c
                if b == 0:
                    pe.wait_ge(gu_low.sem, gu_low.at(g, c + 1))
                pe.wait_ge(prod_ready.sem, prod_ready.at(g, m - 1))
                for n in range(2):
                    last = product(pe, banks[2 * n + m % 2], gu, xT, range(DC), lambda a, k: a[:, c, n, k, :],
                                   lambda a, k: a[:, k, b * BLOCK:(b + 1) * BLOCK])
                last.then_inc(gu_made.sem, 1)

            def result(g, b):
                if b == 0:
                    pe.wait_ge(down_low.sem, down_low.at(g, 1))
                pe.wait_ge(y_added.sem, y_added.at(g, b - 1))
                for c in range(chunks):
                    pe.wait_ge(h_low.sem, h_low.at(g, b * chunks + c + 1))
                    for r in range(BTILES):
                        last = product(pe, banks[4 + 2 * (b % 2) + r // 2][:, (r % 2) * D:(r % 2 + 1) * D], h, down, [c],
                                       lambda a, k: a[:, b % 2, k, r * P:(r + 1) * P], lambda a, k: a[:, k, :],
                                       start=(c == 0 and r % 2 == 0), stop=(c == chunks - 1))
                last.then_inc(y_made.sem, 1)

            def one(g, more):
                for b in range(BLOCKS):
                    for c in range(chunks):
                        if b > 0 and c == chunks - 1:
                            result(g, b - 1)
                        hidden(g, b, c)
                result(g, BLOCKS - 1)

            groups(pe, one)


def pieces(c, width):
    out, at = [], c * P
    while at < (c + 1) * P:
        e = at // width
        end = min((e + 1) * width, (c + 1) * P)
        out.append((at - c * P, end - c * P, e))
        at = end
    return out


def quantised_phase(nc, sems, io, psum, consts, x):
    FC, J = F2 // P, BTILES
    with ExitStack() as ctx:
        def sb(name, shape, dt=F32):
            return ctx.enter_context(nc.sbuf_tensor("q_" + name, shape, dt))

        def sig(name, per=1, free=0):
            return Signal(sems.new("q_" + name), per, free)

        cond_raw, cond = sb("cond_raw", [P, DC, D]), Split(sb, "cond", [P, DC, D])
        down_raw, down = sb("down_raw", [P, DC, P]), Split(sb, "down", [P, DC, P])
        up_raw, up = sb("up_raw", [P, 1, D]), Split(sb, "up", [P, 1, D])
        ids = sb("ids", [P, SEQS], I32)
        ids_f = sb("ids_f", [P, SEQS])
        scaling = sb("scaling", [P, 1])
        own = sb("own", [P, SEQS])
        g1, g2 = sb("g1", [P, D]), sb("g2", [P, F2])
        w1_raw, w1_q = sb("w1_raw", [P, DC, F2]), sb("w1_q", [P, DC, F2], BF16)
        w2_raw, w2_q = sb("w2_raw", [P, FC, D]), sb("w2_q", [P, FC, D], BF16)
        w_abs = sb("w_abs", [P, 2])
        w_mean = sb("w_mean", [P, 2])
        w_scale = sb("w_scale", [P, 2])
        magic = sb("magic", [P, 1])
        magic_off = sb("magic_off", [P, 1])
        eps = sb("eps", [P, 1])
        x_now = sb("x_now", [P, J, D])
        x_T = Split(sb, "x_T", [P, J, DC, P])
        low_rank = sb("low_rank", [P, BLOCK])
        lr = Split(sb, "lr", [P, 1, BLOCK])
        c = sb("c", [P, J, D])
        v = sb("v", [P, J, D])
        q1 = sb("q1", [P, J, DC, P], BF16)
        square = sb("square", [P, 2, F2])
        r = sb("r", [P, 2, F2])
        r2 = sb("r2", [P, 2, F2])
        v2 = sb("v2", [P, J, F2])
        t2 = sb("t2", [P, 2, F2])
        q2 = sb("q2", [P, 2, FC, P], BF16)
        sums, rms, inv, peak, to_q, back = (sb(n, [P, 2, J]) for n in ("sums", "rms", "inv", "peak", "to_q", "back"))

        loaded = sig("loaded")
        prepared_act = sig("prepared_act")
        prepared = sig("prepared")
        abs_summed = sig("abs_summed")
        x_copied = sig("x_copied")
        xT_made = sig("xT_made", 2, 1)
        xT_high = sig("xT_high", 2)
        xT_low = sig("xT_low", 2)
        lr_made = sig("lr_made")
        lr_masked = sig("lr_masked")
        lr_high = sig("lr_high")
        lr_low = sig("lr_low")
        c_made = sig("c_made", 2, 1)
        c_copied = sig("c_copied", 2)
        v_ready = sig("v_ready", 2)
        rms_ready = sig("rms_ready", 2)
        sqrt1, sqrt2 = sig("sqrt1"), sig("sqrt2")
        back_ready = sig("back_ready", 2)
        t_ready = sig("t_ready")
        t_made = sig("t_made", 2)
        q1_ready = sig("q1_ready", 2)
        h_made = sig("h_made", J, 1)
        r_ready = sig("r_ready", J, 2)
        r2_ready = sig("r2_ready", J, 2)
        v2_ready = sig("v2_ready", J, 2)
        sums2_ready = sig("sums2_ready", J, 2)
        to_q2_ready = sig("to_q2_ready")
        t2_ready = sig("t2_ready", J, 1)
        t2_clipped = sig("t2_clipped", J)
        t2_made = sig("t2_made", J, 2)
        q2_act = sig("q2_act", J, 2)
        q2_dve = sig("q2_dve", J, 2)
        y_made = sig("y_made", J, 2)
        y_added = sig("y_added", J, 2)
        steps = sig("steps")
        block = ctx.enter_context(nc.Block())
        ident = const(consts, "ident")
        banks = [psum[:, n, :] for n in range(8)]
        b_lr, b_c = banks[2], banks[3]
        b_y = (banks[2], banks[3])

        def b_h(j):
            first = 4 + 2 * (j % 2)
            return psum[:, first:first + 2, :].rearrange("p n f -> p (n f)")

        def b_t2(j, half):
            return banks[(0, 4)[j % 2] + half]

        @block.sync
        def _(sp):
            def load(dst, src):
                sp.dma_start(dst, src).then_inc(loaded.sem, 16)

            load(w1_raw[:], io["quant_w1"].rearrange("(c p) f -> p c f", p=P))
            load(w2_raw[:], io["quant_w2"].rearrange("(c p) d -> p c d", p=P))
            load(cond_raw[:], io["cond2"].rearrange("(c p) e -> p c e", p=P))
            load(down_raw[:], io["adapter_down"].rearrange("(c p) r -> p c r", p=P))
            load(up_raw[:, 0, :], io["adapter_up"])
            load(ids[:], io["itok_B_0_6"].partition_broadcast(P))
            load(g1[:], io["L2_ffn_g1"].partition_broadcast(P))
            load(g2[:], io["L2_ffn_g2"].partition_broadcast(P))
            for a in range(A2):
                load(scaling[a * R2:(a + 1) * R2, :], io["L2_cond_scalings"][a:a + 1].partition_broadcast(R2))

        LOADED = 16 * (8 + A2)

        @block.gpsimd
        def _(pool):
            v2_ready.grant(pool)
            pool.wait_ge(loaded.sem, loaded.at(0, LOADED))
            with pool.Fori(0, BLOCKS) as i:
                pool.wait_ge(xT_made.sem, xT_made.at(i, 0))
                pool.tensor_copy(x_now[:], x[:, bass.ds(i * J, J), :]).then_inc(x_copied.sem, 1)
                for j in range(J):
                    pool.wait_ge(r2_ready.sem, r2_ready.at(i, j + 1))
                    pool.wait_ge(t2_ready.sem, t2_ready.at(i, 0))
                    pool.tensor_tensor(v2[:, j, :], r2[:, j % 2], g2[:], ALU.mult).then_inc(v2_ready.sem, 1)

        @block.scalar
        def _(act):
            for made in (r_ready, sums2_ready, t2_ready, q2_act):
                made.grant(act)
            act.wait_ge(loaded.sem, loaded.at(0, LOADED))
            for raw, split in ((cond_raw, cond), (down_raw, down), (up_raw, up)):
                act.activation(split.high[:], raw[:], ACT.Copy).then_inc(prepared_act.sem, 1)
            act.wait_ge(prepared.sem, prepared.at(0, 3))

            with act.Fori(0, BLOCKS) as i:
                for half in range(2):
                    act.wait_ge(xT_made.sem, xT_made.at(i, half + 1))
                    act.activation(x_T.high[:, 2 * half:2 * half + 2].rearrange("p j c t -> p (j c t)"), banks[half],
                                   ACT.Copy).then_inc(xT_high.sem, 1)
                act.wait_ge(lr_masked.sem, lr_masked.at(i, 1))
                act.activation(lr.high[:, 0, :], low_rank[:], ACT.Copy).then_inc(lr_high.sem, 1)
                for half in range(2):
                    act.wait_ge(c_made.sem, c_made.at(i, half + 1))
                    act.activation(c[:, 2 * half:2 * half + 2, :].rearrange("p j d -> p (j d)"), b_c, ACT.Copy).then_inc(c_copied.sem, 1)
                    act.wait_ge(c_copied.sem, c_copied.at(i, half + 1))
                    for j in (2 * half, 2 * half + 1):
                        last = act.activation(square[:, j % 2, 0:D], c[:, j, :], ACT.Square, accum_out=sums[:, 0, j:j + 1])
                    last.then_inc(rms_ready.sem, 1)
                act.wait_ge(rms_ready.sem, rms_ready.at(i, 2))
                act.activation(rms[:, 0, :], sums[:, 0, :], ACT.Sqrt, bias=eps[:], scale=1.0 / D).then_inc(sqrt1.sem, 1)

                def sum_squares(j):
                    act.wait_ge(r2_ready.sem, r2_ready.at(i, j + 1))
                    act.activation(square[:, j % 2], r2[:, j % 2], ACT.Square, accum_out=sums[:, 1, j:j + 1]).then_inc(sums2_ready.sem, 1)

                for j in range(J):
                    act.wait_ge(h_made.sem, h_made.at(i, j + 1))
                    act.wait_ge(back_ready.sem, back_ready.at(i, 1))
                    act.wait_ge(r2_ready.sem, r2_ready.at(i, j - 1))
                    act.activation(r[:, j % 2], b_h(j), ACT.Relu, scale=back[:, 0, j:j + 1]).then_inc(r_ready.sem, 1)
                    if j > 0:
                        sum_squares(j - 1)
                sum_squares(J - 1)
                act.wait_ge(sums2_ready.sem, sums2_ready.at(i, J))
                act.activation(rms[:, 1, :], sums[:, 1, :], ACT.Sqrt, bias=eps[:], scale=1.0 / F2).then_inc(sqrt2.sem, 1)
                act.wait_ge(to_q2_ready.sem, to_q2_ready.at(i, 1))

                def take(j):
                    act.wait_ge(t2_made.sem, t2_made.at(i, j + 1))
                    act.wait_ge(y_made.sem, y_made.at(i, j - 1))
                    act.activation(q2[:, j % 2, 0:4, :].rearrange("p f t -> p (f t)"), b_t2(j, 0), ACT.Identity,
                                   bias=magic_off[:]).then_inc(q2_act.sem, 1)

                for j in range(J):
                    act.wait_ge(t2_made.sem, t2_made.at(i, j - 1))
                    act.activation(t2[:, j % 2], v2[:, j, :], ACT.Identity, bias=magic[:], scale=to_q[:, 1, j:j + 1])\
                        .then_inc(t2_ready.sem, 1)
                    if j > 0:
                        take(j - 1)
                take(J - 1)

        @block.vector
        def _(dve):
            chain = Chain(dve, steps.sem, 0)
            for made in (r2_ready, q2_dve, y_added):
                made.grant(dve)
            dve.memset(magic[:], MAGIC).then_inc(prepared.sem, 1)
            dve.memset(magic_off[:], -MAGIC).then_inc(prepared.sem, 1)
            dve.memset(eps[:], 1e-6).then_inc(prepared.sem, 1)
            dve.wait_ge(loaded.sem, loaded.at(0, LOADED))
            for n, (raw, split) in enumerate(((cond_raw, cond), (down_raw, down), (up_raw, up))):
                dve.wait_ge(prepared_act.sem, prepared_act.at(0, n + 1))
                dve.tensor_tensor(split.low[:], raw[:], split.high_read, ALU.subtract).then_inc(prepared.sem, 1)
            dve.tensor_copy(ids_f[:], ids[:]).then_inc(prepared.sem, 1)
            dve.wait_ge(prepared.sem, prepared.at(0, 7))
            dve.tensor_scalar(own[:], ids_f[:], const(consts, "adapter"), scaling[:], ALU.is_equal, ALU.mult).then_inc(prepared.sem, 1)
            for n, raw in enumerate((w1_raw, w2_raw)):
                last = dve.tensor_reduce(w_abs[:, n:n + 1], raw[:].rearrange("p c f -> p (c f)"), AX, ALU.add,
                                         apply_absolute_value=True)
            last.then_inc(prepared.sem, 1)
            dve.wait_ge(abs_summed.sem, abs_summed.at(0, 1))
            dve.tensor_scalar(w_mean[:], b_lr[:, 0:2], 1.0 / (D * F2), 1e-5, ALU.mult, ALU.max).then_inc(prepared.sem, 1)
            dve.wait_ge(prepared.sem, prepared.at(0, 10))
            dve.reciprocal(w_scale[:], w_mean[:]).then_inc(prepared.sem, 1)
            dve.wait_ge(prepared.sem, prepared.at(0, 11))
            for n, raw in enumerate((w1_raw, w2_raw)):
                last = dve.tensor_scalar(raw[:], raw[:], w_scale[:, n:n + 1], MAGIC, ALU.mult, ALU.add)
            last.then_inc(prepared.sem, 1)
            dve.wait_ge(prepared.sem, prepared.at(0, 12))
            for raw in (w1_raw, w2_raw):
                last = dve.tensor_scalar(raw[:], raw[:], MAGIC + 1, MAGIC - 1, ALU.min, ALU.max)
            last.then_inc(prepared.sem, 1)
            dve.wait_ge(prepared.sem, prepared.at(0, 13))
            for raw, whole in ((w1_raw, w1_q), (w2_raw, w2_q)):
                last = dve.tensor_scalar(whole[:], raw[:], -MAGIC, None, ALU.add)
            last.then_inc(prepared.sem, 1)

            def scales(i, n, sqrt):
                dve.wait_ge(sqrt.sem, sqrt.at(i, 1))
                dve.reciprocal(inv[:, n, :], rms[:, n, :]).then_inc(chain.next(), 1)
                dve.wait_ge(chain.sem, chain.count())
                dve.tensor_tensor(peak[:, n, :], peak[:, n, :], inv[:, n, :], ALU.mult).then_inc(chain.next(), 1)
                dve.wait_ge(chain.sem, chain.count())
                dve.tensor_scalar(peak[:, n, :], peak[:, n, :], 1e-5, None, ALU.max).then_inc(chain.next(), 1)
                dve.wait_ge(chain.sem, chain.count())
                dve.reciprocal(to_q[:, n, :], peak[:, n, :]).then_inc(chain.next(), 1)
                dve.tensor_scalar(back[:, n, :], peak[:, n, :], w_mean[:, n:n + 1], 1.0 / 127, ALU.mult, ALU.mult).then_inc(back_ready.sem, 1)
                dve.wait_ge(chain.sem, chain.count())
                return dve.scalar_tensor_tensor(to_q[:, n, :], to_q[:, n, :], 127.0, inv[:, n, :], ALU.mult, ALU.mult)

            chain.per = 12
            with dve.Fori(0, BLOCKS) as i:
                chain.start(i)
                for half in range(2):
                    dve.wait_ge(xT_high.sem, xT_high.at(i, half + 1))
                    out = slice(2 * half, 2 * half + 2)
                    dve.tensor_tensor(x_T.low[:, out].rearrange("p j c t -> p (j c t)"), banks[half],
                                      x_T.high[:, out].rearrange("p j c t -> p (j c t)").bitcast(F32), ALU.subtract).then_inc(xT_low.sem, 1)
                dve.wait_ge(lr_made.sem, lr_made.at(i, 1))
                dve.tensor_tensor(low_rank[:].rearrange("p (b t) -> p b t", t=SEQ), b_lr.rearrange("p (b t) -> p b t", t=SEQ),
                                  spread(own[:, bass.ds(i * BSEQ, BSEQ)], 2, SEQ), ALU.mult).then_inc(lr_masked.sem, 1)
                dve.wait_ge(lr_high.sem, lr_high.at(i, 1))
                dve.tensor_tensor(lr.low[:, 0, :], low_rank[:], lr.high[:, 0, :].bitcast(F32), ALU.subtract).then_inc(lr_low.sem, 1)
                for half in range(2):
                    dve.wait_ge(c_copied.sem, c_copied.at(i, half + 1))
                    out = slice(2 * half, 2 * half + 2)
                    dve.tensor_tensor(v[:, out, :], c[:, out, :], spread(g1[:], 1, 2), ALU.mult).then_inc(v_ready.sem, 1)
                dve.wait_ge(v_ready.sem, v_ready.at(i, 2))
                dve.tensor_reduce(peak[:, 0, :], v[:], AX, ALU.max, apply_absolute_value=True).then_inc(chain.next(), 1)
                dve.wait_ge(chain.sem, chain.count())
                scales(i, 0, sqrt1).then_inc(chain.next(), 1)
                dve.wait_ge(chain.sem, chain.count())
                for j in range(J):
                    last = dve.tensor_scalar(v[:, j, :], v[:, j, :], to_q[:, 0, j:j + 1], MAGIC, ALU.mult, ALU.add)
                last.then_inc(chain.next(), 1)
                dve.wait_ge(chain.sem, chain.count())
                dve.tensor_scalar(v[:], v[:], MAGIC + 127, MAGIC - 128, ALU.min, ALU.max).then_inc(t_ready.sem, 1)
                for half in range(2):
                    dve.wait_ge(t_made.sem, t_made.at(i, half + 1))
                    dve.tensor_scalar(q1[:, 2 * half:2 * half + 2].rearrange("p j c t -> p (j c t)"), banks[half], -MAGIC, None,
                                      ALU.add).then_inc(q1_ready.sem, 1)

                def largest(j):
                    dve.wait_ge(v2_ready.sem, v2_ready.at(i, j + 1))
                    return dve.tensor_reduce(peak[:, 1, j:j + 1], v2[:, j, :], AX, ALU.max, apply_absolute_value=True)

                for j in range(J):
                    dve.wait_ge(r_ready.sem, r_ready.at(i, j + 1))
                    dve.wait_ge(v2_ready.sem, v2_ready.at(i, j - 1))
                    dve.wait_ge(sums2_ready.sem, sums2_ready.at(i, j - 1))
                    dve.tensor_tensor(r2[:, j % 2], r[:, j % 2], r[:, j % 2], ALU.mult).then_inc(r2_ready.sem, 1)
                    if j > 0:
                        largest(j - 1)
                largest(J - 1).then_inc(chain.next(), 1)
                dve.wait_ge(chain.sem, chain.count())
                scales(i, 1, sqrt2).then_inc(to_q2_ready.sem, 1)

                def take(j):
                    dve.wait_ge(t2_made.sem, t2_made.at(i, j + 1))
                    dve.tensor_scalar(q2[:, j % 2, 4:8, :].rearrange("p f t -> p (f t)"), b_t2(j, 1), -MAGIC, None,
                                      ALU.add).then_inc(q2_dve.sem, 1)

                def add(j):
                    dve.wait_ge(y_made.sem, y_made.at(i, j + 1))
                    dve.wait_ge(back_ready.sem, back_ready.at(i, 2))
                    out = x[:, bass.ds(i * J + j, 1), :].rearrange("p o d -> p (o d)")
                    dve.scalar_tensor_tensor(out, b_y[j % 2][:, 0:D], back[:, 1, j:j + 1], out, ALU.mult, ALU.add).then_inc(y_added.sem, 1)

                for j in range(J + 2):
                    if j < J:
                        dve.wait_ge(t2_ready.sem, t2_ready.at(i, j + 1))
                        dve.tensor_scalar(t2[:, j % 2], t2[:, j % 2], MAGIC + 127, MAGIC - 128, ALU.min, ALU.max).then_inc(t2_clipped.sem, 1)
                    if 1 <= j <= J:
                        take(j - 1)
                    if j >= 2:
                        add(j - 2)
                chain.end()

        @block.tensor
        def _(pe):
            for made in (xT_made, c_made, h_made, t2_made, y_made):
                made.grant(pe)
            pe.wait_ge(prepared.sem, prepared.at(0, 9))
            pe.matmul(b_lr[:, 0:2], const(consts, "ones"), w_abs[:], start=True, stop=True).then_inc(abs_summed.sem, 1)
            pe.wait_ge(prepared.sem, prepared.at(0, 14))
            with pe.Fori(0, BLOCKS) as i:
                pe.wait_ge(x_copied.sem, x_copied.at(i, 1))
                pe.wait_ge(q2_act.sem, q2_act.at(i, 0))
                pe.wait_ge(q2_dve.sem, q2_dve.at(i, 0))
                for half in range(2):
                    for n in range(2 * DC):
                        j, k = 2 * half + n // DC, n % DC
                        last = pe.transpose(banks[half][:, n * P:(n + 1) * P], x_now[:, j, k * P:(k + 1) * P], ident)
                    last.then_inc(xT_made.sem, 1)
                pe.wait_ge(xT_low.sem, xT_low.at(i, 2))
                pe.wait_ge(y_added.sem, y_added.at(i, 0))
                product(pe, b_lr, down, x_T, range(DC), lambda a, k: a[:, k, :], lambda a, k: a[:, :, k, :]).then_inc(lr_made.sem, 1)
                for half in range(2):
                    if half:
                        pe.wait_ge(c_copied.sem, c_copied.at(i, half))
                    for n in range(2):
                        out, j = b_c[:, n * D:(n + 1) * D], 2 * half + n
                        product(pe, out, x_T, cond, range(DC), lambda a, k: a[:, j, k, :], lambda a, k: a[:, k, :], stop=False)
                        pe.wait_ge(lr_low.sem, lr_low.at(i, 1))
                        last = product(pe, out, lr, up, [0], lambda a, k: a[:, k, j * P:(j + 1) * P], lambda a, k: a[:, k, :], start=False)
                    last.then_inc(c_made.sem, 1)
                pe.wait_ge(t_ready.sem, t_ready.at(i, 1))
                for half in range(2):
                    for n in range(2 * DC):
                        j, k = 2 * half + n // DC, n % DC
                        last = pe.transpose(banks[half][:, n * P:(n + 1) * P], v[:, j, k * P:(k + 1) * P], ident)
                    last.then_inc(t_made.sem, 1)
                for j in range(J):
                    pe.wait_ge(q1_ready.sem, q1_ready.at(i, j // 2 + 1))
                    pe.wait_ge(r_ready.sem, r_ready.at(i, j - 1))
                    for half in range(2):
                        for k in range(DC):
                            last = pe.matmul(b_h(j)[:, half * 512:(half + 1) * 512], q1[:, j, k, :], w1_q[:, k, half * 512:(half + 1) * 512],
                                             start=(k == 0), stop=(k == DC - 1))
                    last.then_inc(h_made.sem, 1)

                def turn(j):
                    pe.wait_ge(t2_clipped.sem, t2_clipped.at(i, j + 1))
                    pe.wait_ge(q2_act.sem, q2_act.at(i, j - 1))
                    pe.wait_ge(q2_dve.sem, q2_dve.at(i, j - 1))
                    if j == 1:
                        pe.wait_ge(r_ready.sem, r_ready.at(i, J - 1))
                    for f in range(FC):
                        last = pe.transpose(b_t2(j, f // 4)[:, (f % 4) * P:(f % 4 + 1) * P], t2[:, j % 2, f * P:(f + 1) * P], ident)
                    last.then_inc(t2_made.sem, 1)

                def result(j):
                    pe.wait_ge(q2_act.sem, q2_act.at(i, j + 1))
                    pe.wait_ge(q2_dve.sem, q2_dve.at(i, j + 1))
                    pe.wait_ge(y_added.sem, y_added.at(i, j - 1))
                    for f in range(FC):
                        last = pe.matmul(b_y[j % 2][:, 0:D], q2[:, j % 2, f, :], w2_q[:, f, :], start=(f == 0), stop=(f == FC - 1))
                    last.then_inc(y_made.sem, 1)

                for j in range(J + 1):
                    if j < J:
                        turn(j)
                    if j > 0:
                        result(j - 1)


def position_mix_phase(nc, sems, io, psum, consts, mixes, x, xT, combineT):
    J = BTILES
    with ExitStack() as ctx:
        def sb(name, shape, dt=F32):
            return ctx.enter_context(nc.sbuf_tensor("m_" + name, shape, dt))

        def sig(name, per=1, free=0):
            return Signal(sems.new("m_" + name), per, free)

        mix_wide = sb("mix_wide", [P, TILES, TSEQ, SEQ])
        mix = Split(sb, "mix", [P, J, P])
        x_now = Split(sb, "x_now", [P, J, D])
        cT = Split(sb, "cT", [P, J, DC, P])
        gate_raw, gate = sb("gate_raw", [P, DC, E3 + 1]), Split(sb, "gate", [P, DC, E3 + 1])
        gate_b, biases = sb("gate_b", [P, E3]), sb("biases", [P, E3])
        logits = sb("logits", [P, TILES, E3])
        peak = sb("peak", [P, TILES])
        total = sb("total", [P, TILES])
        prob = sb("prob", [P, TILES, E3 + 1])
        biased = sb("biased", [P, TILES, E3 + 1])
        top = sb("top", [P, TILES, 8])
        top_at = sb("top_at", [P, TILES, 8], U32)
        top_e = sb("top_e", [P, TILES, K3])
        hot = sb("hot", [P, TILES, K3, E3 + 1])
        hot_prob = sb("hot_prob", [P, TILES, K3, E3 + 1])
        top_prob = sb("top_prob", [P, TILES, K3])
        comb = sb("comb", [P, E3 + 1, TILES])
        combT = sb("combT", [P, P])

        loaded = sig("loaded")
        set_ = sig("set")
        gate_high = sig("gate_high")
        mix_ready = sig("mix_ready")
        mix_high, mix_low = sig("mix_high"), sig("mix_low")
        x_high, x_low = sig("x_high"), sig("x_low")
        c_made = sig("c_made", 2, 1)
        c_high, c_low = sig("c_high", 2), sig("c_low", 2, 1)
        c_kept = sig("c_kept", 1, 1)
        logits_made = sig("logits_made", 1, 1)
        shifted, exped = sig("shifted"), sig("exped")
        comb_ready, combT_made, combT_ready, stored = sig("comb_ready"), sig("combT_made"), sig("combT_ready"), sig("stored")
        steps = sig("steps")
        dve_passed = sig("dve_passed")
        block = ctx.enter_context(nc.Block())
        ident, quad, count = (const(consts, n) for n in ("ident", "quad", "count"))
        banks = [psum[:, n, :] for n in range(8)]
        b_g, b_t = banks[4], banks[5]

        @block.sync
        def _(sp):
            sp.wait_ge(set_.sem, set_.at(0, 1))
            sp.dma_start(gate_raw[:, :, 0:E3], io["L3_ffn_gate_w"].rearrange("(c p) e -> p c e", p=P)).then_inc(loaded.sem, 16)
            sp.dma_start(gate_b[:], io["L3_ffn_gate_b"].partition_broadcast(P)).then_inc(loaded.sem, 16)
            sp.dma_start(biases[:], io["L3_ffn_biases"].partition_broadcast(P)).then_inc(loaded.sem, 16)
            sp.wait_ge(combT_ready.sem, combT_ready.at(0, 1))
            sp.dma_start(combineT.rearrange("e (n t) -> (e n) t", t=P), combT[:]).then_inc(stored.sem, 16)
            sp.wait_ge(stored.sem, stored.at(0, 16))

        @block.gpsimd
        def _(pool):
            c_kept.grant(pool)
            with pool.Fori(0, BLOCKS) as i:
                pool.wait_ge(c_low.sem, c_low.at(i, 2))
                for src, dst in ((cT.high, xT.high), (cT.low, xT.low)):
                    for k in range(DC):
                        last = pool.tensor_copy(dst[:, k, bass.ds(i * BLOCK, BLOCK)].rearrange("p (j t) -> p j t", t=P), src[:, :, k, :])
                last.then_inc(c_kept.sem, 1)

        @block.scalar
        def _(act):
            act.wait_ge(loaded.sem, loaded.at(0, 48))
            act.activation(gate.high[:], gate_raw[:], ACT.Copy).then_inc(gate_high.sem, 1)
            act.wait_ge(mix_ready.sem, mix_ready.at(0, 1))
            with act.Fori(0, BLOCKS) as i:
                act.wait_ge(c_made.sem, c_made.at(i, 0))
                act.activation(x_now.high[:], x[:, bass.ds(i * J, J), :], ACT.Copy).then_inc(x_high.sem, 1)
                act.activation(mix.high[:], mix_wide[:, bass.ds(i * J, J)].rearrange("p n b t -> p n (b t)"), ACT.Copy).then_inc(mix_high.sem, 1)
                act.wait_ge(logits_made.sem, logits_made.at(i, 0))
                act.wait_ge(c_kept.sem, c_kept.at(i, 0))
                for half in range(2):
                    act.wait_ge(c_made.sem, c_made.at(i, half + 1))
                    act.activation(cT.high[:, 2 * half:2 * half + 2].rearrange("p j c t -> p (j c t)"), banks[half],
                                   ACT.Copy).then_inc(c_high.sem, 1)
            act.wait_ge(shifted.sem, shifted.at(0, 1))
            act.activation(logits[:], logits[:], ACT.Exp).then_inc(exped.sem, 1)
            act.wait_ge(combT_made.sem, combT_made.at(0, 1))
            act.activation(combT[:], b_t[:, 0:P], ACT.Copy).then_inc(combT_ready.sem, 1)

        @block.vector
        def _(dve):
            c_low.grant(dve)
            dve.memset(gate_raw[:], 0.0).then_inc(set_.sem, 1)
            dve.memset(prob[:], 0.0).then_inc(set_.sem, 1)
            dve.memset(biased[:], -1e30).then_inc(set_.sem, 1)
            dve.memset(comb[:], 1.0).then_inc(set_.sem, 1)
            dve.tensor_tensor(mix_wide[:], spread(mixes[:], 2, TSEQ), spread(spread(quad, 2, SEQ), 1, TILES), ALU.mult).then_inc(mix_ready.sem, 1)
            dve.wait_ge(gate_high.sem, gate_high.at(0, 1))
            dve.tensor_tensor(gate.low[:], gate_raw[:], gate.high_read, ALU.subtract).then_inc(gate_high.sem, 1)
            dve.wait_ge(mix_ready.sem, mix_ready.at(0, 1))
            with dve.Fori(0, BLOCKS) as i:
                dve.wait_ge(x_high.sem, x_high.at(i, 1))
                dve.tensor_tensor(x_now.low[:], x[:, bass.ds(i * J, J), :], x_now.high_read, ALU.subtract).then_inc(x_low.sem, 1)
                dve.wait_ge(mix_high.sem, mix_high.at(i, 1))
                dve.tensor_tensor(mix.low[:], mix_wide[:, bass.ds(i * J, J)].rearrange("p n b t -> p n (b t)"), mix.high_read,
                                  ALU.subtract).then_inc(mix_low.sem, 1)
                for half in range(2):
                    dve.wait_ge(c_high.sem, c_high.at(i, half + 1))
                    out = slice(2 * half, 2 * half + 2)
                    dve.tensor_tensor(cT.low[:, out].rearrange("p j c t -> p (j c t)"), banks[half],
                                      cT.high[:, out].rearrange("p j c t -> p (j c t)").bitcast(F32), ALU.subtract).then_inc(c_low.sem, 1)

            chain = Chain(dve, steps.sem, 0)
            dve.wait_ge(logits_made.sem, logits_made.at(BLOCKS, 0))
            dve.wait_ge(set_.sem, set_.at(0, 4))
            dve.tensor_tensor(logits[:], b_g[:, 0:TILES * (E3 + 1)].rearrange("p (n e) -> p n e", e=E3 + 1)[:, :, 0:E3],
                                        spread(gate_b[:], 1, TILES), ALU.add).then_inc(chain.next(), 1)
            dve.wait_ge(chain.sem, chain.count())
            dve.tensor_reduce(peak[:], logits[:], AX, ALU.max).then_inc(chain.next(), 1)
            dve.wait_ge(chain.sem, chain.count())
            dve.tensor_tensor(logits[:], logits[:], spread(peak[:], 2, E3), ALU.subtract).then_inc(shifted.sem, 1)
            dve.wait_ge(exped.sem, exped.at(0, 1))
            dve.tensor_reduce(total[:], logits[:], AX, ALU.add).then_inc(chain.next(), 1)
            dve.wait_ge(chain.sem, chain.count())
            dve.reciprocal(total[:], total[:]).then_inc(chain.next(), 1)
            dve.wait_ge(chain.sem, chain.count())
            dve.tensor_tensor(prob[:, :, 0:E3], logits[:], spread(total[:], 2, E3), ALU.mult).then_inc(chain.next(), 1)
            dve.wait_ge(chain.sem, chain.count())
            dve.tensor_tensor(biased[:, :, 0:E3], prob[:, :, 0:E3], spread(biases[:], 1, TILES), ALU.add).then_inc(chain.next(), 1)
            dve.wait_ge(chain.sem, chain.count())
            for n in range(TILES):
                last = dve.max(top[:, n, :], biased[:, n, :])
            last.then_inc(chain.next(), 1)
            dve.wait_ge(chain.sem, chain.count())
            for n in range(TILES):
                last = dve.max_index(top_at[:, n, :], top[:, n, :], biased[:, n, :])
            last.then_inc(chain.next(), 1)
            dve.wait_ge(chain.sem, chain.count())
            dve.tensor_copy(top_e[:], top_at[:, :, 0:K3]).then_inc(chain.next(), 1)
            dve.wait_ge(chain.sem, chain.count())
            dve.tensor_tensor(hot[:].rearrange("p n k e -> p (n k) e"), spread(count[:, 0:E3 + 1], 1, TILES * K3),
                                        spread(top_e[:].rearrange("p n k -> p (n k)"), 2, E3 + 1), ALU.is_equal).then_inc(chain.next(), 1)
            dve.wait_ge(chain.sem, chain.count())
            dve.tensor_tensor(hot_prob[:], hot[:], spread(prob[:], 2, K3), ALU.mult).then_inc(chain.next(), 1)
            dve.wait_ge(chain.sem, chain.count())
            dve.tensor_reduce(top_prob[:], hot_prob[:], AX, ALU.add).then_inc(chain.next(), 1)
            dve.wait_ge(chain.sem, chain.count())
            dve.tensor_reduce(total[:], top_prob[:], AX, ALU.add).then_inc(chain.next(), 1)
            dve.wait_ge(chain.sem, chain.count())
            dve.reciprocal(total[:], total[:]).then_inc(chain.next(), 1)
            dve.wait_ge(chain.sem, chain.count())
            dve.tensor_tensor(top_prob[:], top_prob[:], spread(total[:], 2, K3), ALU.mult).then_inc(chain.next(), 1)
            dve.wait_ge(chain.sem, chain.count())
            dve.tensor_tensor(hot_prob[:].rearrange("p n k e -> p (n k) e"), hot[:].rearrange("p n k e -> p (n k) e"),
                                        spread(top_prob[:].rearrange("p n k -> p (n k)"), 2, E3 + 1), ALU.mult).then_inc(chain.next(), 1)
            dve.wait_ge(chain.sem, chain.count())
            dve.tensor_reduce(comb[:, 0:E3, :].rearrange("p e n -> p n e"), hot_prob[:, :, :, 0:E3].rearrange("p n k e -> p n e k"),
                              AX, ALU.add).then_inc(comb_ready.sem, 1)

        @block.tensor
        def _(pe):
            for made in (c_made, logits_made):
                made.grant(pe)
            pe.wait_ge(gate_high.sem, gate_high.at(0, 2))
            with pe.Fori(0, BLOCKS) as i:
                pe.wait_ge(x_low.sem, x_low.at(i, 1))
                pe.wait_ge(mix_low.sem, mix_low.at(i, 1))
                for half in range(2):
                    pe.wait_ge(c_low.sem, c_low.at(i, half - 1))
                    for n in range(2 * DC):
                        j, k = 2 * half + n // DC, n % DC
                        last = product(pe, banks[half][:, n * P:(n + 1) * P], x_now, mix, [j],
                                       lambda a, jj: a[:, jj, k * P:(k + 1) * P], lambda a, jj: a[:, jj, :])
                    last.then_inc(c_made.sem, 1)
                pe.wait_ge(c_low.sem, c_low.at(i, 2))
                for j in range(J):
                    last = product(pe, b_g[:, bass.ds(i * (J * (E3 + 1)) + j * (E3 + 1), E3 + 1)], cT, gate, range(DC),
                                   lambda a, k: a[:, j, k, :], lambda a, k: a[:, k, :])
                last.then_inc(logits_made.sem, 1)
            pe.wait_ge(comb_ready.sem, comb_ready.at(0, 1))
            pe.transpose(b_t[:, 0:P], comb[:].rearrange("p e n -> p (e n)"), ident).then_inc(combT_made.sem, 1)


def build_program(nc, names, args, out):
    io = dict(zip(names, args))
    with ExitStack() as ctx:
        def sb(name, shape, dt=F32):
            return ctx.enter_context(nc.sbuf_tensor(name, shape, dt))

        def dram(name, shape):
            return nc.dram_tensor(name, shape, F32, kind="Internal").ap()

        rows, rows_out = dram("expert_rows", [E0 * CAP, D]), dram("expert_results", [E0 * CAP, D])
        combine1T, combine3T = dram("combine1T", [E1, T]), dram("combine3T", [E3 + 1, T])
        psum = ctx.enter_context(nc.psum_tensor("psum", [P, 8, 512], F32))
        consts = sb("consts", [P, CONSTANTS.shape[1]])
        mixes = sb("mixes", [P, TILES, SEQ])
        slots, weights_eff = sb("slots", [P, TILES, 2], U32), sb("weights_eff", [P, TILES, 2])
        sems = Semaphores(nc)
        attention_phase(nc, sems, io, psum, consts, slots, weights_eff, mixes, rows)
        capacity_experts_phase(nc, sems, io, psum, consts, rows, rows_out)
        sems.clear()

        x, xT = sb("residual", [P, TILES, D]), Split(sb, "inputs", [P, DC, T])
        chosen_layer_phase(nc, sems, io, psum, consts, slots, weights_eff, rows_out, x, xT, combine1T)
        gated_experts_phase(nc, sems, "g", psum, io["gate_1"], io["up_1"], io["down_1"], combine1T, F1, E1, 3, x, xT)
        quantised_phase(nc, sems, io, psum, consts, x)
        position_mix_phase(nc, sems, io, psum, consts, mixes, x, xT, combine3T)
        gated_experts_phase(nc, sems, "s", psum, io["gate_3"], io["up_3"], io["down_3"], combine3T, F3, E3 + 1, 2, x, xT)

        stored = sems.new("stored")
        block = ctx.enter_context(nc.Block())

        @block.sync
        def _(sp):
            sp.dma_start(out.rearrange("s t d -> (s t) d").rearrange("(n p) d -> p n d", p=P), x[:]).then_inc(stored, 16)
            sp.wait_ge(stored, 16)


def laid_out(inputs):
    take = {k: np.asarray(v) for k, v in inputs.items()}
    x = take["x"].reshape(T, D)
    swap = {
        "constants": CONSTANTS,
        "x": x,
        "xT": x.T,
        "w_attention": np.stack([take["L0_cond_W" + n].T for n in "qkvo"]),
        "b1": take["L0_ffn_b1"].reshape(E0, F0 // P, P).transpose(2, 0, 1).reshape(P, -1),
        "gate1": take["L1_ffn_gate_weight"].T,
        "gate_1": take["L1_ffn_gate_up_proj"][:, :F1].transpose(2, 0, 1).reshape(D, -1),
        "up_1": take["L1_ffn_gate_up_proj"][:, F1:].transpose(2, 0, 1).reshape(D, -1),
        "down_1": take["L1_ffn_down_proj"].transpose(0, 2, 1).reshape(-1, D),
        "quant_w1": take["L2_ffn_w1"].T,
        "quant_w2": take["L2_ffn_w2"].T,
        "cond2": take["L2_cond_W"].T,
        "adapter_down": take["L2_cond_A"].reshape(P, D).T,
        "adapter_up": take["L2_cond_Bm"].transpose(0, 2, 1).reshape(P, D),
        "mix_rows": take["L3_cond_weights"].reshape(S3 * SEQ, SEQ),
        "gate_3": np.concatenate([take["L3_ffn_W1"], take["L3_ffn_Ws1"][None]]).transpose(1, 0, 2).reshape(D, -1),
        "up_3": np.concatenate([take["L3_ffn_Wg"], take["L3_ffn_Wsg"][None]]).transpose(1, 0, 2).reshape(D, -1),
        "down_3": np.concatenate([take["L3_ffn_W2"], take["L3_ffn_Ws2"][None]]).reshape(-1, D),
    }
    same = ("cond_1", "L0_ffn_gating_w", "L0_ffn_w1", "L0_ffn_w2", "L0_ffn_b2", "itok_B_0_15", "itok_B_0_6", "itok_B_1_198",
            "L1_cond_W", "L1_cond_b", "L1_ffn_similarity", "L2_ffn_g1", "L2_ffn_g2", "L2_cond_scalings",
            "L3_ffn_gate_w", "L3_ffn_gate_b", "L3_ffn_biases")
    swap.update({name: take[name] for name in same})
    return {name: np.ascontiguousarray(a) for name, a in swap.items()}


def kernel(**inputs):
    import concourse.bacc as bacc
    from concourse.bass_utils import run_bass_kernel_spmd

    nc = bacc.Bacc("TRN2", target_bir_lowering=False, num_devices=1)
    arrays = laid_out(inputs)
    args = [nc.dram_tensor(name, a.shape, mybir.dt.from_np(a.dtype), kind="ExternalInput").ap() for name, a in arrays.items()]
    out = nc.dram_tensor("out", (SEQS, SEQ, D), F32, kind="ExternalOutput").ap()
    build_program(nc, list(arrays), args, out)
    result = run_bass_kernel_spmd(nc, [arrays], core_ids=[0])
    return result.results[0]["out"]
```

```python
from contextlib import ExitStack

import numpy as np

import concourse.bass as bass
from concourse import mybir

F32 = mybir.dt.float32
F32R = mybir.dt.float32r
BF16 = mybir.dt.bfloat16
U32 = mybir.dt.uint32
I32 = mybir.dt.int32
ALU = mybir.AluOpType
ACT = mybir.ActivationFunctionType
AX = mybir.AxisListType.X

P = 128
D = 256
DC = D // P
SEQS, SEQ = 64, 32
T = SEQS * SEQ
TILES = T // P
TSEQ = P // SEQ
BLOCK = 512
BLOCKS = T // BLOCK
BTILES = BLOCK // P
BSEQ = BLOCK // SEQ
HEADS, HD = 16, 16
CHEADS = P // HD
E0, F0 = 8, 1024
CAP = (2 * T * 5 // 4 + E0 - 1) // E0
E1, F1, K1, PRIM1 = 32, 96, 8, 4
W1TAB = 16
A2, R2, F2 = 8, 16, 1024
S3, E3, F3, K3 = 200, 7, 256, 3
MAGIC = 1.5 * 2.0 ** 23

CONST = {}


def constants():
    p = np.arange(P)
    parts = {
        "ident": np.eye(P),
        "before": p[:, None] < p[None, :],
        "ones": np.ones((P, P)),
        "causal": np.where(np.arange(SEQ)[None, :] <= (p % SEQ)[:, None], 0.0, -1e30),
        "head": (p // HD)[:, None] == np.arange(CHEADS)[None, :],
        "quad": (p // SEQ)[:, None] == np.arange(TSEQ)[None, :],
        "count": np.broadcast_to(np.arange(32), (P, 32)),
        "adapter": (p // R2)[:, None],
        "position": (p % SEQ)[:, None],
    }
    at = 0
    for name, part in parts.items():
        CONST[name] = (at, at + part.shape[1])
        at += part.shape[1]
    return np.ascontiguousarray(np.concatenate([np.asarray(x, np.float32) for x in parts.values()], axis=1))


CONSTANTS = constants()


class Signal:

    def __init__(self, sem, per=1, free=0):
        self.sem, self.per, self.free = sem, per, free

    def at(self, i, n):
        value = i * self.per + (n + self.free)
        assert not isinstance(value, int) or value > 0
        return value

    def grant(self, eng):
        eng.sem_inc(self.sem, self.free)


class Semaphores:

    def __init__(self, nc):
        self.nc, self.taken = nc, []

    def new(self, name):
        self.taken.append(self.nc.alloc_semaphore(name))
        return self.taken[-1]

    def clear(self):
        self.nc.clear_and_free_semaphores(self.taken)
        self.nc.all_engine_barrier()
        self.taken = []


class Chain:

    def __init__(self, eng, sem, per):
        self.eng, self.sem, self.per = eng, sem, per
        self.i, self.n = 0, 0

    def start(self, i):
        self.i, self.n = i, 0

    def next(self):
        self.n += 1
        return self.sem

    def count(self):
        return self.i * self.per + self.n

    def end(self):
        assert self.n == self.per, f"steps in a pass: {self.n}, not {self.per}"


def spread(ap, axis, n):
    ap = ap.unsqueeze(axis)
    shape = list(ap.shape)
    shape[axis] = n
    return ap.broadcast_to(shape)


def const(consts, name):
    a, b = CONST[name]
    return consts[:, a:b]


class Split:

    def __init__(self, new, name, shape):
        self.high, self.low = new(name + "_high", shape, F32R), new(name + "_low", shape, F32R)

    @property
    def high_read(self):
        return self.high[:].bitcast(F32)

    def passes(self, other):
        return ((self.high, other.high), (self.high, other.low), (self.low, other.high))


def product(pe, out, stationary, moving, ks, pick_s, pick_m, start=True, stop=True):
    last = None
    n, count = 0, 3 * len(ks)
    for k in ks:
        for s, m in stationary.passes(moving):
            last = pe.matmul(out, pick_s(s, k), pick_m(m, k), start=start and n == 0, stop=stop and n == count - 1,
                             skip_group_check=True)
            n += 1
    return last


def attention_phase(nc, sems, io, psum, consts, slots, weights_eff, mixes, rows):
    with ExitStack() as ctx:
        def sb(name, shape, dt=F32):
            return ctx.enter_context(nc.sbuf_tensor("a_" + name, shape, dt))

        def sig(name, per=1, free=0):
            return Signal(sems.new("a_" + name), per, free)

        xT = sb("xT", [P, DC, T])
        xs = Split(sb, "x", [P, DC, BLOCK])
        w_raw = sb("w_raw", [P, 4, DC, D])
        ws = Split(sb, "w", [P, 4, DC, D])
        gate_w = sb("gate_w", [P, DC, E0])
        beta = sb("beta", [P, SEQS])
        q = sb("q", [P, DC, BLOCK])
        k = sb("k", [P, DC, BLOCK])
        k_heads = sb("k_heads", [P, BSEQ, DC, CHEADS, SEQ])
        v_heads = sb("v_heads", [P, BSEQ, 4, 4, HD])
        score = sb("score", [P, 2, HEADS, SEQ])
        peak = sb("peak", [P, 2, HEADS])
        total = sb("total", [P, 2, HEADS])
        prob = sb("prob", [P, 2, HEADS, SEQ])
        probT = sb("probT", [P, 2, 4, P])
        os_ = Split(sb, "o", [P, 2, DC, P])
        y = sb("y", [P, BTILES, D])
        yT = sb("yT", [P, 2, DC, P])
        zeros = sb("zeros", [P, 2560])
        g_peak = sb("g_peak", [P, BTILES])
        g_exp = sb("g_exp", [P, BTILES, E0])
        g_sum = sb("g_sum", [P, BTILES])
        gates = sb("gates", [P, BTILES, E0])
        top = sb("top", [P, BTILES, 8])
        top_at = sb("top_at", [P, BTILES, 8], U32)
        top_e = sb("top_e", [P, BTILES, 2])
        w_sum = sb("w_sum", [P, BTILES])
        w_norm = sb("w_norm", [P, BTILES, 2])
        chosen = sb("chosen", [P, BTILES, 2, E0])
        taken = sb("taken", [P, BTILES, E0])
        before = sb("before", [P, BTILES + 1, E0])
        place_of = sb("place_of", [P, BTILES, 2, E0])
        place = sb("place", [P, BTILES, 2])
        valid = sb("valid", [P, BTILES, 2])
        lost = sb("lost", [P, BTILES, 2])
        slot = sb("slot", [P, BTILES, 2])
        target = sb("target", [P, BTILES, 2])
        scatter_at = sb("scatter_at", [P, BTILES, 2], U32)

        mix_id = sb("mix_id", [P, SEQS], I32)
        mix_own = sb("mix_own", [P, TILES, TSEQ])
        mix_row_f = sb("mix_row_f", [P, TILES])
        mix_row = sb("mix_row", [P, TILES], U32)

        mix_ids_loaded = sig("mix_ids_loaded")
        mix_rows_ready = sig("mix_rows_ready")
        mixes_loaded = sig("mixes_loaded")
        loaded = sig("loaded")
        weights_loaded = sig("weights_loaded")
        rows_cleared = sig("rows_cleared")
        zeros_set = sig("zeros_set")
        beta_ready = sig("beta_ready")
        weights_split = sig("weights_split")
        x_high = sig("x_high")
        x_low = sig("x_low")
        q_made = sig("q_made", 2)
        k_made = sig("k_made", 2)
        v_made = sig("v_made", 1, 1)
        v_cleared = sig("v_cleared")
        q_ready = sig("q_ready", 2)
        k_copied = sig("k_copied", 2)
        k_heads_dve = sig("k_heads_dve")
        k_heads_act = sig("k_heads_act")
        v_ready_act = sig("v_ready_act")
        v_ready_dve = sig("v_ready_dve")
        s_made = sig("s_made", BTILES, 2)
        s_masked = sig("s_masked", BTILES, 2)
        s_shifted = sig("s_shifted", BTILES)
        s_exp = sig("s_exp", BTILES)
        p_ready = sig("p_ready", BTILES, 2)
        pT_made = sig("pT_made", BTILES, 2)
        pT_ready = sig("pT_ready", BTILES, 2)
        o_made = sig("o_made", BTILES, 2)
        o_high = sig("o_high", BTILES)
        o_low = sig("o_low", BTILES, 2)
        y_made = sig("y_made", BTILES, 2)
        y_ready = sig("y_ready", BTILES, 2)
        yT_made = sig("yT_made", BTILES)
        yT_ready = sig("yT_ready", BTILES, 2)
        logits_made = sig("logits_made")
        g_shifted = sig("g_shifted")
        g_exped = sig("g_exped")
        taken_ready = sig("taken_ready")
        places_made = sig("places_made")
        targets_ready = sig("targets_ready")
        scattered = sig("scattered", 2 * BTILES * 16)
        y_left = sig("y_left", 1, 1)
        steps = sig("steps")
        pool_passed = sig("pool_passed")
        dve_passed = sig("dve_passed")
        block = ctx.enter_context(nc.Block())

        ident = const(consts, "ident")
        banks = [psum[:, n, :] for n in range(8)]
        v_psum = psum[:, 4:6, :].rearrange("p n (j g h d) -> p (n j) g h d", g=4, h=4, d=HD)

        def place_values(engine, i, quads):
            engine.wait_ge(v_made.sem, v_made.at(i, 1))
            engine.wait_ge(o_made.sem, o_made.at(i, 0))
            for b in quads:
                for h in range(4):
                    src = v_psum[b * SEQ:(b + 1) * SEQ, :, :, h, :]
                    dst = v_heads[h * SEQ:(h + 1) * SEQ, b:BSEQ:TSEQ, :, h, :]
                    if engine is nc.scalar:
                        last = engine.activation(dst, src, ACT.Copy)
                    else:
                        last = engine.tensor_copy(dst, src)
            return last
        b_q, b_k = banks[0:2], banks[2:4]
        b_s, b_pT, b_y, b_yT, b_o, b_g = banks[0:2], banks[2:4], banks[4], banks[5], banks[6], banks[7]

        def stages(tile_steps):
            for s in range(BTILES + max(lag for lag, _ in tile_steps)):
                for lag, work in tile_steps:
                    if 0 <= s - lag < BTILES:
                        work(s - lag)

        @block.sync
        def _(sp):
            sp.dma_start(consts[:], io["constants"]).then_inc(loaded.sem, 16)
            sp.dma_start(xT[:], io["xT"].rearrange("(c p) t -> p c t", p=P)).then_inc(loaded.sem, 16)
            sp.dma_start(w_raw[:], io["w_attention"].rearrange("w (c p) e -> p w c e", p=P)).then_inc(weights_loaded.sem, 16)
            sp.dma_start(gate_w[:], io["L0_ffn_gating_w"].rearrange("(c p) e -> p c e", p=P)).then_inc(weights_loaded.sem, 16)
            sp.dma_start(beta[:], io["cond_1"].rearrange("b o -> (b o)").partition_broadcast(P)).then_inc(loaded.sem, 16)
            sp.dma_start(mix_id[:], io["itok_B_1_198"].partition_broadcast(P)).then_inc(mix_ids_loaded.sem, 16)
            sp.wait_ge(zeros_set.sem, zeros_set.at(0, 1))
            clear = rows.rearrange("(n p r) d -> n p (r d)", p=P, r=10)
            for n in range(clear.shape[0]):
                sp.dma_start(clear[n], zeros[:]).then_inc(rows_cleared.sem, 16)

        @block.gpsimd
        def _(pool):
            y_left.grant(pool)
            pool.memset(v_heads[:], 0.0).then_inc(v_cleared.sem, 1)
            pool.wait_ge(mix_rows_ready.sem, mix_rows_ready.at(0, 5))
            for n in range(TILES):
                pool.indirect_dma_start(mixes[:, n, :], None, io["mix_rows"],
                                        bass.IndirectOffsetOnAxis(ap=mix_row[:, n:n + 1], axis=0)).then_inc(mixes_loaded.sem, 16)
            pool.wait_ge(rows_cleared.sem, rows_cleared.at(0, 16 * (E0 * CAP // (10 * P))))

            def scatter(i):
                pool.wait_ge(targets_ready.sem, targets_ready.at(i, 1))
                pool.sem_inc(pool_passed.sem, 1)
                for j in range(BTILES):
                    for c in range(2):
                        pool.indirect_dma_start(
                            rows, bass.IndirectOffsetOnAxis(ap=scatter_at[:, j, c:c + 1], axis=0), y[:, j, :], None,
                            bounds_check=E0 * CAP - 1, oob_is_err=False).then_inc(scattered.sem, 16)
                pool.wait_ge(scattered.sem, scattered.at(i, 2 * BTILES * 16))
                pool.sem_inc(y_left.sem, 1)

            with pool.Fori(0, BLOCKS) as i:
                scatter(i)
            pool.wait_ge(mixes_loaded.sem, mixes_loaded.at(0, 16 * TILES))

        @block.scalar
        def _(act):
            act.wait_ge(v_cleared.sem, v_cleared.at(0, 1))
            act.wait_ge(weights_loaded.sem, weights_loaded.at(0, 32))
            act.activation(ws.high[:], w_raw[:], ACT.Copy).then_inc(weights_split.sem, 1)
            act.wait_ge(loaded.sem, loaded.at(0, 48))
            head = const(consts, "head")

            def project(i):
                act.wait_ge(v_made.sem, v_made.at(i, 0))
                act.activation(xs.high[:], xT[:, :, bass.ds(i * BLOCK, BLOCK)], ACT.Copy).then_inc(x_high.sem, 1)
                for c in range(DC):
                    act.wait_ge(k_made.sem, k_made.at(i, c + 1))
                    act.activation(k[:, c, :], b_k[c], ACT.Copy).then_inc(k_copied.sem, 1)
                act.wait_ge(k_copied.sem, k_copied.at(i, 2))
                act.wait_ge(s_made.sem, s_made.at(i, 0))
                for h in range(CHEADS):
                    last = act.activation(k_heads[:, :, 1, h, :], k[:, 1, :].rearrange("p (b t) -> p b t", t=SEQ),
                                          ACT.Copy, scale=head[:, h:h + 1])
                last.then_inc(k_heads_act.sem, 1)
                place_values(act, i, (0, 1)).then_inc(v_ready_act.sem, 1)

            def tiles(i):
                def exp(j):
                    act.wait_ge(s_shifted.sem, s_shifted.at(i, j + 1))
                    act.activation(score[:, j % 2], score[:, j % 2], ACT.Exp).then_inc(s_exp.sem, 1)

                def turn(j):
                    act.wait_ge(pT_made.sem, pT_made.at(i, j + 1))
                    act.wait_ge(o_made.sem, o_made.at(i, j - 1))
                    act.activation(probT[:, j % 2], b_pT[j % 2], ACT.Copy).then_inc(pT_ready.sem, 1)

                def o(j):
                    act.wait_ge(o_made.sem, o_made.at(i, j + 1))
                    act.wait_ge(y_made.sem, y_made.at(i, j - 1))
                    act.activation(os_.high[:, j % 2], b_o[:, 0:D], ACT.Copy).then_inc(o_high.sem, 1)

                def y_out(j):
                    act.wait_ge(y_made.sem, y_made.at(i, j + 1))
                    if j == 0:
                        act.wait_ge(y_left.sem, y_left.at(i, 0))
                    act.activation(y[:, j, :], b_y[:, 0:D], ACT.Copy).then_inc(y_ready.sem, 1)

                def yT_out(j):
                    act.wait_ge(yT_made.sem, yT_made.at(i, j + 1))
                    act.activation(yT[:, j % 2], b_yT[:, 0:D], ACT.Copy).then_inc(yT_ready.sem, 1)

                stages([(0, exp), (2, turn), (3, o), (4, y_out), (5, yT_out)])
                act.wait_ge(g_shifted.sem, g_shifted.at(i, 1))
                act.activation(g_exp[:], g_exp[:], ACT.Exp).then_inc(g_exped.sem, 1)

            for made in (pT_ready, y_ready, yT_ready):
                made.grant(act)
            with act.Fori(0, BLOCKS) as i:
                project(i)
                tiles(i)

        @block.vector
        def _(dve):
            chain = Chain(dve, steps.sem, 34)
            s_masked.grant(dve)
            o_low.grant(dve)
            p_ready.grant(dve)
            dve.memset(zeros[:], 0.0).then_inc(zeros_set.sem, 1)
            dve.wait_ge(v_cleared.sem, v_cleared.at(0, 1))
            dve.wait_ge(weights_split.sem, weights_split.at(0, 1))
            dve.tensor_tensor(ws.low[:], w_raw[:], ws.high_read, ALU.subtract).then_inc(weights_split.sem, 1)
            dve.wait_ge(loaded.sem, loaded.at(0, 48))
            dve.tensor_scalar(beta[:], beta[:], 4.0, 0.25, ALU.min, ALU.mult).then_inc(beta_ready.sem, 1)
            dve.memset(before[:, 0, :], 0.0).then_inc(beta_ready.sem, 1)
            dve.wait_ge(beta_ready.sem, beta_ready.at(0, 2))
            dve.wait_ge(mix_ids_loaded.sem, mix_ids_loaded.at(0, 16))
            dve.tensor_copy(mix_own[:].rearrange("p n b -> p (n b)"), mix_id[:]).then_inc(mix_rows_ready.sem, 1)
            dve.wait_ge(mix_rows_ready.sem, mix_rows_ready.at(0, 1))
            dve.tensor_tensor(mix_own[:], mix_own[:], spread(const(consts, "quad"), 1, TILES), ALU.mult).then_inc(mix_rows_ready.sem, 1)
            dve.wait_ge(mix_rows_ready.sem, mix_rows_ready.at(0, 2))
            dve.tensor_reduce(mix_row_f[:], mix_own[:], AX, ALU.add).then_inc(mix_rows_ready.sem, 1)
            dve.wait_ge(mix_rows_ready.sem, mix_rows_ready.at(0, 3))
            dve.tensor_scalar(mix_row_f[:], mix_row_f[:], float(SEQ), const(consts, "position"), ALU.mult, ALU.add).then_inc(mix_rows_ready.sem, 1)
            dve.wait_ge(mix_rows_ready.sem, mix_rows_ready.at(0, 4))
            dve.tensor_copy(mix_row[:], mix_row_f[:]).then_inc(mix_rows_ready.sem, 1)
            head, causal, count = (const(consts, n) for n in ("head", "causal", "count"))

            def project(i):
                dve.wait_ge(x_high.sem, x_high.at(i, 1))
                dve.tensor_tensor(xs.low[:], xT[:, :, bass.ds(i * BLOCK, BLOCK)], xs.high_read, ALU.subtract).then_inc(x_low.sem, 1)
                for c in range(DC):
                    dve.wait_ge(q_made.sem, q_made.at(i, c + 1))
                    dve.tensor_tensor(q[:, c, :].rearrange("p (b t) -> p b t", t=SEQ),
                                      b_q[c].rearrange("p (b t) -> p b t", t=SEQ),
                                      spread(beta[:, bass.ds(i * BSEQ, BSEQ)], 2, SEQ), ALU.mult).then_inc(q_ready.sem, 1)
                dve.wait_ge(k_copied.sem, k_copied.at(i, 1))
                for h in range(CHEADS):
                    last = dve.tensor_scalar(k_heads[:, :, 0, h, :], k[:, 0, :].rearrange("p (b t) -> p b t", t=SEQ),
                                             head[:, h:h + 1], None, ALU.mult)
                last.then_inc(k_heads_dve.sem, 1)
                place_values(dve, i, (2, 3)).then_inc(v_ready_dve.sem, 1)

            def tiles(i):
                def shift(j):
                    sc = score[:, j % 2]
                    dve.wait_ge(s_made.sem, s_made.at(i, j + 1))
                    dve.wait_ge(p_ready.sem, p_ready.at(i, j - 1))
                    dve.tensor_tensor(sc, b_s[j % 2].rearrange("p (h t) -> p h t", t=SEQ), spread(causal, 1, HEADS),
                                      ALU.add).then_inc(s_masked.sem, 1)
                    dve.wait_ge(s_masked.sem, s_masked.at(i, j + 1))
                    dve.tensor_reduce(peak[:, j % 2], sc, AX, ALU.max).then_inc(chain.next(), 1)
                    dve.wait_ge(chain.sem, chain.count())
                    dve.tensor_tensor(sc, sc, spread(peak[:, j % 2], 2, SEQ), ALU.subtract).then_inc(s_shifted.sem, 1)

                def normalise(j):
                    sc, tot = score[:, j % 2], total[:, j % 2]
                    dve.wait_ge(s_exp.sem, s_exp.at(i, j + 1))
                    dve.tensor_reduce(tot, sc, AX, ALU.add).then_inc(chain.next(), 1)
                    dve.wait_ge(chain.sem, chain.count())
                    dve.reciprocal(tot, tot).then_inc(chain.next(), 1)
                    dve.wait_ge(chain.sem, chain.count())
                    dve.wait_ge(pT_made.sem, pT_made.at(i, j - 1))
                    dve.tensor_tensor(prob[:, j % 2], sc, spread(tot, 2, SEQ), ALU.mult).then_inc(p_ready.sem, 1)

                def o(j):
                    dve.wait_ge(o_high.sem, o_high.at(i, j + 1))
                    dve.tensor_tensor(os_.low[:, j % 2], b_o[:, 0:D].rearrange("p (c t) -> p c t", t=P),
                                      os_.high[:, j % 2].bitcast(F32), ALU.subtract).then_inc(o_low.sem, 1)

                stages([(0, shift), (1, normalise), (3, o)])

            def route(i):
                logits = b_g[:, 0:BTILES * E0].rearrange("p (j e) -> p j e", e=E0)
                dve.wait_ge(logits_made.sem, logits_made.at(i, 1))
                dve.tensor_reduce(g_peak[:], logits, AX, ALU.max).then_inc(chain.next(), 1)
                dve.wait_ge(chain.sem, chain.count())
                dve.tensor_tensor(g_exp[:], logits, spread(g_peak[:], 2, E0), ALU.subtract).then_inc(g_shifted.sem, 1)
                dve.wait_ge(g_exped.sem, g_exped.at(i, 1))
                dve.tensor_reduce(g_sum[:], g_exp[:], AX, ALU.add).then_inc(chain.next(), 1)
                dve.wait_ge(chain.sem, chain.count())
                dve.reciprocal(g_sum[:], g_sum[:]).then_inc(chain.next(), 1)
                dve.wait_ge(chain.sem, chain.count())
                dve.tensor_tensor(gates[:], g_exp[:], spread(g_sum[:], 2, E0), ALU.mult).then_inc(chain.next(), 1)
                dve.wait_ge(chain.sem, chain.count())
                dve.sem_inc(dve_passed.sem, 1)
                for j in range(BTILES):
                    last = dve.max(top[:, j, :], gates[:, j, :])
                last.then_inc(chain.next(), 1)
                dve.wait_ge(chain.sem, chain.count())
                dve.sem_inc(dve_passed.sem, 1)
                for j in range(BTILES):
                    last = dve.max_index(top_at[:, j, :], top[:, j, :], gates[:, j, :])
                last.then_inc(chain.next(), 1)
                dve.wait_ge(chain.sem, chain.count())
                dve.tensor_tensor(w_sum[:], top[:, :, 0], top[:, :, 1], ALU.add)
                dve.tensor_copy(top_e[:], top_at[:, :, 0:2]).then_inc(chain.next(), 1)
                dve.wait_ge(chain.sem, chain.count())
                dve.tensor_scalar(w_sum[:], w_sum[:], 1e-8, None, ALU.add).then_inc(chain.next(), 1)
                dve.tensor_tensor(chosen[:], spread(spread(count[:, 0:E0], 1, 2), 1, BTILES),
                                            spread(top_e[:], 3, E0), ALU.is_equal).then_inc(chain.next(), 1)
                dve.wait_ge(chain.sem, chain.count())
                dve.reciprocal(w_sum[:], w_sum[:]).then_inc(chain.next(), 1)
                dve.tensor_tensor(taken[:], chosen[:, :, 0, :], chosen[:, :, 1, :], ALU.add).then_inc(chain.next(), 1)
                dve.wait_ge(chain.sem, chain.count())
                dve.tensor_tensor(w_norm[:], top[:, :, 0:2], spread(w_sum[:], 2, 2), ALU.mult).then_inc(chain.next(), 1)
                for j in range(BTILES):
                    last = dve.tensor_tensor(before[:, j + 1, :], before[:, j, :], taken[:, j, :], ALU.add)
                    if j < BTILES - 1:
                        last.then_inc(chain.next(), 1)
                        dve.wait_ge(chain.sem, chain.count())
                last.then_inc(taken_ready.sem, 1)

            def assign(i):
                dve.wait_ge(taken_ready.sem, taken_ready.at(i, 1))
                dve.wait_ge(places_made.sem, places_made.at(i, 1))
                counts = b_g[:, 64:64 + BTILES * E0].rearrange("p (j e) -> p j e", e=E0)
                for c in range(2):
                    last = dve.tensor_tensor(place_of[:, :, c, :], chosen[:, :, c, :], counts, ALU.mult)
                last.then_inc(chain.next(), 1)
                dve.tensor_copy(before[:, 0, :], before[:, BTILES, :]).then_inc(chain.next(), 1)
                dve.wait_ge(chain.sem, chain.count())
                dve.tensor_reduce(place[:], place_of[:], AX, ALU.add).then_inc(chain.next(), 1)
                dve.wait_ge(chain.sem, chain.count())
                dve.tensor_scalar(valid[:], place[:], float(CAP), None, ALU.is_lt).then_inc(chain.next(), 1)
                dve.tensor_scalar(place[:], place[:], float(CAP - 1), None, ALU.min).then_inc(chain.next(), 1)
                dve.wait_ge(chain.sem, chain.count())
                dve.tensor_scalar(lost[:], valid[:], -1e6, 1e6, ALU.mult, ALU.add)
                dve.scalar_tensor_tensor(slot[:], top_e[:], float(CAP), place[:], ALU.mult, ALU.add).then_inc(chain.next(), 1)
                dve.wait_ge(chain.sem, chain.count())
                dve.tensor_tensor(target[:], slot[:], lost[:], ALU.add).then_inc(chain.next(), 1)
                dve.tensor_copy(slots[:, bass.ds(i * BTILES, BTILES), :], slot[:])
                dve.tensor_tensor(weights_eff[:, bass.ds(i * BTILES, BTILES), :], w_norm[:], valid[:], ALU.mult)
                dve.wait_ge(chain.sem, chain.count())
                dve.wait_ge(y_left.sem, y_left.at(i, 0))
                dve.tensor_copy(scatter_at[:], target[:]).then_inc(targets_ready.sem, 1)

            with dve.Fori(0, BLOCKS) as i:
                chain.start(i)
                project(i)
                tiles(i)
                route(i)
                assign(i)
                chain.end()

        @block.tensor
        def _(pe):
            pe.wait_ge(weights_split.sem, weights_split.at(0, 2))
            pe.wait_ge(loaded.sem, loaded.at(0, 48))
            for made in (v_made, s_made, pT_made, o_made, y_made):
                made.grant(pe)

            def project(i):
                pe.wait_ge(x_high.sem, x_high.at(i, 1))
                pe.wait_ge(x_low.sem, x_low.at(i, 1))
                for w, made, out in ((0, q_made, b_q), (1, k_made, b_k)):
                    for c in range(DC):
                        if w == 0:
                            pe.wait_ge(s_masked.sem, s_masked.at(i, 0))
                        else:
                            pe.wait_ge(pT_ready.sem, pT_ready.at(i, 0))
                        product(pe, out[c], ws, xs, range(DC), lambda a, kk: a[:, w, kk, c * P:(c + 1) * P],
                                lambda a, kk: a[:, kk, :]).then_inc(made.sem, 1)
                pe.wait_ge(y_ready.sem, y_ready.at(i, 0))
                pe.wait_ge(yT_ready.sem, yT_ready.at(i, 0))
                for j in range(BTILES):
                    last = product(pe, banks[4 + j // 2][:, (j % 2) * D:(j % 2 + 1) * D], xs, ws, range(DC),
                                   lambda a, kk: a[:, kk, j * P:(j + 1) * P], lambda a, kk: a[:, 2, kk, :])
                last.then_inc(v_made.sem, 1)

            def tiles(i):
                def scores(j):
                    if j == 0:
                        pe.wait_ge(q_ready.sem, q_ready.at(i, 2))
                        pe.wait_ge(k_heads_dve.sem, k_heads_dve.at(i, 1))
                        pe.wait_ge(k_heads_act.sem, k_heads_act.at(i, 1))
                    if j < 2:
                        pass
                    else:
                        pe.wait_ge(s_masked.sem, s_masked.at(i, j - 1))
                    for c in range(DC):
                        for b in range(TSEQ):
                            at = j * TSEQ + b
                            last = pe.matmul(b_s[j % 2][b * SEQ:(b + 1) * SEQ, c * D:(c + 1) * D],
                                             q[:, c, at * SEQ:(at + 1) * SEQ],
                                             k_heads[:, at, c].rearrange("p h t -> p (h t)"), start=True, stop=True,
                                             skip_group_check=True)
                    last.then_inc(s_made.sem, 1)

                def turn(j):
                    pe.wait_ge(p_ready.sem, p_ready.at(i, j + 1))
                    if j == 0:
                        pe.wait_ge(k_copied.sem, k_copied.at(i, 2))
                    pe.wait_ge(pT_ready.sem, pT_ready.at(i, j - 1))
                    for g in range(4):
                        last = pe.transpose(b_pT[j % 2][:, g * P:(g + 1) * P],
                                            prob[:, j % 2, 4 * g:4 * g + 4, :].rearrange("p h t -> p (h t)"), ident)
                    last.then_inc(pT_made.sem, 1)

                def mix(j):
                    pe.wait_ge(pT_ready.sem, pT_ready.at(i, j + 1))
                    if j == 0:
                        pe.wait_ge(v_ready_act.sem, v_ready_act.at(i, 1))
                        pe.wait_ge(v_ready_dve.sem, v_ready_dve.at(i, 1))
                    pe.wait_ge(o_low.sem, o_low.at(i, j))
                    for g in range(4):
                        for b in range(TSEQ):
                            out = b_o[64 * (g % 2):64 * (g % 2) + 64, (g // 2) * P + b * SEQ:(g // 2) * P + (b + 1) * SEQ]
                            last = pe.matmul(out, v_heads[:, j * TSEQ + b, g].rearrange("p h d -> p (h d)"),
                                             probT[:, j % 2, g, b * SEQ:(b + 1) * SEQ], start=True, stop=True,
                                             skip_group_check=True)
                    last.then_inc(o_made.sem, 1)

                def out(j):
                    pe.wait_ge(o_high.sem, o_high.at(i, j + 1))
                    pe.wait_ge(o_low.sem, o_low.at(i, j + 1))
                    pe.wait_ge(y_ready.sem, y_ready.at(i, j))
                    product(pe, b_y[:, 0:D], os_, ws, range(DC), lambda a, kk: a[:, j % 2, kk, :],
                            lambda a, kk: a[:, 3, kk, :]).then_inc(y_made.sem, 1)

                def turn_y(j):
                    pe.wait_ge(y_ready.sem, y_ready.at(i, j + 1))
                    pe.wait_ge(yT_ready.sem, yT_ready.at(i, j))
                    for c in range(DC):
                        last = pe.transpose(b_yT[:, c * P:(c + 1) * P], y[:, j, c * P:(c + 1) * P], ident)
                    last.then_inc(yT_made.sem, 1)

                def gate(j):
                    pe.wait_ge(yT_ready.sem, yT_ready.at(i, j + 1))
                    for c in range(DC):
                        last = pe.matmul(b_g[:, j * E0:(j + 1) * E0], yT[:, j % 2, c, :], gate_w[:, c, :],
                                         start=(c == 0), stop=(c == DC - 1), skip_group_check=True)
                    if j == BTILES - 1:
                        last.then_inc(logits_made.sem, 1)

                stages([(0, scores), (2, turn), (3, mix), (4, out), (5, turn_y), (6, gate)])

            def places(i):
                pe.wait_ge(taken_ready.sem, taken_ready.at(i, 1))
                pe.matmul(b_g[:, 64:64 + BTILES * E0], const(consts, "before"), taken[:].rearrange("p j e -> p (j e)"),
                          start=True, stop=False, skip_group_check=True)
                pe.matmul(b_g[:, 64:64 + BTILES * E0], const(consts, "ones"),
                          before[:, 0:BTILES, :].rearrange("p j e -> p (j e)"), start=False, stop=True,
                          skip_group_check=True).then_inc(places_made.sem, 1)

            with pe.Fori(0, BLOCKS) as i:
                project(i)
                tiles(i)
                places(i)


def capacity_experts_phase(nc, sems, io, psum, consts, rows, rows_out):
    CT, HALF, FC = CAP // P, CAP // 2, F0 // P
    STEPS = 2 * FC
    with ExitStack() as ctx:
        def sb(name, shape, dt=F32):
            return ctx.enter_context(nc.sbuf_tensor("e_" + name, shape, dt))

        def sig(name, per=1, free=0):
            return Signal(sems.new("e_" + name), per, free)

        w1_raw, w1 = sb("w1_raw", [P, DC, F0]), Split(sb, "w1", [P, DC, F0])
        w2_raw, w2 = sb("w2_raw", [P, FC, D]), Split(sb, "w2", [P, FC, D])
        row = sb("row", [P, CT, D])
        rT = Split(sb, "rT", [P, DC, CAP])
        relu = sb("relu", [P, 4, HALF])
        h = Split(sb, "h", [P, FC, CAP])
        y = sb("y", [P, CT, D])
        b1 = sb("b1", [P, E0 * FC])
        b1_now = sb("b1_now", [P, FC])
        b2 = sb("b2", [P, E0 * D])

        biases_loaded = sig("biases_loaded")
        rows_loaded = sig("rows_loaded", 16)
        w1_loaded = sig("w1_loaded", 16)
        w2_loaded = sig("w2_loaded", 16)
        w1_high, w1_low = sig("w1_high"), sig("w1_low")
        w2_high, w2_low = sig("w2_high"), sig("w2_low")
        rT_made = sig("rT_made", CT)
        rT_high = sig("rT_high", CT)
        rT_low = sig("rT_low", CT)
        h_made = sig("h_made", STEPS)
        h_relu = sig("h_relu", STEPS, 4)
        h_high = sig("h_high", STEPS)
        h_ready = sig("h_ready", STEPS, 4)
        b1_ready = sig("b1_ready")
        sp_passed = sig("sp_passed")
        y_made = sig("y_made", CT, 2)
        y_ready = sig("y_ready", CT, 2)
        y_stored = sig("y_stored", 16, 16)
        block = ctx.enter_context(nc.Block())
        ident = const(consts, "ident")
        banks = [psum[:, n, :] for n in range(8)]
        b_h, b_t, b_y = banks[0:4], banks[4:6], banks[6:8]

        def experts(engine, one):
            with engine.Fori(0, E0 - 1) as e:
                one(e, True)
            one(E0 - 1, False)

        @block.sync
        def _(sp):
            sp.dma_start(b1[:], io["b1"]).then_inc(biases_loaded.sem, 16)
            sp.dma_start(b2[:], io["L0_ffn_b2"].rearrange("e d -> (e d)").partition_broadcast(P)).then_inc(biases_loaded.sem, 16)
            sp.sem_inc(y_stored.sem, 16)

            def load_first(e):
                sp.dma_start(row[:], rows[bass.ds(e * CAP, CAP), :].rearrange("(r p) d -> p r d", p=P)).then_inc(rows_loaded.sem, 16)
                sp.dma_start(w1_raw[:], io["L0_ffn_w1"][bass.ds(e, 1)].rearrange("o (c p) f -> p (o c) f", p=P)).then_inc(w1_loaded.sem, 16)

            def load_second(e):
                sp.dma_start(w2_raw[:], io["L0_ffn_w2"][bass.ds(e, 1)].rearrange("o (f p) d -> p (o f) d", p=P)).then_inc(w2_loaded.sem, 16)

            load_first(0)
            load_second(0)

            def one(e, more):
                if more:
                    sp.wait_ge(rT_made.sem, rT_made.at(e, CT))
                    sp.sem_inc(sp_passed.sem, 1)
                    sp.wait_ge(w1_low.sem, w1_low.at(e, 1))
                    sp.sem_inc(sp_passed.sem, 1)
                    load_first(e + 1)
                    sp.wait_ge(w2_low.sem, w2_low.at(e, 1))
                    sp.sem_inc(sp_passed.sem, 1)
                    load_second(e + 1)
                sp.wait_ge(y_ready.sem, y_ready.at(e, CT))
                sp.sem_inc(sp_passed.sem, 1)
                sp.dma_start(rows_out[bass.ds(e * CAP, CAP), :].rearrange("(r p) d -> p r d", p=P), y[:]).then_inc(y_stored.sem, 16)

            experts(sp, one)
            sp.wait_ge(y_stored.sem, y_stored.at(E0, 0))

        @block.scalar
        def _(act):
            h_relu.grant(act)
            act.wait_ge(biases_loaded.sem, biases_loaded.at(0, 32))

            def prepare(e):
                for r in range(CT):
                    act.wait_ge(rT_made.sem, rT_made.at(e, r + 1))
                    act.activation(rT.high[:, :, r * P:(r + 1) * P], b_t[r % 2][:, 0:D].rearrange("p (c t) -> p c t", t=P),
                                   ACT.Copy).then_inc(rT_high.sem, 1)
                act.wait_ge(w1_loaded.sem, w1_loaded.at(e, 16))
                act.activation(w1.high[:], w1_raw[:], ACT.Copy).then_inc(w1_high.sem, 1)

            def one(e, more):
                act.wait_ge(b1_ready.sem, b1_ready.at(e, 1))
                for m in range(STEPS):
                    if m == 2:
                        act.wait_ge(w2_loaded.sem, w2_loaded.at(e, 16))
                        act.wait_ge(y_made.sem, y_made.at(e, 0))
                        act.activation(w2.high[:], w2_raw[:], ACT.Copy).then_inc(w2_high.sem, 1)
                    act.wait_ge(h_made.sem, h_made.at(e, m + 1))
                    act.wait_ge(h_ready.sem, h_ready.at(e, m - 3))
                    act.activation(relu[:, m % 4], b_h[m % 4][:, 0:HALF], ACT.Relu,
                                   bias=b1_now[:, m // 2:m // 2 + 1]).then_inc(h_relu.sem, 1)
                if more:
                    prepare(e + 1)

            prepare(0)
            experts(act, one)

        @block.vector
        def _(dve):
            h_ready.grant(dve)
            y_ready.grant(dve)
            dve.wait_ge(biases_loaded.sem, biases_loaded.at(0, 32))

            def prepare(e):
                for r in range(CT):
                    dve.wait_ge(rT_high.sem, rT_high.at(e, r + 1))
                    dve.tensor_tensor(rT.low[:, :, r * P:(r + 1) * P], b_t[r % 2][:, 0:D].rearrange("p (c t) -> p c t", t=P),
                                      rT.high[:, :, r * P:(r + 1) * P].bitcast(F32), ALU.subtract).then_inc(rT_low.sem, 1)
                dve.wait_ge(w1_high.sem, w1_high.at(e, 1))
                dve.tensor_tensor(w1.low[:], w1_raw[:], w1.high_read, ALU.subtract).then_inc(w1_low.sem, 1)

            def one(e, more):
                dve.wait_ge(h_relu.sem, h_relu.at(e, 0))
                dve.tensor_scalar(b1_now[:], b1[:, bass.ds(e * FC, FC)], 1.0, None, ALU.mult).then_inc(b1_ready.sem, 1)
                for m in range(STEPS):
                    if m == 3:
                        dve.wait_ge(w2_high.sem, w2_high.at(e, 1))
                        dve.tensor_tensor(w2.low[:], w2_raw[:], w2.high_read, ALU.subtract).then_inc(w2_low.sem, 1)
                    f, part = m // 2, slice((m % 2) * HALF, (m % 2 + 1) * HALF)
                    dve.wait_ge(h_relu.sem, h_relu.at(e, m + 1))
                    if m == 0:
                        dve.wait_ge(y_made.sem, y_made.at(e, 0))
                    dve.tensor_copy(h.high[:, f, part], relu[:, m % 4]).then_inc(h_high.sem, 1)
                    dve.wait_ge(h_high.sem, h_high.at(e, m + 1))
                    dve.tensor_tensor(h.low[:, f, part], relu[:, m % 4], h.high[:, f, part].bitcast(F32),
                                      ALU.subtract).then_inc(h_ready.sem, 1)
                if more:
                    prepare(e + 1)
                dve.wait_ge(y_stored.sem, y_stored.at(e, 0))
                for r in range(CT):
                    dve.wait_ge(y_made.sem, y_made.at(e, r + 1))
                    dve.tensor_tensor(y[:, r, :], b_y[r % 2][:, 0:D], b2[:, bass.ds(e * D, D)], ALU.add).then_inc(y_ready.sem, 1)

            prepare(0)
            experts(dve, one)

        @block.tensor
        def _(pe):
            y_made.grant(pe)

            def prepare(e):
                pe.wait_ge(rows_loaded.sem, rows_loaded.at(e, 16))
                for r in range(CT):
                    if r >= 2:
                        pe.wait_ge(rT_low.sem, rT_low.at(e, r - 1))
                    for c in range(DC):
                        last = pe.transpose(b_t[r % 2][:, c * P:(c + 1) * P], row[:, r, c * P:(c + 1) * P], ident)
                    last.then_inc(rT_made.sem, 1)

            def one(e, more):
                pe.wait_ge(rT_low.sem, rT_low.at(e, CT))
                pe.wait_ge(w1_low.sem, w1_low.at(e, 1))
                for m in range(STEPS):
                    f, part = m // 2, slice((m % 2) * HALF, (m % 2 + 1) * HALF)
                    pe.wait_ge(h_relu.sem, h_relu.at(e, m - 3))
                    product(pe, b_h[m % 4][:, 0:HALF], w1, rT, range(DC), lambda a, k: a[:, k, f * P:(f + 1) * P],
                            lambda a, k: a[:, k, part]).then_inc(h_made.sem, 1)
                if more:
                    prepare(e + 1)
                pe.wait_ge(w2_low.sem, w2_low.at(e, 1))
                pe.wait_ge(h_ready.sem, h_ready.at(e, STEPS))
                for r in range(CT):
                    pe.wait_ge(y_ready.sem, y_ready.at(e, r - 1))
                    product(pe, b_y[r % 2][:, 0:D], h, w2, range(FC), lambda a, k: a[:, k, r * P:(r + 1) * P],
                            lambda a, k: a[:, k, :]).then_inc(y_made.sem, 1)

            prepare(0)
            experts(pe, one)


def chosen_layer_phase(nc, sems, io, psum, consts, slots, weights_eff, rows_out, x, xT, combineT, load_next):
    PAIRS, J = TILES // 2, 2
    with ExitStack() as ctx:
        def sb(name, shape, dt=F32):
            return ctx.enter_context(nc.sbuf_tensor("c_" + name, shape, dt))

        def sem(name):
            return sems.new("c_" + name)

        def sig(name, per=1, free=0):
            return Signal(sem(name), per, free)

        PIECE = 2
        PIECES = W1TAB // PIECE
        w_raw = sb("w_raw", [P, 2, PIECE, DC, D])
        w = Split(sb, "w", [P, W1TAB, DC, D])
        bias_raw, bias = sb("bias_raw", [W1TAB, D]), Split(sb, "bias", [W1TAB, D])
        gate_raw, gate = sb("gate_raw", [P, DC, E1]), Split(sb, "gate", [P, DC, E1])
        ids = sb("ids", [W1TAB, SEQS], I32)
        ids_f = sb("ids_f", [W1TAB, SEQS])
        is_id = sb("is_id", [W1TAB, J, TSEQ, SEQ], F32R)
        sim = sb("sim", [P, 4, E1])
        got = sb("got", [P, TILES, 2, D])
        part = sb("part", [P, J, D])
        x_now = sb("x_now", [P, J, D])
        x_nowT = Split(sb, "x_nowT", [P, J, DC, P])
        c = sb("c", [P, J, D])
        cT = Split(sb, "cT", [P, J, DC, P])
        r_peak = sb("r_peak", [P, J])
        r_prob = sb("r_prob", [P, J, E1])
        r_sum = sb("r_sum", [P, J])
        top = sb("top", [P, J, K1])
        top_at = sb("top_at", [P, J, K1], U32)
        top_e = sb("top_e", [P, J, K1])
        t_sum = sb("t_sum", [P, J])
        route = sb("route", [P, J, K1])
        hot = sb("hot", [P, J, K1, E1])
        hotT = sb("hotT", [P, J, P])
        pairs = sb("pairs", [P, J, 4, PRIM1, E1])
        likeness = sb("likeness", [P, J, 4, PRIM1])
        best = sb("best", [P, J, 4])
        keep = sb("keep", [P, J, 4])
        stays = sb("stays", [P, J, 4])
        leaves = sb("leaves", [P, J, 4])
        first = sb("first", [P, J, 4, PRIM1])
        first_of = sb("first_of", [P, J, 4])
        more_w = sb("more_w", [P, J, PRIM1])
        spread_w = sb("spread_w", [P, J, K1, E1])
        comb = sb("comb", [P, 2 * J, E1])
        combT = sb("combT", [J * E1, P])

        x_loaded = sig("x_loaded")
        small_loaded = sig("small_loaded")
        sim_cleared = sig("sim_cleared")
        sim_loaded = sig("sim_loaded")
        sim_ready = sig("sim_ready")
        w_loaded = [sem(f"w_loaded{n}") for n in range(2)]
        w_high = sig("w_high")
        w_low = sig("w_low")
        got_pair = [sem(f"got_pair{n}") for n in range(PAIRS)]
        small_ready = sig("small_ready")
        weighted, part_ready = sig("weighted"), sig("part_ready")
        x_ready = sig("x_ready", 1, 1)
        x_kept = sig("x_kept", 1, 1)
        xT_made = sig("xT_made", 1, 1)
        xT_high = sig("xT_high")
        xT_low = sig("xT_low", 1, 1)
        is_id_ready = sig("is_id_ready")
        c_made = sig("c_made", J, 2)
        c_ready = sig("c_ready", J, 2)
        cT_made = sig("cT_made", 1, 1)
        cT_high = sig("cT_high")
        cT_low = sig("cT_low", 1, 1)
        cT_kept = sig("cT_kept", 1, 1)
        logits_made = sig("logits_made", 1, 1)
        r_shifted = sig("r_shifted")
        r_exp = sig("r_exp")
        hot_ready = sig("hot_ready")
        hotT_made = sig("hotT_made")
        hotT_ready = sig("hotT_ready")
        sim_made = sig("sim_made")
        sim_read = sig("sim_read", 1, 1)
        comb_ready = sig("comb_ready")
        combT_made = sig("combT_made")
        combT_ready = sig("combT_ready", 1, 1)
        combT_stored = sig("combT_stored", 2 * 16, 16)
        steps = sig("steps")
        dve_passed, sp_passed = sig("dve_passed"), sig("sp_passed")
        block = ctx.enter_context(nc.Block())
        ident, count = const(consts, "ident"), const(consts, "count")
        banks = [psum[:, n, :] for n in range(8)]
        b_xT, b_cT, b_g, b_sim, b_hotT, b_combT = banks[4], banks[5], banks[6], banks[6][:, P:3 * P], banks[7], banks[7]

        def skewed(engine, step):
            step(-1, True, False, False)
            step(0, True, True, False)
            with engine.Fori(1, PAIRS - 1) as i:
                step(i, True, True, True)
            step(PAIRS - 1, False, True, True)
            step(PAIRS, False, False, True)

        @block.sync
        def _(sp):
            sp.sem_inc(combT_stored.sem, 16)
            sp.dma_start(x[:], io["x"].rearrange("(n p) d -> p n d", p=P)).then_inc(x_loaded.sem, 16)
            sp.dma_start(ids[:], io["itok_B_0_15"].partition_broadcast(W1TAB)).then_inc(small_loaded.sem, 16)
            sp.dma_start(bias_raw[:], io["L1_cond_b"]).then_inc(small_loaded.sem, 16)
            sp.dma_start(gate_raw[:], io["gate1"].rearrange("(c p) e -> p c e", p=P)).then_inc(small_loaded.sem, 16)
            sp.wait_ge(sim_cleared.sem, sim_cleared.at(0, 1))
            for n in range(4):
                sp.dma_start(sim[n * E1:(n + 1) * E1, n, :], io["L1_ffn_similarity"]).then_inc(sim_loaded.sem, 16)
            for n in range(PIECES):
                if n >= 2:
                    sp.wait_ge(w_low.sem, w_low.at(0, n - 1))
                sp.dma_start(w_raw[:, n % 2], io["L1_cond_W"][n * PIECE:(n + 1) * PIECE].rearrange("w (c p) e -> p w c e", p=P))\
                    .then_inc(w_loaded[n % 2], 16)

            load_next(sp)

            def one(i, ahead, front, back):
                if back:
                    sp.wait_ge(combT_ready.sem, combT_ready.at(i, 0))
                    sp.sem_inc(sp_passed.sem, 1)
                    for j in range(J):
                        at = (i - 1) * (J * P) + j * P
                        sp.dma_start(combineT[:, bass.ds(at, P)], combT[j * E1:(j + 1) * E1, :]).then_inc(combT_stored.sem, 16)

            skewed(sp, one)
            sp.wait_ge(combT_stored.sem, combT_stored.at(PAIRS, 0))

        @block.gpsimd
        def _(pool):
            pool.memset(sim[:], 0.0).then_inc(sim_cleared.sem, 1)

            pool.sem_inc(x_ready.sem, x_ready.free)

            def combine(m):
                pool.wait_ge(got_pair[m], 4 * 16)
                now = slice(m * J, (m + 1) * J)
                pool.tensor_tensor(got[:, now], got[:, now], spread(weights_eff[:, now, :], 3, D), ALU.mult).then_inc(weighted.sem, 1)
                pool.wait_ge(weighted.sem, weighted.at(m, 1))
                pool.wait_ge(x_ready.sem, x_ready.at(m, 0))
                pool.tensor_tensor(part[:], got[:, now, 0, :], got[:, now, 1, :], ALU.add).then_inc(part_ready.sem, 1)
                pool.wait_ge(part_ready.sem, part_ready.at(m, 1))
                pool.wait_ge(xT_made.sem, xT_made.at(m, 0))
                pool.wait_ge(x_kept.sem, x_kept.at(m, 0))
                pool.tensor_tensor(x_now[:], x[:, now, :], part[:], ALU.add).then_inc(x_ready.sem, 1)

            for m in range(PAIRS):
                for n in (2 * m, 2 * m + 1):
                    for k in range(2):
                        pool.indirect_dma_start(got[:, n, k, :], None, rows_out,
                                                bass.IndirectOffsetOnAxis(ap=slots[:, n, k:k + 1], axis=0)).then_inc(got_pair[m], 16)
                if m == 0:
                    pool.wait_ge(sim_loaded.sem, sim_loaded.at(0, 64))
                    flat = sim[:].rearrange("p k e -> p (k e)")
                    pool.affine_select(out=flat, in_=flat, compare_op=ALU.not_equal, fill=1.0, base=0,
                                       pattern=[[-1, P]], channel_multiplier=1).then_inc(sim_ready.sem, 1)
                    pool.wait_ge(x_loaded.sem, x_loaded.at(0, 16))
                if m >= 2:
                    combine(m - 2)
            combine(PAIRS - 2)
            combine(PAIRS - 1)

        @block.scalar
        def _(act):
            for made in (x_kept, c_ready, cT_kept, combT_ready):
                made.grant(act)
            act.wait_ge(small_loaded.sem, small_loaded.at(0, 48))
            act.activation(bias.high[:], bias_raw[:], ACT.Copy).then_inc(small_ready.sem, 1)
            act.activation(gate.high[:], gate_raw[:], ACT.Copy).then_inc(small_ready.sem, 1)
            for n in range(PIECES):
                act.wait_ge(w_loaded[n % 2], 16 * (n // 2 + 1))
                act.activation(w.high[:, n * PIECE:(n + 1) * PIECE], w_raw[:, n % 2], ACT.Copy).then_inc(w_high.sem, 1)

            def one(i, ahead, front, back):
                if back:
                    act.wait_ge(r_shifted.sem, r_shifted.at(i - 1, 1))
                    act.activation(r_prob[:], r_prob[:], ACT.Exp).then_inc(r_exp.sem, 1)

                def take(j):
                    act.wait_ge(c_made.sem, c_made.at(i, j + 1))
                    act.wait_ge(cT_made.sem, cT_made.at(i, 0))
                    for b in range(TSEQ):
                        quad = slice(b * SEQ, (b + 1) * SEQ)
                        last = act.activation(c[quad, j, :], banks[2 * j + b // 2][quad, (b % 2) * D:(b % 2 + 1) * D], ACT.Copy)
                    last.then_inc(c_ready.sem, 1)

                if back:
                    act.wait_ge(hotT_made.sem, hotT_made.at(i - 1, 1))
                    act.activation(hotT[:].rearrange("p j t -> p (j t)"), b_hotT[:, 0:J * P], ACT.Copy).then_inc(hotT_ready.sem, 1)
                if front:
                    take(0)
                    take(1)
                if ahead:
                    act.wait_ge(xT_made.sem, xT_made.at(i + 1, 1))
                    act.activation(x_nowT.high[:].rearrange("p j c t -> p (j c t)"), b_xT, ACT.Copy).then_inc(xT_high.sem, 1)
                    act.activation(x[:, bass.ds((i + 1) * J, J), :], x_now[:], ACT.Copy).then_inc(x_kept.sem, 1)
                if front:
                    act.wait_ge(cT_made.sem, cT_made.at(i, 1))
                    act.wait_ge(logits_made.sem, logits_made.at(i, 0))
                    act.wait_ge(cT_kept.sem, cT_kept.at(i, 0))
                    act.activation(cT.high[:].rearrange("p j c t -> p (j c t)"), b_cT, ACT.Copy).then_inc(cT_high.sem, 1)
                if back:
                    act.wait_ge(combT_made.sem, combT_made.at(i - 1, 1))
                    act.wait_ge(combT_stored.sem, combT_stored.at(i - 1, 0))
                    act.activation(combT[:], b_combT[0:J * E1, 0:P], ACT.Copy).then_inc(combT_ready.sem, 1)
                if front:
                    act.wait_ge(cT_low.sem, cT_low.at(i, 1))
                    for half in ("high", "low"):
                        src = (cT.high, cT.low)[half == "low"]
                        dst = (xT.high, xT.low)[half == "low"]
                        last = act.activation(dst[:, :, bass.ds(i * J * P, J * P)].rearrange("p c (j t) -> p j c t", j=J).bitcast(F32R),
                                              src[:].bitcast(F32), ACT.Copy)
                    last.then_inc(cT_kept.sem, 1)

            skewed(act, one)

        @block.vector
        def _(dve):
            chain = Chain(dve, steps.sem, 25)
            sim_read.grant(dve)
            cT_low.grant(dve)
            xT_low.grant(dve)
            dve.memset(comb[:], 0.0).then_inc(small_ready.sem, 1)
            dve.wait_ge(small_ready.sem, small_ready.at(0, 3))
            dve.tensor_tensor(bias.low[:], bias_raw[:], bias.high_read, ALU.subtract).then_inc(small_ready.sem, 1)
            dve.tensor_tensor(gate.low[:], gate_raw[:], gate.high_read, ALU.subtract).then_inc(small_ready.sem, 1)
            dve.tensor_copy(ids_f[:], ids[:]).then_inc(small_ready.sem, 1)
            for n in range(PIECES):
                dve.wait_ge(w_high.sem, w_high.at(0, n + 1))
                dve.tensor_tensor(w.low[:, n * PIECE:(n + 1) * PIECE], w_raw[:, n % 2],
                                  w.high[:, n * PIECE:(n + 1) * PIECE].bitcast(F32), ALU.subtract).then_inc(w_low.sem, 1)
            dve.wait_ge(small_ready.sem, small_ready.at(0, 6))

            def select(i):
                dve.wait_ge(c_made.sem, c_made.at(i, 0))
                dve.tensor_scalar(is_id[:], spread(ids_f[:, bass.ds(i * J * TSEQ, J * TSEQ)].rearrange("p (j b) -> p j b", j=J), 3, SEQ),
                                  consts[0:W1TAB, CONST["position"][0]:CONST["position"][1]], None, ALU.is_equal).then_inc(is_id_ready.sem, 1)

            def low(dst, bank):
                return dve.tensor_tensor(dst.low[:].rearrange("p j c t -> p (j c t)"), bank,
                                         dst.high[:].rearrange("p j c t -> p (j c t)").bitcast(F32), ALU.subtract)

            def choose(i):
                logits = b_g[:, 0:J * E1].rearrange("p (j e) -> p j e", e=E1)
                chain.start(i)
                dve.wait_ge(logits_made.sem, logits_made.at(i, 1))
                dve.tensor_reduce(r_peak[:], logits, AX, ALU.max).then_inc(chain.next(), 1)
                dve.wait_ge(chain.sem, chain.count())
                dve.tensor_tensor(r_prob[:], logits, spread(r_peak[:], 2, E1), ALU.subtract).then_inc(r_shifted.sem, 1)
                dve.wait_ge(r_exp.sem, r_exp.at(i, 1))
                dve.tensor_reduce(r_sum[:], r_prob[:], AX, ALU.add).then_inc(chain.next(), 1)
                dve.wait_ge(chain.sem, chain.count())
                dve.reciprocal(r_sum[:], r_sum[:]).then_inc(chain.next(), 1)
                dve.wait_ge(chain.sem, chain.count())
                dve.tensor_tensor(r_prob[:], r_prob[:], spread(r_sum[:], 2, E1), ALU.mult).then_inc(chain.next(), 1)
                dve.wait_ge(chain.sem, chain.count())
                dve.sem_inc(dve_passed.sem, 1)
                for j in range(J):
                    last = dve.max(top[:, j, :], r_prob[:, j, :])
                last.then_inc(chain.next(), 1)
                dve.wait_ge(chain.sem, chain.count())
                dve.sem_inc(dve_passed.sem, 1)
                for j in range(J):
                    last = dve.max_index(top_at[:, j, :], top[:, j, :], r_prob[:, j, :])
                last.then_inc(chain.next(), 1)
                dve.wait_ge(chain.sem, chain.count())
                dve.tensor_copy(top_e[:], top_at[:]).then_inc(chain.next(), 1)
                dve.tensor_reduce(t_sum[:], top[:], AX, ALU.add).then_inc(chain.next(), 1)
                dve.wait_ge(chain.sem, chain.count())
                dve.tensor_scalar(t_sum[:], t_sum[:], 1e-12, None, ALU.max).then_inc(chain.next(), 1)
                dve.tensor_tensor(hot[:].rearrange("p j k e -> p (j k) e"), spread(count, 1, J * K1),
                                  spread(top_e[:].rearrange("p j k -> p (j k)"), 2, E1), ALU.is_equal).then_inc(hot_ready.sem, 1)
                dve.wait_ge(chain.sem, chain.count())
                dve.reciprocal(t_sum[:], t_sum[:]).then_inc(chain.next(), 1)
                dve.wait_ge(chain.sem, chain.count())
                dve.tensor_tensor(route[:], top[:], spread(t_sum[:], 2, K1), ALU.mult).then_inc(chain.next(), 1)

            def likenesses(i):
                dve.wait_ge(sim_made.sem, sim_made.at(i, 1))
                dve.wait_ge(hot_ready.sem, hot_ready.at(i, 1))
                for j in range(J):
                    last = dve.tensor_tensor(pairs[:, j], spread(b_sim[:, j * P:(j + 1) * P].rearrange("p (k e) -> p k e", e=E1), 2, PRIM1),
                                             spread(hot[:, j, 0:PRIM1, :], 1, 4), ALU.mult)
                last.then_inc(sim_read.sem, 1)
                dve.wait_ge(sim_read.sem, sim_read.at(i, 1))
                dve.tensor_reduce(likeness[:].rearrange("p j s m -> p (j s m)"),
                                            pairs[:].rearrange("p j s m e -> p (j s m) e"), AX, ALU.add).then_inc(chain.next(), 1)

            def reroute(i):
                dve.wait_ge(chain.sem, chain.count())
                dve.tensor_reduce(best[:], likeness[:], AX, ALU.max).then_inc(chain.next(), 1)
                dve.wait_ge(chain.sem, chain.count())
                dve.tensor_scalar(keep[:], best[:], 0.5, None, ALU.is_lt).then_inc(chain.next(), 1)
                dve.tensor_tensor(first[:].rearrange("p j s m -> p (j s) m"), likeness[:].rearrange("p j s m -> p (j s) m"),
                                            spread(best[:].rearrange("p j s -> p (j s)"), 2, PRIM1), ALU.is_equal).then_inc(chain.next(), 1)
                dve.wait_ge(chain.sem, chain.count())
                dve.scalar_tensor_tensor(first[:].rearrange("p j s m -> p (j s) m"),
                                                   spread(count[:, 0:PRIM1], 1, J * 4), -8.0,
                                                   first[:].rearrange("p j s m -> p (j s) m"), ALU.add, ALU.mult).then_inc(chain.next(), 1)
                dve.tensor_tensor(stays[:], route[:, :, PRIM1:K1], keep[:], ALU.mult).then_inc(chain.next(), 1)
                dve.wait_ge(chain.sem, chain.count())
                dve.tensor_reduce(first_of[:], first[:], AX, ALU.min).then_inc(chain.next(), 1)
                dve.wait_ge(chain.sem, chain.count())
                dve.tensor_tensor(first[:].rearrange("p j s m -> p (j s) m"), first[:].rearrange("p j s m -> p (j s) m"),
                                            spread(first_of[:].rearrange("p j s -> p (j s)"), 2, PRIM1), ALU.is_equal).then_inc(chain.next(), 1)
                dve.tensor_tensor(leaves[:], route[:, :, PRIM1:K1], stays[:], ALU.subtract).then_inc(chain.next(), 1)
                dve.wait_ge(chain.sem, chain.count())
                dve.tensor_copy(route[:, :, PRIM1:K1], stays[:]).then_inc(chain.next(), 1)
                dve.tensor_tensor(first[:].rearrange("p j s m -> p (j s) m"), first[:].rearrange("p j s m -> p (j s) m"),
                                            spread(leaves[:].rearrange("p j s -> p (j s)"), 2, PRIM1), ALU.mult).then_inc(chain.next(), 1)
                dve.wait_ge(chain.sem, chain.count())
                dve.tensor_reduce(more_w[:], first[:].rearrange("p j s m -> p j m s"), AX, ALU.add).then_inc(chain.next(), 1)
                dve.wait_ge(chain.sem, chain.count())
                dve.tensor_tensor(route[:, :, 0:PRIM1], route[:, :, 0:PRIM1], more_w[:], ALU.add).then_inc(chain.next(), 1)
                dve.wait_ge(chain.sem, chain.count())
                dve.tensor_tensor(spread_w[:].rearrange("p j k e -> p (j k) e"), hot[:].rearrange("p j k e -> p (j k) e"),
                                            spread(route[:].rearrange("p j k -> p (j k)"), 2, E1), ALU.mult).then_inc(chain.next(), 1)
                dve.wait_ge(chain.sem, chain.count())
                dve.tensor_reduce(comb[:, 0:J, :], spread_w[:].rearrange("p j k e -> p j e k"), AX, ALU.add).then_inc(comb_ready.sem, 1)
                dve.wait_ge(comb_ready.sem, comb_ready.at(i, 1))
                chain.end()

            def one(i, ahead, front, back):
                if back:
                    choose(i - 1)
                    likenesses(i - 1)
                    reroute(i - 1)
                if ahead:
                    dve.wait_ge(xT_high.sem, xT_high.at(i + 1, 1))
                    low(x_nowT, b_xT).then_inc(xT_low.sem, 1)
                    select(i + 1)
                if front:
                    dve.wait_ge(cT_high.sem, cT_high.at(i, 1))
                    low(cT, b_cT).then_inc(cT_low.sem, 1)

            skewed(dve, one)

        @block.tensor
        def _(pe):
            for made in (xT_made, c_made, cT_made, logits_made):
                made.grant(pe)
            pe.wait_ge(small_ready.sem, small_ready.at(0, 6))
            pe.wait_ge(w_low.sem, w_low.at(0, PIECES))
            pe.wait_ge(sim_ready.sem, sim_ready.at(0, 1))

            def turn_x(i):
                pe.wait_ge(x_ready.sem, x_ready.at(i, 1))
                pe.wait_ge(xT_low.sem, xT_low.at(i, 0))
                for j in range(J):
                    for k in range(DC):
                        last = pe.transpose(b_xT[:, (j * DC + k) * P:(j * DC + k + 1) * P], x_now[:, j, k * P:(k + 1) * P], ident)
                last.then_inc(xT_made.sem, 1)

            def layer(i, j):
                pe.wait_ge(xT_low.sem, xT_low.at(i, 1))
                pe.wait_ge(is_id_ready.sem, is_id_ready.at(i, 1))
                pe.wait_ge(c_ready.sem, c_ready.at(i, j - 1))
                for pair in range(2):
                    out = banks[2 * j + pair]
                    which = is_id[:, j].rearrange("p b t -> p (b t)")
                    for n, half in enumerate((bias.high, bias.low)):
                        pe.matmul(out, which, spread(half[:], 1, 2), start=(n == 0), stop=False, skip_group_check=True)
                    for b in (2 * pair, 2 * pair + 1):
                        own = pe.value_load(ids[0:1, bass.ds(i * J * TSEQ + j * TSEQ + b, 1)], min_val=0, max_val=W1TAB - 1)
                        last = product(pe, out[:, (b % 2) * D:(b % 2 + 1) * D], x_nowT, w, range(DC), lambda a, k: a[:, j, k, :],
                                       lambda a, k: a[:, bass.ds(own, 1), k, :].rearrange("p o e -> p (o e)"), start=False)
                last.then_inc(c_made.sem, 1)

            def one(i, ahead, front, back):
                if front:
                    layer(i, 0)
                if back:
                    pe.wait_ge(hot_ready.sem, hot_ready.at(i - 1, 1))
                    pe.wait_ge(combT_ready.sem, combT_ready.at(i - 1, 0))
                    for j in range(J):
                        last = pe.transpose(b_hotT[:, j * P:(j + 1) * P], hot[:, j, PRIM1:K1, :].rearrange("p k e -> p (k e)"), ident)
                    last.then_inc(hotT_made.sem, 1)
                if ahead:
                    turn_x(i + 1)
                if back:
                    pe.wait_ge(hotT_ready.sem, hotT_ready.at(i - 1, 1))
                    for j in range(J):
                        last = pe.matmul(b_sim[:, j * P:(j + 1) * P], hotT[:, j, :], sim[:].rearrange("p k e -> p (k e)"),
                                         start=True, stop=True, skip_group_check=True)
                    last.then_inc(sim_made.sem, 1)
                if front:
                    layer(i, 1)
                if front:
                    pe.wait_ge(c_ready.sem, c_ready.at(i, J))
                    pe.wait_ge(cT_low.sem, cT_low.at(i, 0))
                    for j in range(J):
                        for k in range(DC):
                            last = pe.transpose(b_cT[:, (j * DC + k) * P:(j * DC + k + 1) * P], c[:, j, k * P:(k + 1) * P], ident)
                    last.then_inc(cT_made.sem, 1)
                if back:
                    pe.wait_ge(comb_ready.sem, comb_ready.at(i - 1, 1))
                    pe.transpose(b_combT[:, 0:P], comb[:].rearrange("p j e -> p (j e)"), ident).then_inc(combT_made.sem, 1)
                if front:
                    pe.wait_ge(cT_low.sem, cT_low.at(i, 1))
                    pe.wait_ge(sim_read.sem, sim_read.at(i, 0))
                    for j in range(J):
                        last = product(pe, b_g[:, j * E1:(j + 1) * E1], cT, gate, range(DC), lambda a, k: a[:, j, k, :],
                                       lambda a, k: a[:, k, :])
                    last.then_inc(logits_made.sem, 1)

            skewed(pe, one)


class ExpertWeights:

    def __init__(self, sb, sems, name, gate_w, up_w, down_w, chunks):
        self.gate_w, self.up_w, self.down_w, self.chunks = gate_w, up_w, down_w, chunks
        self.gu = sb(name + "_gu_raw", [P, chunks, 2, DC, P])
        self.down = sb(name + "_down_raw", [P, chunks, D])
        self.gu_loaded = [Signal(sems.new(f"{name}_gu_loaded{c}"), 32) for c in range(chunks)]
        self.down_loaded = Signal(sems.new(name + "_down_loaded"), 16)

    def load_gate_up(self, sp, g, c):
        for n, w in enumerate((self.gate_w, self.up_w)):
            src = w[:, bass.ds((g * self.chunks + c) * P, P)].rearrange("(k p) f -> p k f", p=P)
            sp.dma_start(self.gu[:, c, n], src).then_inc(self.gu_loaded[c].sem, 16)

    def load_down(self, sp, g):
        src = self.down_w[bass.ds(g * (self.chunks * P), self.chunks * P), :].rearrange("(c p) d -> p c d", p=P)
        sp.dma_start(self.down[:], src).then_inc(self.down_loaded.sem, 16)

    def load(self, sp):
        for c in range(self.chunks):
            self.load_gate_up(sp, 0, c)
        self.load_down(sp, 0)


def gated_experts_phase(nc, sems, name, psum, raws, combineT, width, experts, x, xT, load_next=None):
    chunks, gu_loaded, down_loaded = raws.chunks, raws.gu_loaded, raws.down_loaded
    gu_raw, down_raw = raws.gu, raws.down
    group = chunks * P // width
    GROUPS = experts // group
    STEPS = BLOCKS * chunks
    with ExitStack() as ctx:
        def sb(n, shape, dt=F32):
            return ctx.enter_context(nc.sbuf_tensor(f"{name}_{n}", shape, dt))

        def sig(n, per=1, free=0):
            return Signal(sems.new(f"{name}_{n}"), per, free)

        gu, down = Split(sb, "gu", [P, chunks, 2, DC, P]), Split(sb, "down", [P, chunks, D])
        weight = sb("weight", [P, chunks, T])
        silu = sb("silu", [P, 2, BLOCK])
        prod = sb("prod", [P, 2, BLOCK])
        hw = sb("hw", [P, 2, BLOCK])
        h = Split(sb, "h", [P, 2, chunks, BLOCK])

        weight_loaded = [sig(f"weight_loaded{c}", 16 * len(pieces(c, width))) for c in range(chunks)]
        gu_high, gu_low = sig("gu_high", chunks), sig("gu_low", chunks)
        down_high, down_low = sig("down_high"), sig("down_low")
        gu_made = sig("gu_made", STEPS)
        silu_ready = sig("silu_ready", STEPS)
        prod_ready = sig("prod_ready", STEPS, 2)
        hw_ready = sig("hw_ready", STEPS, 2)
        h_high = sig("h_high", STEPS)
        h_low = sig("h_low", STEPS, 2)
        y_made = sig("y_made", BLOCKS, 2)
        y_added = sig("y_added", BLOCKS, 2)
        sp_passed = sig("sp_passed")
        block = ctx.enter_context(nc.Block())
        banks = [psum[:, n, :] for n in range(8)]

        def groups(engine, one):
            with engine.Fori(0, GROUPS - 1) as g:
                one(g, True)
            one(GROUPS - 1, False)

        @block.sync
        def _(sp):
            def load_weight(g, c):
                for a, b, e in pieces(c, width):
                    src = combineT[bass.ds(g * group + e, 1), :].rearrange("o t -> (o t)").partition_broadcast(b - a)
                    sp.dma_start(weight[a:b, c, :], src).then_inc(weight_loaded[c].sem, 16)

            for c in range(chunks):
                load_weight(0, c)
            if load_next:
                load_next(sp)

            def one(g, more):
                if more:
                    for c in range(chunks):
                        sp.wait_ge(gu_low.sem, gu_low.at(g, c + 1))
                        sp.sem_inc(sp_passed.sem, 1)
                        raws.load_gate_up(sp, g + 1, c)
                    sp.wait_ge(down_low.sem, down_low.at(g, 1))
                    sp.sem_inc(sp_passed.sem, 1)
                    raws.load_down(sp, g + 1)
                    for c in range(chunks):
                        sp.wait_ge(hw_ready.sem, hw_ready.at(g, STEPS - chunks + c + 1))
                        sp.sem_inc(sp_passed.sem, 1)
                        load_weight(g + 1, c)

            groups(sp, one)

        @block.gpsimd
        def _(pool):
            hw_ready.grant(pool)

            def one(g, more):
                for m in range(STEPS):
                    b, c = divmod(m, chunks)
                    if b == 0:
                        pool.wait_ge(weight_loaded[c].sem, weight_loaded[c].at(g, weight_loaded[c].per))
                    pool.wait_ge(prod_ready.sem, prod_ready.at(g, m + 1))
                    pool.wait_ge(h_low.sem, h_low.at(g, m - 1))
                    pool.tensor_tensor(hw[:, m % 2], prod[:, m % 2], weight[:, c, b * BLOCK:(b + 1) * BLOCK],
                                       ALU.mult).then_inc(hw_ready.sem, 1)

            groups(pool, one)

        @block.scalar
        def _(act):
            def split_gu(g, c):
                act.wait_ge(gu_loaded[c].sem, gu_loaded[c].at(g, 32))
                act.activation(gu.high[:, c], gu_raw[:, c], ACT.Copy).then_inc(gu_high.sem, 1)

            for c in range(chunks):
                split_gu(0, c)

            def one(g, more):
                for m in range(STEPS):
                    b, c = divmod(m, chunks)
                    act.wait_ge(gu_made.sem, gu_made.at(g, m + 1))
                    act.wait_ge(prod_ready.sem, prod_ready.at(g, m - 1))
                    act.activation(silu[:, m % 2], banks[m % 2], ACT.Silu).then_inc(silu_ready.sem, 1)
                    if m == 0:
                        act.wait_ge(down_loaded.sem, down_loaded.at(g, 16))
                        act.wait_ge(y_made.sem, y_made.at(g, 0))
                        act.activation(down.high[:], down_raw[:], ACT.Copy).then_inc(down_high.sem, 1)
                    if more and b == BLOCKS - 1:
                        split_gu(g + 1, c)
                    act.wait_ge(hw_ready.sem, hw_ready.at(g, m + 1))
                    act.wait_ge(y_made.sem, y_made.at(g, b - 1))
                    act.activation(h.high[:, b % 2, c], hw[:, m % 2], ACT.Copy).then_inc(h_high.sem, 1)

            groups(act, one)

        @block.vector
        def _(dve):
            for made in (prod_ready, h_low, y_added):
                made.grant(dve)

            def split_gu(g, c):
                dve.wait_ge(gu_high.sem, gu_high.at(g, c + 1))
                dve.tensor_tensor(gu.low[:, c], gu_raw[:, c], gu.high[:, c].bitcast(F32), ALU.subtract).then_inc(gu_low.sem, 1)

            for c in range(chunks):
                split_gu(0, c)

            def add(g, b):
                dve.wait_ge(y_made.sem, y_made.at(g, b + 1))
                dve.wait_ge(y_added.sem, y_added.at(g, b))
                for half in range(2):
                    out = x[:, b * BTILES + 2 * half:b * BTILES + 2 * half + 2, :].rearrange("p n d -> p (n d)")
                    last = dve.tensor_tensor(out, banks[4 + 2 * (b % 2) + half], out, ALU.add)
                last.then_inc(y_added.sem, 1)

            def one(g, more):
                for m in range(STEPS):
                    b, c = divmod(m, chunks)
                    dve.wait_ge(silu_ready.sem, silu_ready.at(g, m + 1))
                    dve.wait_ge(hw_ready.sem, hw_ready.at(g, m - 1))
                    dve.tensor_tensor(prod[:, m % 2], banks[2 + m % 2], silu[:, m % 2], ALU.mult).then_inc(prod_ready.sem, 1)
                    if m == 0:
                        dve.wait_ge(down_high.sem, down_high.at(g, 1))
                        dve.tensor_tensor(down.low[:], down_raw[:], down.high_read, ALU.subtract).then_inc(down_low.sem, 1)
                    if more and b == BLOCKS - 1:
                        split_gu(g + 1, c)
                    dve.wait_ge(h_high.sem, h_high.at(g, m + 1))
                    dve.tensor_tensor(h.low[:, b % 2, c], hw[:, m % 2], h.high[:, b % 2, c].bitcast(F32),
                                      ALU.subtract).then_inc(h_low.sem, 1)
                    if c == chunks - 1 and b > 0:
                        add(g, b - 1)
                add(g, BLOCKS - 1)

            groups(dve, one)

        @block.tensor
        def _(pe):
            y_made.grant(pe)

            def hidden(g, b, c):
                m = b * chunks + c
                if b == 0:
                    pe.wait_ge(gu_low.sem, gu_low.at(g, c + 1))
                pe.wait_ge(prod_ready.sem, prod_ready.at(g, m - 1))
                for n in range(2):
                    last = product(pe, banks[2 * n + m % 2], gu, xT, range(DC), lambda a, k: a[:, c, n, k, :],
                                   lambda a, k: a[:, k, b * BLOCK:(b + 1) * BLOCK])
                last.then_inc(gu_made.sem, 1)

            def result(g, b):
                if b == 0:
                    pe.wait_ge(down_low.sem, down_low.at(g, 1))
                pe.wait_ge(y_added.sem, y_added.at(g, b - 1))
                for c in range(chunks):
                    pe.wait_ge(h_low.sem, h_low.at(g, b * chunks + c + 1))
                    for r in range(BTILES):
                        last = product(pe, banks[4 + 2 * (b % 2) + r // 2][:, (r % 2) * D:(r % 2 + 1) * D], h, down, [c],
                                       lambda a, k: a[:, b % 2, k, r * P:(r + 1) * P], lambda a, k: a[:, k, :],
                                       start=(c == 0 and r % 2 == 0), stop=(c == chunks - 1))
                last.then_inc(y_made.sem, 1)

            def one(g, more):
                for b in range(BLOCKS):
                    for c in range(chunks):
                        if b > 0 and c == chunks - 1:
                            result(g, b - 1)
                        hidden(g, b, c)
                result(g, BLOCKS - 1)

            groups(pe, one)


def pieces(c, width):
    out, at = [], c * P
    while at < (c + 1) * P:
        e = at // width
        end = min((e + 1) * width, (c + 1) * P)
        out.append((at - c * P, end - c * P, e))
        at = end
    return out


class QuantisedInputs:

    def __init__(self, sb, sems, io):
        self.io = io
        self.cond, self.down, self.up = sb("q_cond_raw", [P, DC, D]), sb("q_down_raw", [P, DC, P]), sb("q_up_raw", [P, 1, D])
        self.ids, self.scaling = sb("q_ids", [P, SEQS], I32), sb("q_scaling", [P, 1])
        self.g1, self.g2 = sb("q_g1", [P, D]), sb("q_g2", [P, F2])
        self.w1, self.w2 = sb("q_w1_raw", [P, DC, F2]), sb("q_w2_raw", [P, F2 // P, D])
        self.loaded = Signal(sems.new("q_loaded"))
        self.all_loaded = 16 * (8 + A2)

    def load(self, sp):
        def load(dst, src):
            sp.dma_start(dst, src).then_inc(self.loaded.sem, 16)

        io = self.io
        load(self.cond[:], io["cond2"].rearrange("(c p) e -> p c e", p=P))
        load(self.down[:], io["adapter_down"].rearrange("(c p) r -> p c r", p=P))
        load(self.up[:, 0, :], io["adapter_up"])
        load(self.w1[:], io["quant_w1"].rearrange("(c p) f -> p c f", p=P))
        load(self.w2[:], io["quant_w2"].rearrange("(c p) d -> p c d", p=P))
        load(self.ids[:], io["itok_B_0_6"].partition_broadcast(P))
        load(self.g1[:], io["L2_ffn_g1"].partition_broadcast(P))
        load(self.g2[:], io["L2_ffn_g2"].partition_broadcast(P))
        for a in range(A2):
            load(self.scaling[a * R2:(a + 1) * R2, :], io["L2_cond_scalings"][a:a + 1].partition_broadcast(R2))


def quantised_phase(nc, sems, psum, consts, raws, x):
    FC, J = F2 // P, BTILES
    with ExitStack() as ctx:
        def sb(name, shape, dt=F32):
            return ctx.enter_context(nc.sbuf_tensor("q_" + name, shape, dt))

        def sig(name, per=1, free=0):
            return Signal(sems.new("q_" + name), per, free)

        loaded, g1, g2, w1_raw, w2_raw = raws.loaded, raws.g1, raws.g2, raws.w1, raws.w2
        cond = Split(sb, "cond", [P, DC, D])
        down = Split(sb, "down", [P, DC, P])
        up = Split(sb, "up", [P, 1, D])
        ids_f = sb("ids_f", [P, SEQS])
        own = sb("own", [P, SEQS])
        w1_q = sb("w1_q", [P, DC, F2], BF16)
        w2_q = sb("w2_q", [P, FC, D], BF16)
        w_abs = sb("w_abs", [P, 2])
        w_mean = sb("w_mean", [P, 2])
        w_scale = sb("w_scale", [P, 2])
        magic = sb("magic", [P, 1])
        magic_off = sb("magic_off", [P, 1])
        eps = sb("eps", [P, 1])
        x_now = sb("x_now", [P, J, D])
        x_T = Split(sb, "x_T", [P, J, DC, P])
        low_rank = sb("low_rank", [P, BLOCK])
        lr = Split(sb, "lr", [P, 1, BLOCK])
        c = sb("c", [P, J, D])
        v = sb("v", [P, J, D])
        q1 = sb("q1", [P, J, DC, P], BF16)
        square = sb("square", [P, 2, F2])
        square1 = sb("square1", [P, J, D])
        r = sb("r", [P, 2, F2])
        r2 = sb("r2", [P, 2, F2])
        v2 = sb("v2", [P, J, F2])
        t2 = sb("t2", [P, 2, F2])
        q2 = sb("q2", [P, 2, FC, P], BF16)
        sums, rms, inv, peak, to_q, back = (sb(n, [P, 2, J]) for n in ("sums", "rms", "inv", "peak", "to_q", "back"))

        constants_set = sig("constants_set")
        split_high, split_low = sig("split_high"), sig("split_low")
        own_ready = sig("own_ready")
        abs_ready = sig("abs_ready")
        w_scale_ready = sig("w_scale_ready")
        w_scaled, w_clipped, w_ready = sig("w_scaled"), sig("w_clipped"), sig("w_ready")
        abs_summed = sig("abs_summed")
        x_copied = sig("x_copied")
        xT_made = sig("xT_made", 2, 1)
        xT_high = sig("xT_high", 2)
        xT_low = sig("xT_low", 2)
        lr_made = sig("lr_made")
        lr_masked = sig("lr_masked")
        lr_high = sig("lr_high")
        lr_low = sig("lr_low")
        c_made = sig("c_made", 2, 1)
        c_copied = sig("c_copied", 2)
        v_ready = sig("v_ready", 2)
        rms_ready = sig("rms_ready", 2)
        sqrt1, sqrt2 = sig("sqrt1"), sig("sqrt2")
        back1_ready, back2_ready = sig("back1_ready"), sig("back2_ready")
        t_ready = sig("t_ready")
        t_made = sig("t_made", 2)
        q1_ready = sig("q1_ready", 2, 2)
        h_made = sig("h_made", J, 1)
        r_ready = sig("r_ready", J, 2)
        r2_ready = sig("r2_ready", J, 2)
        v2_ready = sig("v2_ready", J, 2)
        sums2_ready = sig("sums2_ready", J, 2)
        to_q2_ready = sig("to_q2_ready")
        t2_ready = sig("t2_ready", J, 1)
        t2_clipped = sig("t2_clipped", J)
        t2_made = sig("t2_made", J, 2)
        q2_act = sig("q2_act", J, 2)
        q2_dve = sig("q2_dve", J, 2)
        y_made = sig("y_made", J, 2)
        y_added = sig("y_added", J, J + 1)
        steps1, steps2 = sig("steps1"), sig("steps2")
        block = ctx.enter_context(nc.Block())
        ident = const(consts, "ident")
        banks = [psum[:, n, :] for n in range(8)]
        b_lr, b_c = banks[2], banks[3]
        b_abs = banks[4][:, 0:2]
        b_y = (banks[2], banks[3])

        def b_h(j):
            first = 4 + 2 * (j % 2)
            return psum[:, first:first + 2, :].rearrange("p n f -> p (n f)")

        def b_t2(j, half):
            return banks[4 + 2 * (j % 2) + half]

        def skewed(engine, step):
            step(-1, True, False)
            with engine.Fori(0, BLOCKS - 1) as i:
                step(i, True, True)
            step(BLOCKS - 1, False, True)

        @block.gpsimd
        def _(pool):
            v2_ready.grant(pool)
            pool.wait_ge(loaded.sem, loaded.at(0, raws.all_loaded))

            def step(i, ahead, now):
                if ahead:
                    pool.wait_ge(xT_made.sem, xT_made.at(i + 1, 0))
                    pool.tensor_copy(x_now[:], x[:, bass.ds((i + 1) * J, J), :]).then_inc(x_copied.sem, 1)
                if now:
                    for j in range(J):
                        pool.wait_ge(r2_ready.sem, r2_ready.at(i, j + 1))
                        pool.wait_ge(t2_ready.sem, t2_ready.at(i, 0))
                        pool.tensor_tensor(v2[:, j, :], r2[:, j % 2], g2[:], ALU.mult).then_inc(v2_ready.sem, 1)

            skewed(pool, step)

        @block.scalar
        def _(act):
            for made in (r_ready, sums2_ready, t2_ready, q2_act):
                made.grant(act)
            act.wait_ge(loaded.sem, loaded.at(0, raws.all_loaded))
            for raw, split in ((raws.cond, cond), (raws.down, down), (raws.up, up)):
                act.activation(split.high[:], raw[:], ACT.Copy).then_inc(split_high.sem, 1)
            act.wait_ge(constants_set.sem, constants_set.at(0, 3))

            def x_high(i):
                for half in range(2):
                    act.wait_ge(xT_made.sem, xT_made.at(i, half + 1))
                    act.activation(x_T.high[:, 2 * half:2 * half + 2].rearrange("p j c t -> p (j c t)"), banks[half],
                                   ACT.Copy).then_inc(xT_high.sem, 1)

            def low_rank_high(i):
                act.wait_ge(lr_masked.sem, lr_masked.at(i, 1))
                act.activation(lr.high[:, 0, :], low_rank[:], ACT.Copy).then_inc(lr_high.sem, 1)

            def dense(i, half):
                act.wait_ge(c_made.sem, c_made.at(i, half + 1))
                act.activation(c[:, 2 * half:2 * half + 2, :].rearrange("p j d -> p (j d)"), b_c, ACT.Copy).then_inc(c_copied.sem, 1)
                act.wait_ge(c_copied.sem, c_copied.at(i, half + 1))
                for j in (2 * half, 2 * half + 1):
                    last = act.activation(square1[:, j, :], c[:, j, :], ACT.Square, accum_out=sums[:, 0, j:j + 1])
                last.then_inc(rms_ready.sem, 1)

            def root(i):
                act.wait_ge(rms_ready.sem, rms_ready.at(i, 2))
                act.activation(rms[:, 0, :], sums[:, 0, :], ACT.Sqrt, bias=eps[:], scale=1.0 / D).then_inc(sqrt1.sem, 1)

            def relu(i, j):
                act.wait_ge(h_made.sem, h_made.at(i, j + 1))
                act.wait_ge(back1_ready.sem, back1_ready.at(i, 1))
                act.wait_ge(r2_ready.sem, r2_ready.at(i, j - 1))
                act.activation(r[:, j % 2], b_h(j), ACT.Relu, scale=back[:, 0, j:j + 1]).then_inc(r_ready.sem, 1)

            def sum_squares(i, j):
                act.wait_ge(r2_ready.sem, r2_ready.at(i, j + 1))
                act.activation(square[:, j % 2], r2[:, j % 2], ACT.Square, accum_out=sums[:, 1, j:j + 1]).then_inc(sums2_ready.sem, 1)

            def take(i, j):
                act.wait_ge(t2_made.sem, t2_made.at(i, j + 1))
                act.wait_ge(y_made.sem, y_made.at(i, j - 1))
                act.activation(q2[:, j % 2, 0:4, :].rearrange("p f t -> p (f t)"), b_t2(j, 0), ACT.Identity,
                               bias=magic_off[:]).then_inc(q2_act.sem, 1)

            def second(i):
                act.wait_ge(sums2_ready.sem, sums2_ready.at(i, J))
                act.activation(rms[:, 1, :], sums[:, 1, :], ACT.Sqrt, bias=eps[:], scale=1.0 / F2).then_inc(sqrt2.sem, 1)
                act.wait_ge(to_q2_ready.sem, to_q2_ready.at(i, 1))
                for j in range(J):
                    act.wait_ge(t2_made.sem, t2_made.at(i, j - 1))
                    act.activation(t2[:, j % 2], v2[:, j, :], ACT.Identity, bias=magic[:], scale=to_q[:, 1, j:j + 1])\
                        .then_inc(t2_ready.sem, 1)
                    if j > 0:
                        take(i, j - 1)
                take(i, J - 1)

            def whole_weights():
                act.wait_ge(w_scale_ready.sem, w_scale_ready.at(0, 2))
                for n, raw in enumerate((w1_raw, w2_raw)):
                    act.activation(raw[:], raw[:], ACT.Identity, bias=magic[:], scale=w_scale[:, n:n + 1]).then_inc(w_scaled.sem, 1)
                for n, (raw, whole) in enumerate(((w1_raw, w1_q), (w2_raw, w2_q))):
                    act.wait_ge(w_clipped.sem, w_clipped.at(0, n + 1))
                    act.activation(whole[:], raw[:], ACT.Identity, bias=magic_off[:]).then_inc(w_ready.sem, 1)

            def step(i, ahead, now):
                if now:
                    relu(i, 0)
                if ahead:
                    x_high(i + 1)
                if now:
                    relu(i, 1)
                    sum_squares(i, 0)
                if ahead:
                    low_rank_high(i + 1)
                if now:
                    relu(i, 2)
                if ahead:
                    dense(i + 1, 0)
                if now:
                    sum_squares(i, 1)
                    relu(i, 3)
                if ahead:
                    dense(i + 1, 1)
                    root(i + 1)
                if not now:
                    whole_weights()
                if now:
                    sum_squares(i, 2)
                    sum_squares(i, 3)
                    second(i)

            skewed(act, step)

        @block.vector
        def _(dve):
            first, second = Chain(dve, steps1.sem, 7), Chain(dve, steps2.sem, 5)
            for made in (r2_ready, q2_dve, q1_ready, y_added):
                made.grant(dve)
            dve.memset(magic[:], MAGIC).then_inc(constants_set.sem, 1)
            dve.memset(magic_off[:], -MAGIC).then_inc(constants_set.sem, 1)
            dve.memset(eps[:], 1e-6).then_inc(constants_set.sem, 1)
            dve.wait_ge(loaded.sem, loaded.at(0, raws.all_loaded))
            for n, (raw, split) in enumerate(((raws.cond, cond), (raws.down, down), (raws.up, up))):
                dve.wait_ge(split_high.sem, split_high.at(0, n + 1))
                dve.tensor_tensor(split.low[:], raw[:], split.high_read, ALU.subtract).then_inc(split_low.sem, 1)
            dve.tensor_copy(ids_f[:], raws.ids[:]).then_inc(own_ready.sem, 1)
            dve.wait_ge(own_ready.sem, own_ready.at(0, 1))
            dve.tensor_scalar(own[:], ids_f[:], const(consts, "adapter"), raws.scaling[:], ALU.is_equal, ALU.mult).then_inc(own_ready.sem, 1)
            dve.wait_ge(own_ready.sem, own_ready.at(0, 2))

            def absolute(n):
                dve.tensor_reduce(w_abs[:, n:n + 1], (w1_raw, w2_raw)[n][:].rearrange("p c f -> p (c f)"), AX, ALU.add,
                                  apply_absolute_value=True).then_inc(abs_ready.sem, 1)

            def weight_scales():
                dve.wait_ge(abs_summed.sem, abs_summed.at(0, 1))
                dve.tensor_scalar(w_mean[:], b_abs, 1.0 / (D * F2), 1e-5, ALU.mult, ALU.max).then_inc(w_scale_ready.sem, 1)
                dve.wait_ge(w_scale_ready.sem, w_scale_ready.at(0, 1))
                dve.reciprocal(w_scale[:], w_mean[:]).then_inc(w_scale_ready.sem, 1)

            def clip_weights():
                for n, raw in enumerate((w1_raw, w2_raw)):
                    dve.wait_ge(w_scaled.sem, w_scaled.at(0, n + 1))
                    dve.tensor_scalar(raw[:], raw[:], MAGIC + 1, MAGIC - 1, ALU.min, ALU.max).then_inc(w_clipped.sem, 1)

            def scales(i, n, chain, sqrt, back_ready):
                dve.wait_ge(sqrt.sem, sqrt.at(i, 1))
                dve.reciprocal(inv[:, n, :], rms[:, n, :]).then_inc(chain.next(), 1)
                dve.wait_ge(chain.sem, chain.count())
                dve.tensor_tensor(peak[:, n, :], peak[:, n, :], inv[:, n, :], ALU.mult).then_inc(chain.next(), 1)
                dve.wait_ge(chain.sem, chain.count())
                dve.tensor_scalar(peak[:, n, :], peak[:, n, :], 1e-5, None, ALU.max).then_inc(chain.next(), 1)
                dve.wait_ge(chain.sem, chain.count())
                dve.reciprocal(to_q[:, n, :], peak[:, n, :]).then_inc(chain.next(), 1)
                dve.tensor_scalar(back[:, n, :], peak[:, n, :], w_mean[:, n:n + 1], 1.0 / 127, ALU.mult, ALU.mult).then_inc(back_ready.sem, 1)
                dve.wait_ge(chain.sem, chain.count())
                return dve.scalar_tensor_tensor(to_q[:, n, :], to_q[:, n, :], 127.0, inv[:, n, :], ALU.mult, ALU.mult)

            def x_low(i):
                for half in range(2):
                    dve.wait_ge(xT_high.sem, xT_high.at(i, half + 1))
                    out = slice(2 * half, 2 * half + 2)
                    dve.tensor_tensor(x_T.low[:, out].rearrange("p j c t -> p (j c t)"), banks[half],
                                      x_T.high[:, out].rearrange("p j c t -> p (j c t)").bitcast(F32), ALU.subtract).then_inc(xT_low.sem, 1)

            def low_rank_own(i):
                dve.wait_ge(lr_made.sem, lr_made.at(i, 1))
                dve.tensor_tensor(low_rank[:].rearrange("p (b t) -> p b t", t=SEQ), b_lr.rearrange("p (b t) -> p b t", t=SEQ),
                                  spread(own[:, bass.ds(i * BSEQ, BSEQ)], 2, SEQ), ALU.mult).then_inc(lr_masked.sem, 1)

            def low_rank_low(i):
                dve.wait_ge(lr_high.sem, lr_high.at(i, 1))
                dve.tensor_tensor(lr.low[:, 0, :], low_rank[:], lr.high[:, 0, :].bitcast(F32), ALU.subtract).then_inc(lr_low.sem, 1)

            def gain(i, half):
                dve.wait_ge(c_copied.sem, c_copied.at(i, half + 1))
                out = slice(2 * half, 2 * half + 2)
                dve.tensor_tensor(v[:, out, :], c[:, out, :], spread(g1[:], 1, 2), ALU.mult).then_inc(v_ready.sem, 1)

            def peaks(i):
                first.start(i)
                dve.wait_ge(v_ready.sem, v_ready.at(i, 2))
                dve.tensor_reduce(peak[:, 0, :], v[:], AX, ALU.max, apply_absolute_value=True).then_inc(first.next(), 1)
                dve.wait_ge(first.sem, first.count())

            def quantise(i):
                scales(i, 0, first, sqrt1, back1_ready).then_inc(first.next(), 1)
                dve.wait_ge(first.sem, first.count())
                for j in range(J):
                    last = dve.tensor_scalar(v[:, j, :], v[:, j, :], to_q[:, 0, j:j + 1], MAGIC, ALU.mult, ALU.add)
                last.then_inc(first.next(), 1)
                dve.wait_ge(first.sem, first.count())
                dve.tensor_scalar(v[:], v[:], MAGIC + 127, MAGIC - 128, ALU.min, ALU.max).then_inc(t_ready.sem, 1)
                first.end()

            def integers(i):
                for half in range(2):
                    dve.wait_ge(t_made.sem, t_made.at(i, half + 1))
                    dve.tensor_scalar(q1[:, 2 * half:2 * half + 2].rearrange("p j c t -> p (j c t)"), banks[half], -MAGIC, None,
                                      ALU.add).then_inc(q1_ready.sem, 1)

            def square_relu(i, j):
                dve.wait_ge(r_ready.sem, r_ready.at(i, j + 1))
                dve.wait_ge(v2_ready.sem, v2_ready.at(i, j - 1))
                dve.wait_ge(sums2_ready.sem, sums2_ready.at(i, j - 1))
                dve.tensor_tensor(r2[:, j % 2], r[:, j % 2], r[:, j % 2], ALU.mult).then_inc(r2_ready.sem, 1)

            def peak2(i, j):
                dve.wait_ge(v2_ready.sem, v2_ready.at(i, j + 1))
                return dve.tensor_reduce(peak[:, 1, j:j + 1], v2[:, j, :], AX, ALU.max, apply_absolute_value=True)

            def take(i, j):
                dve.wait_ge(t2_made.sem, t2_made.at(i, j + 1))
                dve.tensor_scalar(q2[:, j % 2, 4:8, :].rearrange("p f t -> p (f t)"), b_t2(j, 1), -MAGIC, None,
                                  ALU.add).then_inc(q2_dve.sem, 1)

            def add(i, j):
                dve.wait_ge(y_made.sem, y_made.at(i, j + 1))
                dve.wait_ge(back2_ready.sem, back2_ready.at(i, 1))
                out = x[:, bass.ds(i * J + j, 1), :].rearrange("p o d -> p (o d)")
                dve.scalar_tensor_tensor(out, b_y[j % 2][:, 0:D], back[:, 1, j:j + 1], out, ALU.mult, ALU.add).then_inc(y_added.sem, 1)

            def step(i, ahead, now):
                if now:
                    square_relu(i, 0)
                if ahead:
                    x_low(i + 1)
                if now:
                    square_relu(i, 1)
                if ahead:
                    low_rank_own(i + 1)
                if now:
                    second.start(i)
                    peak2(i, 0)
                if not now:
                    absolute(0)
                if ahead:
                    low_rank_low(i + 1)
                if not now:
                    absolute(1)
                if now:
                    square_relu(i, 2)
                    peak2(i, 1)
                if ahead:
                    gain(i + 1, 0)
                if now:
                    square_relu(i, 3)
                if ahead:
                    gain(i + 1, 1)
                    peaks(i + 1)
                if not now:
                    weight_scales()
                if now:
                    peak2(i, 2)
                if ahead:
                    quantise(i + 1)
                if now:
                    peak2(i, 3).then_inc(second.next(), 1)
                    dve.wait_ge(second.sem, second.count())
                    scales(i, 1, second, sqrt2, back2_ready).then_inc(to_q2_ready.sem, 1)
                if ahead:
                    integers(i + 1)
                if not now:
                    clip_weights()
                if now:
                    for j in range(J + 2):
                        if j < J:
                            dve.wait_ge(t2_ready.sem, t2_ready.at(i, j + 1))
                            dve.tensor_scalar(t2[:, j % 2], t2[:, j % 2], MAGIC + 127, MAGIC - 128, ALU.min, ALU.max).then_inc(t2_clipped.sem, 1)
                        if 1 <= j <= J:
                            take(i, j - 1)
                        if j >= 2:
                            add(i, j - 2)
                    second.end()

            skewed(dve, step)

        @block.tensor
        def _(pe):
            for made in (xT_made, c_made, h_made, t2_made, y_made):
                made.grant(pe)
            pe.wait_ge(split_low.sem, split_low.at(0, 3))

            def turn_x(i):
                pe.wait_ge(x_copied.sem, x_copied.at(i, 1))
                pe.wait_ge(q1_ready.sem, q1_ready.at(i, 0))
                for half in range(2):
                    for n in range(2 * DC):
                        j, k = 2 * half + n // DC, n % DC
                        last = pe.transpose(banks[half][:, n * P:(n + 1) * P], x_now[:, j, k * P:(k + 1) * P], ident)
                    last.then_inc(xT_made.sem, 1)

            def adapters_down(i):
                pe.wait_ge(xT_low.sem, xT_low.at(i, 2))
                pe.wait_ge(y_added.sem, y_added.at(i - 1, 0))
                product(pe, b_lr, down, x_T, range(DC), lambda a, k: a[:, k, :], lambda a, k: a[:, :, k, :]).then_inc(lr_made.sem, 1)

            def dense(i, half):
                if half:
                    pe.wait_ge(c_copied.sem, c_copied.at(i, half))
                for n in range(2):
                    out, j = b_c[:, n * D:(n + 1) * D], 2 * half + n
                    product(pe, out, x_T, cond, range(DC), lambda a, k: a[:, j, k, :], lambda a, k: a[:, k, :], stop=False)
                    pe.wait_ge(lr_low.sem, lr_low.at(i, 1))
                    last = product(pe, out, lr, up, [0], lambda a, k: a[:, k, j * P:(j + 1) * P], lambda a, k: a[:, k, :], start=False)
                last.then_inc(c_made.sem, 1)

            def turn_v(i):
                pe.wait_ge(t_ready.sem, t_ready.at(i, 1))
                for half in range(2):
                    for n in range(2 * DC):
                        j, k = 2 * half + n // DC, n % DC
                        last = pe.transpose(banks[half][:, n * P:(n + 1) * P], v[:, j, k * P:(k + 1) * P], ident)
                    last.then_inc(t_made.sem, 1)

            def hidden(i, j):
                pe.wait_ge(q1_ready.sem, q1_ready.at(i, j // 2 + 1))
                pe.wait_ge(r_ready.sem, r_ready.at(i, j - 1))
                pe.wait_ge(q2_act.sem, q2_act.at(i, 0))
                pe.wait_ge(q2_dve.sem, q2_dve.at(i, 0))
                for half in range(2):
                    for k in range(DC):
                        last = pe.matmul(b_h(j)[:, half * 512:(half + 1) * 512], q1[:, j, k, :], w1_q[:, k, half * 512:(half + 1) * 512],
                                         start=(k == 0), stop=(k == DC - 1))
                last.then_inc(h_made.sem, 1)

            def turn_t2(i, j):
                pe.wait_ge(t2_clipped.sem, t2_clipped.at(i, j + 1))
                pe.wait_ge(q2_act.sem, q2_act.at(i, j - 1))
                pe.wait_ge(q2_dve.sem, q2_dve.at(i, j - 1))
                for f in range(FC):
                    last = pe.transpose(b_t2(j, f // 4)[:, (f % 4) * P:(f % 4 + 1) * P], t2[:, j % 2, f * P:(f + 1) * P], ident)
                last.then_inc(t2_made.sem, 1)

            def result(i, j):
                pe.wait_ge(q2_act.sem, q2_act.at(i, j + 1))
                pe.wait_ge(q2_dve.sem, q2_dve.at(i, j + 1))
                pe.wait_ge(y_added.sem, y_added.at(i, j - 1))
                for f in range(FC):
                    last = pe.matmul(b_y[j % 2][:, 0:D], q2[:, j % 2, f, :], w2_q[:, f, :], start=(f == 0), stop=(f == FC - 1))
                last.then_inc(y_made.sem, 1)

            def step(i, ahead, now):
                if now:
                    hidden(i, 0)
                    hidden(i, 1)
                if ahead:
                    turn_x(i + 1)
                if now:
                    hidden(i, 2)
                if ahead:
                    adapters_down(i + 1)
                if now:
                    hidden(i, 3)
                if ahead:
                    dense(i + 1, 0)
                    dense(i + 1, 1)
                if not now:
                    pe.wait_ge(abs_ready.sem, abs_ready.at(0, 2))
                    pe.matmul(b_abs, const(consts, "ones"), w_abs[:], start=True, stop=True).then_inc(abs_summed.sem, 1)
                if ahead:
                    turn_v(i + 1)
                    pe.wait_ge(c_copied.sem, c_copied.at(i + 1, 2))
                if not now:
                    pe.wait_ge(w_ready.sem, w_ready.at(0, 2))
                if now:
                    for j in range(J + 1):
                        if j < J:
                            turn_t2(i, j)
                        if j > 0:
                            result(i, j - 1)

            skewed(pe, step)


def position_mix_phase(nc, sems, io, psum, consts, mixes, x, xT, combineT, load_next):
    J = BTILES
    with ExitStack() as ctx:
        def sb(name, shape, dt=F32):
            return ctx.enter_context(nc.sbuf_tensor("m_" + name, shape, dt))

        def sig(name, per=1, free=0):
            return Signal(sems.new("m_" + name), per, free)

        mix_wide = sb("mix_wide", [P, TILES, TSEQ, SEQ])
        mix = [Split(sb, f"mix{u}", [P, J, P]) for u in range(2)]
        x_now = [Split(sb, f"x_now{u}", [P, J, D]) for u in range(2)]
        gate_raw, gate = sb("gate_raw", [P, DC, E3 + 1]), Split(sb, "gate", [P, DC, E3 + 1])
        gate_b, biases = sb("gate_b", [P, E3]), sb("biases", [P, E3])
        logitsT = sb("logitsT", [E3 + 1, T])
        logits = sb("logits", [P, TILES, E3])
        peak = sb("peak", [P, TILES])
        total = sb("total", [P, TILES])
        prob = sb("prob", [P, TILES, E3 + 1])
        biased = sb("biased", [P, TILES, E3 + 1])
        top = sb("top", [P, TILES, 8])
        top_at = sb("top_at", [P, TILES, 8], U32)
        top_e = sb("top_e", [P, TILES, K3])
        hot = sb("hot", [P, TILES, K3, E3 + 1])
        hot_prob = sb("hot_prob", [P, TILES, K3, E3 + 1])
        top_prob = sb("top_prob", [P, TILES, K3])
        comb = sb("comb", [P, E3 + 1, TILES])
        combT = sb("combT", [P, P])

        loaded = sig("loaded")
        set_ = sig("set")
        gate_high = sig("gate_high")
        mix_ready = sig("mix_ready")
        mix_high, mix_low = sig("mix_high", 2), sig("mix_low", 2)
        x_high, x_low = sig("x_high", 2), sig("x_low", 2)
        c_made = sig("c_made", 4, 4)
        c_high, c_low = sig("c_high", 4), sig("c_low", 4, 4)
        logitsT_made, logitsT_ready, logits_made = sig("logitsT_made", 2), sig("logitsT_ready", 2, 2), sig("logits_made")
        act_passed = sig("act_passed")
        shifted, exped = sig("shifted"), sig("exped")
        comb_ready, combT_made, combT_ready, stored = sig("comb_ready"), sig("combT_made"), sig("combT_ready"), sig("stored")
        steps = sig("steps")
        dve_passed = sig("dve_passed")
        block = ctx.enter_context(nc.Block())
        ident, quad, count = (const(consts, n) for n in ("ident", "quad", "count"))
        banks = [psum[:, n, :] for n in range(8)]
        b_gT, b_g, b_t = banks[4:6], banks[6], banks[7]

        @block.sync
        def _(sp):
            sp.wait_ge(set_.sem, set_.at(0, 1))
            sp.dma_start(gate_raw[:, :, 0:E3], io["L3_ffn_gate_w"].rearrange("(c p) e -> p c e", p=P)).then_inc(loaded.sem, 16)
            sp.dma_start(gate_b[:], io["L3_ffn_gate_b"].partition_broadcast(P)).then_inc(loaded.sem, 16)
            sp.dma_start(biases[:], io["L3_ffn_biases"].partition_broadcast(P)).then_inc(loaded.sem, 16)
            load_next(sp)
            sp.wait_ge(combT_ready.sem, combT_ready.at(0, 1))
            sp.dma_start(combineT.rearrange("e (n t) -> (e n) t", t=P), combT[:]).then_inc(stored.sem, 16)
            sp.wait_ge(stored.sem, stored.at(0, 16))

        @block.scalar
        def _(act):
            act.wait_ge(loaded.sem, loaded.at(0, 48))
            act.activation(gate.high[:], gate_raw[:], ACT.Copy).then_inc(gate_high.sem, 1)
            act.wait_ge(mix_ready.sem, mix_ready.at(0, 1))
            logitsT_ready.grant(act)
            def split(i, u):
                act.wait_ge(c_made.sem, c_made.at(i, 2 * u - 2))
                act.sem_inc(act_passed.sem, 1)
                act.activation(x_now[u].high[:], x[:, bass.ds(i * 2 * J + u * J, J), :], ACT.Copy).then_inc(x_high.sem, 1)
                act.activation(mix[u].high[:], mix_wide[:, bass.ds(i * 2 * J + u * J, J)].rearrange("p n b t -> p n (b t)"),
                               ACT.Copy).then_inc(mix_high.sem, 1)

            def keep(i, u):
                for k in range(DC):
                    act.wait_ge(c_made.sem, c_made.at(i, 2 * u + k + 1))
                    act.sem_inc(act_passed.sem, 1)
                    act.activation(xT.high[:, k, bass.ds(i * 2 * BLOCK + u * BLOCK, BLOCK)], banks[2 * u + k], ACT.Copy).then_inc(c_high.sem, 1)

            def keep_logits(i, u):
                act.wait_ge(logitsT_made.sem, logitsT_made.at(i, u + 1))
                act.sem_inc(act_passed.sem, 1)
                act.activation(logitsT[:, bass.ds(i * 2 * BLOCK + u * BLOCK, BLOCK)], b_gT[u][0:E3 + 1, :], ACT.Copy).then_inc(logitsT_ready.sem, 1)

            with act.Fori(0, BLOCKS // 2) as i:
                split(i, 0)
                split(i, 1)
                keep(i, 0)
                keep(i, 1)
                keep_logits(i, 0)
                keep_logits(i, 1)
            act.wait_ge(shifted.sem, shifted.at(0, 1))
            act.activation(logits[:], logits[:], ACT.Exp).then_inc(exped.sem, 1)
            act.wait_ge(combT_made.sem, combT_made.at(0, 1))
            act.activation(combT[:], b_t[:, 0:P], ACT.Copy).then_inc(combT_ready.sem, 1)

        @block.vector
        def _(dve):
            c_low.grant(dve)
            dve.memset(gate_raw[:], 0.0).then_inc(set_.sem, 1)
            dve.memset(prob[:], 0.0).then_inc(set_.sem, 1)
            dve.memset(biased[:], -1e30).then_inc(set_.sem, 1)
            dve.memset(comb[:], 1.0).then_inc(set_.sem, 1)
            dve.tensor_tensor(mix_wide[:], spread(mixes[:], 2, TSEQ), spread(spread(quad, 2, SEQ), 1, TILES), ALU.mult).then_inc(mix_ready.sem, 1)
            dve.wait_ge(gate_high.sem, gate_high.at(0, 1))
            dve.tensor_tensor(gate.low[:], gate_raw[:], gate.high_read, ALU.subtract).then_inc(gate_high.sem, 1)
            dve.wait_ge(mix_ready.sem, mix_ready.at(0, 1))
            def split(i, u):
                dve.wait_ge(x_high.sem, x_high.at(i, u + 1))
                dve.tensor_tensor(x_now[u].low[:], x[:, bass.ds(i * 2 * J + u * J, J), :], x_now[u].high_read, ALU.subtract).then_inc(x_low.sem, 1)
                dve.wait_ge(mix_high.sem, mix_high.at(i, u + 1))
                dve.tensor_tensor(mix[u].low[:], mix_wide[:, bass.ds(i * 2 * J + u * J, J)].rearrange("p n b t -> p n (b t)"),
                                  mix[u].high_read, ALU.subtract).then_inc(mix_low.sem, 1)

            def keep(i, u):
                for k in range(DC):
                    at = bass.ds(i * 2 * BLOCK + u * BLOCK, BLOCK)
                    dve.wait_ge(c_high.sem, c_high.at(i, 2 * u + k + 1))
                    dve.tensor_tensor(xT.low[:, k, at], banks[2 * u + k], xT.high[:, k, at].bitcast(F32), ALU.subtract).then_inc(c_low.sem, 1)

            with dve.Fori(0, BLOCKS // 2) as i:
                split(i, 0)
                split(i, 1)
                keep(i, 0)
                keep(i, 1)

            chain = Chain(dve, steps.sem, 0)
            dve.wait_ge(logits_made.sem, logits_made.at(0, 1))
            dve.wait_ge(set_.sem, set_.at(0, 4))
            dve.tensor_tensor(logits[:], b_g[:, 0:TILES * (E3 + 1)].rearrange("p (n e) -> p n e", e=E3 + 1)[:, :, 0:E3],
                                        spread(gate_b[:], 1, TILES), ALU.add).then_inc(chain.next(), 1)
            dve.wait_ge(chain.sem, chain.count())
            dve.tensor_reduce(peak[:], logits[:], AX, ALU.max).then_inc(chain.next(), 1)
            dve.wait_ge(chain.sem, chain.count())
            dve.tensor_tensor(logits[:], logits[:], spread(peak[:], 2, E3), ALU.subtract).then_inc(shifted.sem, 1)
            dve.wait_ge(exped.sem, exped.at(0, 1))
            dve.tensor_reduce(total[:], logits[:], AX, ALU.add).then_inc(chain.next(), 1)
            dve.wait_ge(chain.sem, chain.count())
            dve.reciprocal(total[:], total[:]).then_inc(chain.next(), 1)
            dve.wait_ge(chain.sem, chain.count())
            dve.tensor_tensor(prob[:, :, 0:E3], logits[:], spread(total[:], 2, E3), ALU.mult).then_inc(chain.next(), 1)
            dve.wait_ge(chain.sem, chain.count())
            dve.tensor_tensor(biased[:, :, 0:E3], prob[:, :, 0:E3], spread(biases[:], 1, TILES), ALU.add).then_inc(chain.next(), 1)
            dve.wait_ge(chain.sem, chain.count())
            for n in range(TILES):
                last = dve.max(top[:, n, :], biased[:, n, :])
            last.then_inc(chain.next(), 1)
            dve.wait_ge(chain.sem, chain.count())
            for n in range(TILES):
                last = dve.max_index(top_at[:, n, :], top[:, n, :], biased[:, n, :])
            last.then_inc(chain.next(), 1)
            dve.wait_ge(chain.sem, chain.count())
            dve.tensor_copy(top_e[:], top_at[:, :, 0:K3]).then_inc(chain.next(), 1)
            dve.wait_ge(chain.sem, chain.count())
            dve.tensor_tensor(hot[:].rearrange("p n k e -> p (n k) e"), spread(count[:, 0:E3 + 1], 1, TILES * K3),
                                        spread(top_e[:].rearrange("p n k -> p (n k)"), 2, E3 + 1), ALU.is_equal).then_inc(chain.next(), 1)
            dve.wait_ge(chain.sem, chain.count())
            dve.tensor_tensor(hot_prob[:], hot[:], spread(prob[:], 2, K3), ALU.mult).then_inc(chain.next(), 1)
            dve.wait_ge(chain.sem, chain.count())
            dve.tensor_reduce(top_prob[:], hot_prob[:], AX, ALU.add).then_inc(chain.next(), 1)
            dve.wait_ge(chain.sem, chain.count())
            dve.tensor_reduce(total[:], top_prob[:], AX, ALU.add).then_inc(chain.next(), 1)
            dve.wait_ge(chain.sem, chain.count())
            dve.reciprocal(total[:], total[:]).then_inc(chain.next(), 1)
            dve.wait_ge(chain.sem, chain.count())
            dve.tensor_tensor(top_prob[:], top_prob[:], spread(total[:], 2, K3), ALU.mult).then_inc(chain.next(), 1)
            dve.wait_ge(chain.sem, chain.count())
            dve.tensor_tensor(hot_prob[:].rearrange("p n k e -> p (n k) e"), hot[:].rearrange("p n k e -> p (n k) e"),
                                        spread(top_prob[:].rearrange("p n k -> p (n k)"), 2, E3 + 1), ALU.mult).then_inc(chain.next(), 1)
            dve.wait_ge(chain.sem, chain.count())
            dve.tensor_reduce(comb[:, 0:E3, :].rearrange("p e n -> p n e"), hot_prob[:, :, :, 0:E3].rearrange("p n k e -> p n e k"),
                              AX, ALU.add).then_inc(comb_ready.sem, 1)

        @block.tensor
        def _(pe):
            c_made.grant(pe)
            pe.wait_ge(gate_high.sem, gate_high.at(0, 2))

            def mixed(i, u):
                pe.wait_ge(x_low.sem, x_low.at(i, u + 1))
                pe.wait_ge(mix_low.sem, mix_low.at(i, u + 1))
                pe.wait_ge(c_low.sem, c_low.at(i, 2 * u - 2))
                for k in range(DC):
                    for j in range(J):
                        last = product(pe, banks[2 * u + k][:, j * P:(j + 1) * P], x_now[u], mix[u], [j],
                                       lambda a, jj: a[:, jj, k * P:(k + 1) * P], lambda a, jj: a[:, jj, :])
                    last.then_inc(c_made.sem, 1)

            def router(i, u):
                pe.wait_ge(c_low.sem, c_low.at(i, 2 * u + 2))
                pe.wait_ge(logitsT_ready.sem, logitsT_ready.at(i, u - 1))
                product(pe, b_gT[u][0:E3 + 1, :], gate, xT, range(DC), lambda a, k: a[:, k, :],
                        lambda a, k: a[:, k, bass.ds(i * 2 * BLOCK + u * BLOCK, BLOCK)]).then_inc(logitsT_made.sem, 1)

            with pe.Fori(0, BLOCKS // 2) as i:
                mixed(i, 0)
                mixed(i, 1)
                router(i, 0)
                router(i, 1)
            pe.wait_ge(logitsT_ready.sem, logitsT_ready.at(BLOCKS // 2, 0))
            for n in range(TILES):
                last = pe.transpose(b_g[:, n * (E3 + 1):(n + 1) * (E3 + 1)], logitsT[:, n * P:(n + 1) * P], ident[0:E3 + 1, 0:E3 + 1])
            last.then_inc(logits_made.sem, 1)
            pe.wait_ge(comb_ready.sem, comb_ready.at(0, 1))
            pe.transpose(b_t[:, 0:P], comb[:].rearrange("p e n -> p (e n)"), ident).then_inc(combT_made.sem, 1)


def build_program(nc, names, args, out):
    io = dict(zip(names, args))
    with ExitStack() as ctx:
        def sb(name, shape, dt=F32):
            return ctx.enter_context(nc.sbuf_tensor(name, shape, dt))

        def dram(name, shape):
            return nc.dram_tensor(name, shape, F32, kind="Internal").ap()

        rows, rows_out = dram("expert_rows", [E0 * CAP, D]), dram("expert_results", [E0 * CAP, D])
        combine1T, combine3T = dram("combine1T", [E1, T]), dram("combine3T", [E3 + 1, T])
        psum = ctx.enter_context(nc.psum_tensor("psum", [P, 8, 512], F32))
        consts = sb("consts", [P, CONSTANTS.shape[1]])
        mixes = sb("mixes", [P, TILES, SEQ])
        slots, weights_eff = sb("slots", [P, TILES, 2], U32), sb("weights_eff", [P, TILES, 2])
        sems = Semaphores(nc)
        attention_phase(nc, sems, io, psum, consts, slots, weights_eff, mixes, rows)
        capacity_experts_phase(nc, sems, io, psum, consts, rows, rows_out)
        sems.clear()

        x, xT = sb("residual", [P, TILES, D]), Split(sb, "inputs", [P, DC, T])
        experts1 = ExpertWeights(sb, sems, "g", io["gate_1"], io["up_1"], io["down_1"], 3)
        chosen_layer_phase(nc, sems, io, psum, consts, slots, weights_eff, rows_out, x, xT, combine1T, experts1.load)
        quantised = QuantisedInputs(sb, sems, io)
        gated_experts_phase(nc, sems, "g", psum, experts1, combine1T, F1, E1, x, xT, quantised.load)
        quantised_phase(nc, sems, psum, consts, quantised, x)
        experts3 = ExpertWeights(sb, sems, "s", io["gate_3"], io["up_3"], io["down_3"], 2)
        position_mix_phase(nc, sems, io, psum, consts, mixes, x, xT, combine3T, experts3.load)
        gated_experts_phase(nc, sems, "s", psum, experts3, combine3T, F3, E3 + 1, x, xT)

        stored = sems.new("stored")
        block = ctx.enter_context(nc.Block())

        @block.sync
        def _(sp):
            sp.dma_start(out.rearrange("s t d -> (s t) d").rearrange("(n p) d -> p n d", p=P), x[:]).then_inc(stored, 16)
            sp.wait_ge(stored, 16)


def laid_out(inputs):
    take = {k: np.asarray(v) for k, v in inputs.items()}
    x = take["x"].reshape(T, D)
    swap = {
        "constants": CONSTANTS,
        "x": x,
        "xT": x.T,
        "w_attention": np.stack([take["L0_cond_W" + n].T for n in "qkvo"]),
        "b1": take["L0_ffn_b1"].reshape(E0, F0 // P, P).transpose(2, 0, 1).reshape(P, -1),
        "gate1": take["L1_ffn_gate_weight"].T,
        "gate_1": take["L1_ffn_gate_up_proj"][:, :F1].transpose(2, 0, 1).reshape(D, -1),
        "up_1": take["L1_ffn_gate_up_proj"][:, F1:].transpose(2, 0, 1).reshape(D, -1),
        "down_1": take["L1_ffn_down_proj"].transpose(0, 2, 1).reshape(-1, D),
        "quant_w1": take["L2_ffn_w1"].T,
        "quant_w2": take["L2_ffn_w2"].T,
        "cond2": take["L2_cond_W"].T,
        "adapter_down": take["L2_cond_A"].reshape(P, D).T,
        "adapter_up": take["L2_cond_Bm"].transpose(0, 2, 1).reshape(P, D),
        "mix_rows": take["L3_cond_weights"].reshape(S3 * SEQ, SEQ),
        "gate_3": np.concatenate([take["L3_ffn_W1"], take["L3_ffn_Ws1"][None]]).transpose(1, 0, 2).reshape(D, -1),
        "up_3": np.concatenate([take["L3_ffn_Wg"], take["L3_ffn_Wsg"][None]]).transpose(1, 0, 2).reshape(D, -1),
        "down_3": np.concatenate([take["L3_ffn_W2"], take["L3_ffn_Ws2"][None]]).reshape(-1, D),
    }
    same = ("cond_1", "L0_ffn_gating_w", "L0_ffn_w1", "L0_ffn_w2", "L0_ffn_b2", "itok_B_0_15", "itok_B_0_6", "itok_B_1_198",
            "L1_cond_W", "L1_cond_b", "L1_ffn_similarity", "L2_ffn_g1", "L2_ffn_g2", "L2_cond_scalings",
            "L3_ffn_gate_w", "L3_ffn_gate_b", "L3_ffn_biases")
    swap.update({name: take[name] for name in same})
    return {name: np.ascontiguousarray(a) for name, a in swap.items()}


def kernel(**inputs):
    import concourse.bacc as bacc
    from concourse.bass_utils import run_bass_kernel_spmd

    nc = bacc.Bacc("TRN2", target_bir_lowering=False, num_devices=1)
    arrays = laid_out(inputs)
    args = [nc.dram_tensor(name, a.shape, mybir.dt.from_np(a.dtype), kind="ExternalInput").ap() for name, a in arrays.items()]
    out = nc.dram_tensor("out", (SEQS, SEQ, D), F32, kind="ExternalOutput").ap()
    build_program(nc, list(arrays), args, out)
    result = run_bass_kernel_spmd(nc, [arrays], core_ids=[0])
    return result.results[0]["out"]
```

```python
from contextlib import ExitStack

import numpy as np

import concourse.bass as bass
from concourse import mybir

F32 = mybir.dt.float32
F32R = mybir.dt.float32r
BF16 = mybir.dt.bfloat16
U32 = mybir.dt.uint32
I32 = mybir.dt.int32
ALU = mybir.AluOpType
ACT = mybir.ActivationFunctionType
AX = mybir.AxisListType.X

P = 128
D = 256
DC = D // P
SEQS, SEQ = 64, 32
T = SEQS * SEQ
TILES = T // P
TSEQ = P // SEQ
BLOCK = 512
BLOCKS = T // BLOCK
BTILES = BLOCK // P
BSEQ = BLOCK // SEQ
HEADS, HD = 16, 16
CHEADS = P // HD
E0, F0 = 8, 1024
CAP = (2 * T * 5 // 4 + E0 - 1) // E0
E1, F1, K1, PRIM1 = 32, 96, 8, 4
W1TAB = 16
A2, R2, F2 = 8, 16, 1024
S3, E3, F3, K3 = 200, 7, 256, 3
MAGIC = 1.5 * 2.0 ** 23

CONST = {}


def constants():
    p = np.arange(P)
    parts = {
        "ident": np.eye(P),
        "before": p[:, None] < p[None, :],
        "ones": np.ones((P, P)),
        "causal": np.where(np.arange(SEQ)[None, :] <= (p % SEQ)[:, None], 0.0, -1e30),
        "head": (p // HD)[:, None] == np.arange(CHEADS)[None, :],
        "quad": (p // SEQ)[:, None] == np.arange(TSEQ)[None, :],
        "count": np.broadcast_to(np.arange(32), (P, 32)),
        "adapter": (p // R2)[:, None],
        "position": (p % SEQ)[:, None],
    }
    at = 0
    for name, part in parts.items():
        CONST[name] = (at, at + part.shape[1])
        at += part.shape[1]
    return np.ascontiguousarray(np.concatenate([np.asarray(x, np.float32) for x in parts.values()], axis=1))


CONSTANTS = constants()


class Signal:

    def __init__(self, sem, per=1, free=0):
        self.sem, self.per, self.free = sem, per, free

    def at(self, i, n):
        value = i * self.per + (n + self.free)
        assert not isinstance(value, int) or value > 0
        return value

    def grant(self, eng):
        eng.sem_inc(self.sem, self.free)


class Semaphores:

    def __init__(self, nc):
        self.nc, self.taken = nc, []

    def new(self, name):
        self.taken.append(self.nc.alloc_semaphore(name))
        return self.taken[-1]

    def clear(self):
        self.nc.clear_and_free_semaphores(self.taken)
        self.nc.all_engine_barrier()
        self.taken = []


class Chain:

    def __init__(self, eng, sem, per):
        self.eng, self.sem, self.per = eng, sem, per
        self.i, self.n = 0, 0

    def start(self, i, n=0):
        self.i, self.n = i, n

    def next(self):
        self.n += 1
        return self.sem

    def count(self):
        return self.i * self.per + self.n

    def end(self):
        assert self.n == self.per, f"steps in a pass: {self.n}, not {self.per}"


def spread(ap, axis, n):
    ap = ap.unsqueeze(axis)
    shape = list(ap.shape)
    shape[axis] = n
    return ap.broadcast_to(shape)


def const(consts, name):
    a, b = CONST[name]
    return consts[:, a:b]


class Split:

    def __init__(self, new, name, shape, low=None):
        self.high = new(name + "_high", shape, F32R)
        self.low = new(name + "_low", shape, F32R) if low is None else low[:].bitcast(F32R)

    @property
    def high_read(self):
        return self.high[:].bitcast(F32)

    def passes(self, other):
        return ((self.high, other.high), (self.high, other.low), (self.low, other.high))


def product(pe, out, stationary, moving, ks, pick_s, pick_m, start=True, stop=True):
    last = None
    n, count = 0, 3 * len(ks)
    for k in ks:
        for s, m in stationary.passes(moving):
            last = pe.matmul(out, pick_s(s, k), pick_m(m, k), start=start and n == 0, stop=stop and n == count - 1,
                             skip_group_check=True)
            n += 1
    return last


def attention_phase(nc, sems, io, psum, consts, slots, weights_eff, mixes, rows, load_next):
    with ExitStack() as ctx:
        def sb(name, shape, dt=F32):
            return ctx.enter_context(nc.sbuf_tensor("a_" + name, shape, dt))

        def sig(name, per=1, free=0):
            return Signal(sems.new("a_" + name), per, free)

        xT = sb("xT", [P, DC, T])
        xs = Split(sb, "x", [P, DC, BLOCK])
        w_raw = sb("w_raw", [P, 4, DC, D])
        ws = Split(sb, "w", [P, 4, DC, D])
        gate_w = sb("gate_w", [P, DC, E0])
        beta = sb("beta", [P, SEQS])
        q = sb("q", [P, DC, BLOCK])
        k = sb("k", [P, DC, BLOCK])
        k_heads = sb("k_heads", [P, BSEQ, DC, CHEADS, SEQ])
        v_heads = sb("v_heads", [P, BSEQ, 4, 4, HD])
        score = sb("score", [P, 2, HEADS, SEQ])
        peak = sb("peak", [P, 2, HEADS])
        total = sb("total", [P, 2, HEADS])
        prob = sb("prob", [P, 2, HEADS, SEQ])
        probT = sb("probT", [P, 2, 4, P])
        os_ = Split(sb, "o", [P, 2, DC, P])
        y = sb("y", [P, BTILES, D])
        yT = sb("yT", [P, 2, DC, P])
        zeros = sb("zeros", [P, 2560])
        g_peak = sb("g_peak", [P, BTILES])
        g_exp = sb("g_exp", [P, BTILES, E0])
        g_sum = sb("g_sum", [P, BTILES])
        gates = sb("gates", [P, BTILES, E0])
        top = sb("top", [P, BTILES, 8])
        top_at = sb("top_at", [P, BTILES, 8], U32)
        top_e = sb("top_e", [P, BTILES, 2])
        w_sum = sb("w_sum", [P, BTILES])
        w_norm = sb("w_norm", [P, BTILES, 2])
        chosen = sb("chosen", [P, BTILES, 2, E0])
        taken = sb("taken", [P, BTILES, E0])
        before = sb("before", [P, BTILES + 1, E0])
        place_of = sb("place_of", [P, BTILES, 2, E0])
        place = sb("place", [P, BTILES, 2])
        valid = sb("valid", [P, BTILES, 2])
        lost = sb("lost", [P, BTILES, 2])
        slot = sb("slot", [P, BTILES, 2])
        target = sb("target", [P, BTILES, 2])
        scatter_at = sb("scatter_at", [P, BTILES, 2], U32)

        mix_id = sb("mix_id", [P, SEQS], I32)
        mix_own = sb("mix_own", [P, TILES, TSEQ])
        mix_row_f = sb("mix_row_f", [P, TILES])
        mix_row = sb("mix_row", [P, TILES], U32)

        mix_ids_loaded = sig("mix_ids_loaded")
        mix_rows_ready = sig("mix_rows_ready")
        mixes_loaded = sig("mixes_loaded")
        loaded = sig("loaded")
        weights_loaded = sig("weights_loaded")
        x_loaded, x_rest_loaded = sig("x_loaded"), sig("x_rest_loaded")
        rows_cleared = sig("rows_cleared")
        zeros_set = sig("zeros_set")
        beta_ready = sig("beta_ready")
        w_high, w_low = sig("w_high"), sig("w_low")
        x_high = sig("x_high")
        x_low = sig("x_low")
        q_made = sig("q_made", 2)
        k_made = sig("k_made", 2)
        v_made = sig("v_made", 1, 1)
        v_cleared = sig("v_cleared")
        q_ready = sig("q_ready", 2)
        k_copied = sig("k_copied", 2)
        k_heads_dve = sig("k_heads_dve")
        k_heads_act = sig("k_heads_act", 2)
        v_ready_act = sig("v_ready_act")
        v_ready_dve = sig("v_ready_dve")
        s_made = sig("s_made", BTILES, 2)
        s_masked = sig("s_masked", BTILES, 2)
        s_shifted = sig("s_shifted", BTILES)
        s_exp = sig("s_exp", BTILES)
        p_ready = sig("p_ready", BTILES, 2)
        pT_made = sig("pT_made", BTILES, 2)
        pT_ready = sig("pT_ready", BTILES, 2)
        o_made = sig("o_made", BTILES, 2)
        o_high = sig("o_high", BTILES)
        o_low = sig("o_low", BTILES, 2)
        y_made = sig("y_made", BTILES, 2)
        y_ready = sig("y_ready", BTILES, 2)
        yT_made = sig("yT_made", BTILES)
        yT_ready = sig("yT_ready", BTILES, 2)
        logits_made = sig("logits_made")
        g_shifted = sig("g_shifted")
        g_exped = sig("g_exped")
        taken_ready = sig("taken_ready")
        places_made = sig("places_made")
        targets_ready = sig("targets_ready")
        scattered = sig("scattered", 2 * BTILES * 16)
        y_left = sig("y_left", 1, 1)
        steps, softmax_steps = sig("steps"), sig("softmax_steps")
        pool_passed = sig("pool_passed")
        dve_passed = sig("dve_passed")
        block = ctx.enter_context(nc.Block())

        ident = const(consts, "ident")
        banks = [psum[:, n, :] for n in range(8)]
        v_psum = psum[:, 4:6, :].rearrange("p n (j g h d) -> p (n j) g h d", g=4, h=4, d=HD)

        def place_values(engine, i, quads):
            engine.wait_ge(v_made.sem, v_made.at(i, 1))
            engine.wait_ge(o_made.sem, o_made.at(i, 0))
            for b in quads:
                for h in range(4):
                    src = v_psum[b * SEQ:(b + 1) * SEQ, :, :, h, :]
                    dst = v_heads[h * SEQ:(h + 1) * SEQ, b:BSEQ:TSEQ, :, h, :]
                    if engine is nc.scalar:
                        last = engine.activation(dst, src, ACT.Copy)
                    else:
                        last = engine.tensor_copy(dst, src)
            return last
        b_q, b_k = banks[0:2], banks[2:4]
        b_s, b_pT, b_y, b_yT, b_o, b_g = banks[0:2], banks[2:4], banks[4], banks[5], banks[6], banks[7]

        def stages(tile_steps, first=0, beside=None):
            for s in range(first, BTILES + max(lag for lag, _ in tile_steps)):
                for lag, work in tile_steps:
                    if 0 <= s - lag < BTILES:
                        work(s - lag)
                for work in (beside or {}).get(s, ()):
                    work()

        def skewed(engine, step):
            step(-1, True, False)
            with engine.Fori(0, BLOCKS - 1) as i:
                step(i, True, True)
            step(BLOCKS - 1, False, True)

        @block.sync
        def _(sp):
            sp.dma_start(w_raw[:], io["w_attention"].rearrange("w (c p) e -> p w c e", p=P)).then_inc(weights_loaded.sem, 16)
            x_rows = io["xT"].rearrange("(c p) t -> p c t", p=P)
            sp.dma_start(xT[:, :, 0:BLOCK], x_rows[:, :, 0:BLOCK]).then_inc(x_loaded.sem, 16)
            sp.dma_start(consts[:], io["constants"]).then_inc(loaded.sem, 16)
            sp.dma_start(gate_w[:], io["L0_ffn_gating_w"].rearrange("(c p) e -> p c e", p=P)).then_inc(loaded.sem, 16)
            sp.dma_start(beta[:], io["cond_1"].rearrange("b o -> (b o)").partition_broadcast(P)).then_inc(loaded.sem, 16)
            sp.dma_start(xT[:, :, BLOCK:T], x_rows[:, :, BLOCK:T]).then_inc(x_rest_loaded.sem, 16)
            sp.dma_start(mix_id[:], io["itok_B_1_198"].partition_broadcast(P)).then_inc(mix_ids_loaded.sem, 16)
            sp.wait_ge(zeros_set.sem, zeros_set.at(0, 1))
            clear = rows.rearrange("(n p r) d -> n p (r d)", p=P, r=10)
            for n in range(clear.shape[0]):
                sp.dma_start(clear[n], zeros[:]).then_inc(rows_cleared.sem, 16)
            load_next(sp)

        @block.gpsimd
        def _(pool):
            y_left.grant(pool)
            pool.memset(v_heads[:], 0.0).then_inc(v_cleared.sem, 1)
            pool.wait_ge(mix_rows_ready.sem, mix_rows_ready.at(0, 5))
            for n in range(TILES):
                pool.indirect_dma_start(mixes[:, n, :], None, io["mix_rows"],
                                        bass.IndirectOffsetOnAxis(ap=mix_row[:, n:n + 1], axis=0)).then_inc(mixes_loaded.sem, 16)
            pool.wait_ge(rows_cleared.sem, rows_cleared.at(0, 16 * (E0 * CAP // (10 * P))))

            def scatter(i):
                pool.wait_ge(targets_ready.sem, targets_ready.at(i, 1))
                pool.sem_inc(pool_passed.sem, 1)
                for j in range(BTILES):
                    for c in range(2):
                        pool.indirect_dma_start(
                            rows, bass.IndirectOffsetOnAxis(ap=scatter_at[:, j, c:c + 1], axis=0), y[:, j, :], None,
                            bounds_check=E0 * CAP - 1, oob_is_err=False).then_inc(scattered.sem, 16)
                pool.wait_ge(scattered.sem, scattered.at(i, 2 * BTILES * 16))
                pool.sem_inc(y_left.sem, 1)

            with pool.Fori(0, BLOCKS) as i:
                scatter(i)
            pool.wait_ge(mixes_loaded.sem, mixes_loaded.at(0, 16 * TILES))

        @block.scalar
        def _(act):
            act.wait_ge(v_cleared.sem, v_cleared.at(0, 1))
            act.wait_ge(weights_loaded.sem, weights_loaded.at(0, 16))
            for w in range(4):
                act.activation(ws.high[:, w], w_raw[:, w], ACT.Copy).then_inc(w_high.sem, 1)
            act.wait_ge(x_loaded.sem, x_loaded.at(0, 16))
            head = const(consts, "head")

            def x_split(i):
                act.wait_ge(v_made.sem, v_made.at(i, 0))
                act.activation(xs.high[:], xT[:, :, bass.ds(i * BLOCK, BLOCK)], ACT.Copy).then_inc(x_high.sem, 1)

            def k_out(i):
                for c in range(DC):
                    act.wait_ge(k_made.sem, k_made.at(i, c + 1))
                    act.activation(k[:, c, :], b_k[c], ACT.Copy).then_inc(k_copied.sem, 1)

            def k_spread(i, heads):
                act.wait_ge(k_copied.sem, k_copied.at(i, 2))
                act.wait_ge(s_made.sem, s_made.at(i, 0))
                for h in heads:
                    last = act.activation(k_heads[:, :, 1, h, :], k[:, 1, :].rearrange("p (b t) -> p b t", t=SEQ),
                                          ACT.Copy, scale=head[:, h:h + 1])
                last.then_inc(k_heads_act.sem, 1)

            def exp(i, j):
                act.wait_ge(s_shifted.sem, s_shifted.at(i, j + 1))
                act.activation(score[:, j % 2], score[:, j % 2], ACT.Exp).then_inc(s_exp.sem, 1)

            def turn(i, j):
                act.wait_ge(pT_made.sem, pT_made.at(i, j + 1))
                act.wait_ge(o_made.sem, o_made.at(i, j - 1))
                act.activation(probT[:, j % 2], b_pT[j % 2], ACT.Copy).then_inc(pT_ready.sem, 1)

            def o(i, j):
                act.wait_ge(o_made.sem, o_made.at(i, j + 1))
                act.wait_ge(y_made.sem, y_made.at(i, j - 1))
                act.activation(os_.high[:, j % 2], b_o[:, 0:D], ACT.Copy).then_inc(o_high.sem, 1)

            def y_out(i, j):
                act.wait_ge(y_made.sem, y_made.at(i, j + 1))
                if j == 0:
                    act.wait_ge(y_left.sem, y_left.at(i, 0))
                act.activation(y[:, j, :], b_y[:, 0:D], ACT.Copy).then_inc(y_ready.sem, 1)

            def yT_out(i, j):
                act.wait_ge(yT_made.sem, yT_made.at(i, j + 1))
                act.activation(yT[:, j % 2], b_yT[:, 0:D], ACT.Copy).then_inc(yT_ready.sem, 1)

            for made in (pT_ready, y_ready, yT_ready):
                made.grant(act)

            def step(i, ahead, now):
                if not now:
                    x_split(i + 1)
                    act.wait_ge(loaded.sem, loaded.at(0, 48))
                    act.wait_ge(x_rest_loaded.sem, x_rest_loaded.at(0, 16))
                    k_out(i + 1)
                if now:
                    work = [(2, lambda j: turn(i, j)), (0, lambda j: exp(i, j)), (3, lambda j: o(i, j)), (4, lambda j: y_out(i, j)),
                            (5, lambda j: yT_out(i, j))]
                    stages(work, 2, {2: [lambda: x_split(i + 1)], 7: [lambda: k_out(i + 1)]} if ahead else None)
                if ahead:
                    k_spread(i + 1, range(0, CHEADS // 2))
                if now:
                    act.wait_ge(g_shifted.sem, g_shifted.at(i, 1))
                    act.activation(g_exp[:], g_exp[:], ACT.Exp).then_inc(g_exped.sem, 1)
                if ahead:
                    k_spread(i + 1, range(CHEADS // 2, CHEADS))
                    place_values(act, i + 1, (0, 1)).then_inc(v_ready_act.sem, 1)
                    exp(i + 1, 0)
                    exp(i + 1, 1)

            skewed(act, step)

        @block.vector
        def _(dve):
            chain, softmax = Chain(dve, steps.sem, 22), Chain(dve, softmax_steps.sem, 3 * BTILES)
            s_masked.grant(dve)
            o_low.grant(dve)
            p_ready.grant(dve)
            dve.memset(zeros[:], 0.0).then_inc(zeros_set.sem, 1)
            dve.wait_ge(v_cleared.sem, v_cleared.at(0, 1))
            def x_split(i):
                dve.wait_ge(x_high.sem, x_high.at(i, 1))
                dve.tensor_tensor(xs.low[:], xT[:, :, bass.ds(i * BLOCK, BLOCK)], xs.high_read, ALU.subtract).then_inc(x_low.sem, 1)

            for w in range(4):
                dve.wait_ge(w_high.sem, w_high.at(0, w + 1))
                dve.tensor_tensor(ws.low[:, w], w_raw[:, w], ws.high[:, w].bitcast(F32), ALU.subtract).then_inc(w_low.sem, 1)
            x_split(0)
            dve.wait_ge(loaded.sem, loaded.at(0, 48))
            dve.tensor_scalar(beta[:], beta[:], 4.0, 0.25, ALU.min, ALU.mult).then_inc(beta_ready.sem, 1)
            dve.memset(before[:, 0, :], 0.0).then_inc(beta_ready.sem, 1)
            dve.wait_ge(beta_ready.sem, beta_ready.at(0, 2))
            dve.wait_ge(mix_ids_loaded.sem, mix_ids_loaded.at(0, 16))
            dve.tensor_copy(mix_own[:].rearrange("p n b -> p (n b)"), mix_id[:]).then_inc(mix_rows_ready.sem, 1)
            dve.wait_ge(mix_rows_ready.sem, mix_rows_ready.at(0, 1))
            dve.tensor_tensor(mix_own[:], mix_own[:], spread(const(consts, "quad"), 1, TILES), ALU.mult).then_inc(mix_rows_ready.sem, 1)
            dve.wait_ge(mix_rows_ready.sem, mix_rows_ready.at(0, 2))
            dve.tensor_reduce(mix_row_f[:], mix_own[:], AX, ALU.add).then_inc(mix_rows_ready.sem, 1)
            dve.wait_ge(mix_rows_ready.sem, mix_rows_ready.at(0, 3))
            dve.tensor_scalar(mix_row_f[:], mix_row_f[:], float(SEQ), const(consts, "position"), ALU.mult, ALU.add).then_inc(mix_rows_ready.sem, 1)
            dve.wait_ge(mix_rows_ready.sem, mix_rows_ready.at(0, 4))
            dve.tensor_copy(mix_row[:], mix_row_f[:]).then_inc(mix_rows_ready.sem, 1)
            head, causal, count = (const(consts, n) for n in ("head", "causal", "count"))

            def q_out(i):
                for c in range(DC):
                    dve.wait_ge(q_made.sem, q_made.at(i, c + 1))
                    dve.tensor_tensor(q[:, c, :].rearrange("p (b t) -> p b t", t=SEQ),
                                      b_q[c].rearrange("p (b t) -> p b t", t=SEQ),
                                      spread(beta[:, bass.ds(i * BSEQ, BSEQ)], 2, SEQ), ALU.mult).then_inc(q_ready.sem, 1)

            def k_spread(i):
                dve.wait_ge(k_copied.sem, k_copied.at(i, 1))
                for h in range(CHEADS):
                    last = dve.tensor_scalar(k_heads[:, :, 0, h, :], k[:, 0, :].rearrange("p (b t) -> p b t", t=SEQ),
                                             head[:, h:h + 1], None, ALU.mult)
                last.then_inc(k_heads_dve.sem, 1)

            def shift(i, j):
                sc = score[:, j % 2]
                dve.wait_ge(s_made.sem, s_made.at(i, j + 1))
                dve.wait_ge(p_ready.sem, p_ready.at(i, j - 1))
                dve.tensor_tensor(sc, b_s[j % 2].rearrange("p (h t) -> p h t", t=SEQ), spread(causal, 1, HEADS),
                                  ALU.add).then_inc(s_masked.sem, 1)
                dve.wait_ge(s_masked.sem, s_masked.at(i, j + 1))
                dve.tensor_reduce(peak[:, j % 2], sc, AX, ALU.max).then_inc(softmax.next(), 1)
                dve.wait_ge(softmax.sem, softmax.count())
                dve.tensor_tensor(sc, sc, spread(peak[:, j % 2], 2, SEQ), ALU.subtract).then_inc(s_shifted.sem, 1)

            def normalise(i, j):
                sc, tot = score[:, j % 2], total[:, j % 2]
                dve.wait_ge(s_exp.sem, s_exp.at(i, j + 1))
                dve.tensor_reduce(tot, sc, AX, ALU.add).then_inc(softmax.next(), 1)
                dve.wait_ge(softmax.sem, softmax.count())
                dve.reciprocal(tot, tot).then_inc(softmax.next(), 1)
                dve.wait_ge(softmax.sem, softmax.count())
                dve.wait_ge(pT_made.sem, pT_made.at(i, j - 1))
                dve.tensor_tensor(prob[:, j % 2], sc, spread(tot, 2, SEQ), ALU.mult).then_inc(p_ready.sem, 1)

            def o(i, j):
                dve.wait_ge(o_high.sem, o_high.at(i, j + 1))
                dve.tensor_tensor(os_.low[:, j % 2], b_o[:, 0:D].rearrange("p (c t) -> p c t", t=P),
                                  os_.high[:, j % 2].bitcast(F32), ALU.subtract).then_inc(o_low.sem, 1)

            def route(i):
                logits = b_g[:, 0:BTILES * E0].rearrange("p (j e) -> p j e", e=E0)
                dve.wait_ge(logits_made.sem, logits_made.at(i, 1))
                dve.tensor_reduce(g_peak[:], logits, AX, ALU.max).then_inc(chain.next(), 1)
                dve.wait_ge(chain.sem, chain.count())
                dve.tensor_tensor(g_exp[:], logits, spread(g_peak[:], 2, E0), ALU.subtract).then_inc(g_shifted.sem, 1)
                dve.wait_ge(g_exped.sem, g_exped.at(i, 1))
                dve.tensor_reduce(g_sum[:], g_exp[:], AX, ALU.add).then_inc(chain.next(), 1)
                dve.wait_ge(chain.sem, chain.count())
                dve.reciprocal(g_sum[:], g_sum[:]).then_inc(chain.next(), 1)
                dve.wait_ge(chain.sem, chain.count())
                dve.tensor_tensor(gates[:], g_exp[:], spread(g_sum[:], 2, E0), ALU.mult).then_inc(chain.next(), 1)
                dve.wait_ge(chain.sem, chain.count())
                dve.sem_inc(dve_passed.sem, 1)
                for j in range(BTILES):
                    last = dve.max(top[:, j, :], gates[:, j, :])
                last.then_inc(chain.next(), 1)
                dve.wait_ge(chain.sem, chain.count())
                dve.sem_inc(dve_passed.sem, 1)
                for j in range(BTILES):
                    last = dve.max_index(top_at[:, j, :], top[:, j, :], gates[:, j, :])
                last.then_inc(chain.next(), 1)
                dve.wait_ge(chain.sem, chain.count())
                dve.tensor_tensor(w_sum[:], top[:, :, 0], top[:, :, 1], ALU.add)
                dve.tensor_copy(top_e[:], top_at[:, :, 0:2]).then_inc(chain.next(), 1)
                dve.wait_ge(chain.sem, chain.count())
                dve.tensor_scalar(w_sum[:], w_sum[:], 1e-8, None, ALU.add).then_inc(chain.next(), 1)
                dve.tensor_tensor(chosen[:], spread(spread(count[:, 0:E0], 1, 2), 1, BTILES),
                                            spread(top_e[:], 3, E0), ALU.is_equal).then_inc(chain.next(), 1)
                dve.wait_ge(chain.sem, chain.count())
                dve.reciprocal(w_sum[:], w_sum[:]).then_inc(chain.next(), 1)
                dve.tensor_tensor(taken[:], chosen[:, :, 0, :], chosen[:, :, 1, :], ALU.add).then_inc(chain.next(), 1)
                dve.wait_ge(chain.sem, chain.count())
                dve.tensor_tensor(w_norm[:], top[:, :, 0:2], spread(w_sum[:], 2, 2), ALU.mult).then_inc(chain.next(), 1)
                for j in range(BTILES):
                    last = dve.tensor_tensor(before[:, j + 1, :], before[:, j, :], taken[:, j, :], ALU.add)
                    if j < BTILES - 1:
                        last.then_inc(chain.next(), 1)
                        dve.wait_ge(chain.sem, chain.count())
                last.then_inc(taken_ready.sem, 1)

            def assign(i):
                dve.wait_ge(taken_ready.sem, taken_ready.at(i, 1))
                dve.wait_ge(places_made.sem, places_made.at(i, 1))
                counts = b_g[:, 64:64 + BTILES * E0].rearrange("p (j e) -> p j e", e=E0)
                for c in range(2):
                    last = dve.tensor_tensor(place_of[:, :, c, :], chosen[:, :, c, :], counts, ALU.mult)
                last.then_inc(chain.next(), 1)
                dve.tensor_copy(before[:, 0, :], before[:, BTILES, :]).then_inc(chain.next(), 1)
                dve.wait_ge(chain.sem, chain.count())
                dve.tensor_reduce(place[:], place_of[:], AX, ALU.add).then_inc(chain.next(), 1)
                dve.wait_ge(chain.sem, chain.count())
                dve.tensor_scalar(valid[:], place[:], float(CAP), None, ALU.is_lt).then_inc(chain.next(), 1)
                dve.tensor_scalar(place[:], place[:], float(CAP - 1), None, ALU.min).then_inc(chain.next(), 1)
                dve.wait_ge(chain.sem, chain.count())
                dve.tensor_scalar(lost[:], valid[:], -1e6, 1e6, ALU.mult, ALU.add)
                dve.scalar_tensor_tensor(slot[:], top_e[:], float(CAP), place[:], ALU.mult, ALU.add).then_inc(chain.next(), 1)
                dve.wait_ge(chain.sem, chain.count())
                dve.tensor_tensor(target[:], slot[:], lost[:], ALU.add).then_inc(chain.next(), 1)
                dve.tensor_copy(slots[:, bass.ds(i * BTILES, BTILES), :], slot[:])
                dve.tensor_tensor(weights_eff[:, bass.ds(i * BTILES, BTILES), :], w_norm[:], valid[:], ALU.mult)
                dve.wait_ge(chain.sem, chain.count())
                dve.wait_ge(y_left.sem, y_left.at(i, 0))
                dve.tensor_copy(scatter_at[:], target[:]).then_inc(targets_ready.sem, 1)

            def step(i, ahead, now):
                if not now:
                    q_out(i + 1)
                if now:
                    softmax.start(i, 6)
                    shift(i, 2)
                    work = [(0, lambda j: shift(i, j)), (1, lambda j: normalise(i, j)), (3, lambda j: o(i, j))]
                    stages(work, 3, {3: [lambda: x_split(i + 1)], 5: [lambda: q_out(i + 1)]} if ahead else None)
                    softmax.end()
                if ahead:
                    k_spread(i + 1)
                if now:
                    chain.start(i)
                    route(i)
                if ahead:
                    softmax.start(i + 1)
                    shift(i + 1, 0)
                    shift(i + 1, 1)
                    normalise(i + 1, 0)
                    place_values(dve, i + 1, (2, 3)).then_inc(v_ready_dve.sem, 1)
                    normalise(i + 1, 1)
                if now:
                    assign(i)
                    chain.end()

            skewed(dve, step)

        @block.tensor
        def _(pe):
            for made in (v_made, s_made, pT_made, o_made, y_made):
                made.grant(pe)

            def project(i, w, made, out, c):
                if w == 0:
                    pe.wait_ge(x_high.sem, x_high.at(i, 1))
                    pe.wait_ge(x_low.sem, x_low.at(i, 1))
                    pe.wait_ge(s_masked.sem, s_masked.at(i, 0))
                else:
                    pe.wait_ge(pT_ready.sem, pT_ready.at(i, 0))
                product(pe, out[c], ws, xs, range(DC), lambda a, kk: a[:, w, kk, c * P:(c + 1) * P],
                        lambda a, kk: a[:, kk, :]).then_inc(made.sem, 1)

            def project_v(i):
                pe.wait_ge(y_ready.sem, y_ready.at(i, 0))
                pe.wait_ge(yT_ready.sem, yT_ready.at(i, 0))
                for j in range(BTILES):
                    last = product(pe, banks[4 + j // 2][:, (j % 2) * D:(j % 2 + 1) * D], xs, ws, range(DC),
                                   lambda a, kk: a[:, kk, j * P:(j + 1) * P], lambda a, kk: a[:, 2, kk, :])
                last.then_inc(v_made.sem, 1)

            def scores(i, j):
                if j == 0:
                    pe.wait_ge(q_ready.sem, q_ready.at(i, 2))
                    pe.wait_ge(k_heads_dve.sem, k_heads_dve.at(i, 1))
                    pe.wait_ge(k_heads_act.sem, k_heads_act.at(i, 2))
                if j >= 2:
                    pe.wait_ge(s_masked.sem, s_masked.at(i, j - 1))
                for c in range(DC):
                    for b in range(TSEQ):
                        at = j * TSEQ + b
                        last = pe.matmul(b_s[j % 2][b * SEQ:(b + 1) * SEQ, c * D:(c + 1) * D],
                                         q[:, c, at * SEQ:(at + 1) * SEQ],
                                         k_heads[:, at, c].rearrange("p h t -> p (h t)"), start=True, stop=True,
                                         skip_group_check=True)
                last.then_inc(s_made.sem, 1)

            def turn(i, j):
                pe.wait_ge(p_ready.sem, p_ready.at(i, j + 1))
                if j == 0:
                    pe.wait_ge(k_copied.sem, k_copied.at(i, 2))
                pe.wait_ge(pT_ready.sem, pT_ready.at(i, j - 1))
                for g in range(4):
                    last = pe.transpose(b_pT[j % 2][:, g * P:(g + 1) * P],
                                        prob[:, j % 2, 4 * g:4 * g + 4, :].rearrange("p h t -> p (h t)"), ident)
                last.then_inc(pT_made.sem, 1)

            def mix(i, j):
                pe.wait_ge(pT_ready.sem, pT_ready.at(i, j + 1))
                if j == 0:
                    pe.wait_ge(v_ready_act.sem, v_ready_act.at(i, 1))
                    pe.wait_ge(v_ready_dve.sem, v_ready_dve.at(i, 1))
                pe.wait_ge(o_low.sem, o_low.at(i, j))
                for g in range(4):
                    for b in range(TSEQ):
                        out = b_o[64 * (g % 2):64 * (g % 2) + 64, (g // 2) * P + b * SEQ:(g // 2) * P + (b + 1) * SEQ]
                        last = pe.matmul(out, v_heads[:, j * TSEQ + b, g].rearrange("p h d -> p (h d)"),
                                         probT[:, j % 2, g, b * SEQ:(b + 1) * SEQ], start=True, stop=True,
                                         skip_group_check=True)
                last.then_inc(o_made.sem, 1)

            def out(i, j):
                pe.wait_ge(o_high.sem, o_high.at(i, j + 1))
                pe.wait_ge(o_low.sem, o_low.at(i, j + 1))
                pe.wait_ge(y_ready.sem, y_ready.at(i, j))
                product(pe, b_y[:, 0:D], os_, ws, range(DC), lambda a, kk: a[:, j % 2, kk, :],
                        lambda a, kk: a[:, 3, kk, :]).then_inc(y_made.sem, 1)

            def turn_y(i, j):
                pe.wait_ge(y_ready.sem, y_ready.at(i, j + 1))
                pe.wait_ge(yT_ready.sem, yT_ready.at(i, j))
                for c in range(DC):
                    last = pe.transpose(b_yT[:, c * P:(c + 1) * P], y[:, j, c * P:(c + 1) * P], ident)
                last.then_inc(yT_made.sem, 1)

            def gate(i, j):
                pe.wait_ge(yT_ready.sem, yT_ready.at(i, j + 1))
                for c in range(DC):
                    last = pe.matmul(b_g[:, j * E0:(j + 1) * E0], yT[:, j % 2, c, :], gate_w[:, c, :],
                                     start=(c == 0), stop=(c == DC - 1), skip_group_check=True)
                if j == BTILES - 1:
                    last.then_inc(logits_made.sem, 1)

            def places(i):
                pe.wait_ge(taken_ready.sem, taken_ready.at(i, 1))
                pe.matmul(b_g[:, 64:64 + BTILES * E0], const(consts, "before"), taken[:].rearrange("p j e -> p (j e)"),
                          start=True, stop=False, skip_group_check=True)
                pe.matmul(b_g[:, 64:64 + BTILES * E0], const(consts, "ones"),
                          before[:, 0:BTILES, :].rearrange("p j e -> p (j e)"), start=False, stop=True,
                          skip_group_check=True).then_inc(places_made.sem, 1)

            def step(i, ahead, now):
                q_parts = [lambda c=c: project(i + 1, 0, q_made, b_q, c) for c in range(DC)]
                k_parts = [lambda c=c: project(i + 1, 1, k_made, b_k, c) for c in range(DC)]
                if not now:
                    for part, w in zip(q_parts + k_parts, (0, 0, 1, 1)):
                        pe.wait_ge(w_low.sem, w_low.at(0, w + 1))
                        part()
                    pe.wait_ge(w_low.sem, w_low.at(0, 4))
                    pe.wait_ge(loaded.sem, loaded.at(0, 48))
                if now:
                    work = [(0, lambda j: scores(i, j)), (2, lambda j: turn(i, j)), (3, lambda j: mix(i, j)), (4, lambda j: out(i, j)),
                            (5, lambda j: turn_y(i, j)), (6, lambda j: gate(i, j))]
                    stages(work, 2, {4: q_parts[0:1], 5: q_parts[1:2], 6: k_parts[0:1], 7: k_parts[1:2]} if ahead else None)
                if ahead:
                    project_v(i + 1)
                    scores(i + 1, 0)
                    scores(i + 1, 1)
                if now:
                    places(i)

            skewed(pe, step)


class CapacityWeights:

    def __init__(self, sb, sems, io):
        self.io = io
        self.w1, self.w2 = sb("e_w1_raw", [P, DC, F0]), sb("e_w2_raw", [P, F0 // P, D])
        self.b1, self.b2 = sb("e_b1", [P, E0 * F0 // P]), sb("e_b2", [P, E0 * D])
        self.biases_loaded = Signal(sems.new("e_biases_loaded"))
        self.w1_loaded, self.w2_loaded = Signal(sems.new("e_w1_loaded"), 16), Signal(sems.new("e_w2_loaded"), 16)

    def load_w1(self, sp, e):
        sp.dma_start(self.w1[:], self.io["L0_ffn_w1"][bass.ds(e, 1)].rearrange("o (c p) f -> p (o c) f", p=P)).then_inc(self.w1_loaded.sem, 16)

    def load_w2(self, sp, e):
        sp.dma_start(self.w2[:], self.io["L0_ffn_w2"][bass.ds(e, 1)].rearrange("o (f p) d -> p (o f) d", p=P)).then_inc(self.w2_loaded.sem, 16)

    def load(self, sp):
        self.load_w1(sp, 0)
        self.load_w2(sp, 0)
        sp.dma_start(self.b1[:], self.io["b1"]).then_inc(self.biases_loaded.sem, 16)
        sp.dma_start(self.b2[:], self.io["L0_ffn_b2"].rearrange("e d -> (e d)").partition_broadcast(P)).then_inc(self.biases_loaded.sem, 16)


def capacity_experts_phase(nc, sems, psum, consts, raws, rows, rows_out, load_next):
    CT, HALF, FC = CAP // P, CAP // 2, F0 // P
    STEPS = 2 * FC
    TURNS = ((4,), (0, 1), (2, 3))
    with ExitStack() as ctx:
        def sb(name, shape, dt=F32):
            return ctx.enter_context(nc.sbuf_tensor("e_" + name, shape, dt))

        def sig(name, per=1, free=0):
            return Signal(sems.new("e_" + name), per, free)

        w1_raw, w2_raw, b1, b2 = raws.w1, raws.w2, raws.b1, raws.b2
        biases_loaded, w1_loaded, w2_loaded = raws.biases_loaded, raws.w1_loaded, raws.w2_loaded
        w1, w2 = Split(sb, "w1", [P, DC, F0]), Split(sb, "w2", [P, FC, D])
        row = sb("row", [P, CT, D])
        rT = Split(sb, "rT", [P, DC, CAP])
        relu = sb("relu", [P, 4, HALF])
        h = Split(sb, "h", [P, FC, CAP])
        y = sb("y", [P, CT, D])
        b1_now = sb("b1_now", [P, FC])

        rows_loaded = sig("rows_loaded", 16)
        w1_high, w1_low = sig("w1_high"), sig("w1_low")
        w2_high, w2_low = sig("w2_high"), sig("w2_low")
        rT_made = sig("rT_made", len(TURNS))
        rT_high = sig("rT_high", len(TURNS))
        rT_low = sig("rT_low", len(TURNS))
        h_made = sig("h_made", STEPS)
        h_relu = sig("h_relu", STEPS, 4)
        h_high_act, h_high_dve = sig("h_high_act", STEPS // 2), sig("h_high_dve", STEPS // 2)
        h_ready = sig("h_ready", STEPS, 4)
        b1_ready = sig("b1_ready")
        sp_passed = sig("sp_passed")
        y_made = sig("y_made", CT, 2)
        y_ready = sig("y_ready", CT, 2)
        y_stored = sig("y_stored", 16, 16)
        block = ctx.enter_context(nc.Block())
        ident = const(consts, "ident")
        banks = [psum[:, n, :] for n in range(8)]
        b_h, b_t, b_y = banks[0:4], (banks[6], banks[4], banks[5]), (banks[7], banks[6])

        def turned(n):
            tiles = TURNS[n]
            bank = b_t[n][:, 0:len(tiles) * D].rearrange("p (r c t) -> p r c t", c=DC, t=P)
            return bank, slice(tiles[0] * P, (tiles[-1] + 1) * P)

        def columns(a, cols):
            return a[:, :, cols].rearrange("p c (r t) -> p r c t", t=P)

        def experts(engine, one):
            with engine.Fori(0, E0 - 1) as e:
                one(e, True)
            one(E0 - 1, False)

        @block.sync
        def _(sp):
            sp.sem_inc(y_stored.sem, 16)

            def load_rows(e):
                sp.dma_start(row[:], rows[bass.ds(e * CAP, CAP), :].rearrange("(r p) d -> p r d", p=P)).then_inc(rows_loaded.sem, 16)

            load_rows(0)
            load_next(sp)

            def one(e, more):
                if more:
                    sp.wait_ge(rT_made.sem, rT_made.at(e, len(TURNS)))
                    sp.sem_inc(sp_passed.sem, 1)
                    load_rows(e + 1)
                    sp.wait_ge(w1_low.sem, w1_low.at(e, 1))
                    sp.sem_inc(sp_passed.sem, 1)
                    raws.load_w1(sp, e + 1)
                    sp.wait_ge(w2_low.sem, w2_low.at(e, 1))
                    sp.sem_inc(sp_passed.sem, 1)
                    raws.load_w2(sp, e + 1)
                sp.wait_ge(y_ready.sem, y_ready.at(e, CT))
                sp.sem_inc(sp_passed.sem, 1)
                sp.dma_start(rows_out[bass.ds(e * CAP, CAP), :].rearrange("(r p) d -> p r d", p=P), y[:]).then_inc(y_stored.sem, 16)

            experts(sp, one)
            sp.wait_ge(y_stored.sem, y_stored.at(E0, 0))

        @block.scalar
        def _(act):
            h_relu.grant(act)
            act.wait_ge(biases_loaded.sem, biases_loaded.at(0, 32))

            def turn_rows(e):
                for n in range(len(TURNS)):
                    bank, cols = turned(n)
                    act.wait_ge(rT_made.sem, rT_made.at(e, n + 1))
                    act.activation(columns(rT.high, cols), bank, ACT.Copy).then_inc(rT_high.sem, 1)

            def split_w1(e):
                act.wait_ge(w1_loaded.sem, w1_loaded.at(e, 16))
                act.activation(w1.high[:], w1_raw[:], ACT.Copy).then_inc(w1_high.sem, 1)

            def one(e, more):
                act.wait_ge(b1_ready.sem, b1_ready.at(e, 1))
                for m in range(STEPS):
                    if m == 2:
                        act.wait_ge(w2_loaded.sem, w2_loaded.at(e, 16))
                        act.wait_ge(y_made.sem, y_made.at(e, 0))
                        act.activation(w2.high[:], w2_raw[:], ACT.Copy).then_inc(w2_high.sem, 1)
                    act.wait_ge(h_made.sem, h_made.at(e, m + 1))
                    act.wait_ge(h_ready.sem, h_ready.at(e, m - 3))
                    act.activation(relu[:, m % 4], b_h[m % 4][:, 0:HALF], ACT.Relu,
                                   bias=b1_now[:, m // 2:m // 2 + 1]).then_inc(h_relu.sem, 1)
                    if m % 2:
                        act.wait_ge(h_relu.sem, h_relu.at(e, m + 1))
                        act.wait_ge(y_made.sem, y_made.at(e, 0))
                        act.activation(h.high[:, m // 2, HALF:CAP], relu[:, m % 4], ACT.Copy).then_inc(h_high_act.sem, 1)
                if more:
                    turn_rows(e + 1)
                    split_w1(e + 1)

            split_w1(0)
            turn_rows(0)
            experts(act, one)

        @block.vector
        def _(dve):
            h_ready.grant(dve)
            y_ready.grant(dve)
            dve.wait_ge(biases_loaded.sem, biases_loaded.at(0, 32))

            def turn_rows(e):
                for n in range(len(TURNS)):
                    bank, cols = turned(n)
                    dve.wait_ge(rT_high.sem, rT_high.at(e, n + 1))
                    dve.tensor_tensor(columns(rT.low, cols), bank, columns(rT.high, cols).bitcast(F32), ALU.subtract).then_inc(rT_low.sem, 1)

            def split_w1(e):
                dve.wait_ge(w1_high.sem, w1_high.at(e, 1))
                dve.tensor_tensor(w1.low[:], w1_raw[:], w1.high_read, ALU.subtract).then_inc(w1_low.sem, 1)

            def one(e, more):
                dve.wait_ge(h_relu.sem, h_relu.at(e, 0))
                dve.tensor_scalar(b1_now[:], b1[:, bass.ds(e * FC, FC)], 1.0, None, ALU.mult).then_inc(b1_ready.sem, 1)
                for m in range(STEPS):
                    if m == 3:
                        dve.wait_ge(w2_high.sem, w2_high.at(e, 1))
                        dve.tensor_tensor(w2.low[:], w2_raw[:], w2.high_read, ALU.subtract).then_inc(w2_low.sem, 1)
                    f, part = m // 2, slice((m % 2) * HALF, (m % 2 + 1) * HALF)
                    dve.wait_ge(h_relu.sem, h_relu.at(e, m + 1))
                    if m == 0:
                        dve.wait_ge(y_made.sem, y_made.at(e, 0))
                    if m % 2:
                        dve.wait_ge(h_high_act.sem, h_high_act.at(e, f + 1))
                    else:
                        dve.tensor_copy(h.high[:, f, part], relu[:, m % 4]).then_inc(h_high_dve.sem, 1)
                        dve.wait_ge(h_high_dve.sem, h_high_dve.at(e, f + 1))
                    dve.tensor_tensor(h.low[:, f, part], relu[:, m % 4], h.high[:, f, part].bitcast(F32),
                                      ALU.subtract).then_inc(h_ready.sem, 1)
                if more:
                    turn_rows(e + 1)
                    split_w1(e + 1)
                dve.wait_ge(y_stored.sem, y_stored.at(e, 0))
                for r in range(CT):
                    dve.wait_ge(y_made.sem, y_made.at(e, r + 1))
                    dve.tensor_tensor(y[:, r, :], b_y[r % 2][:, 0:D], b2[:, bass.ds(e * D, D)], ALU.add).then_inc(y_ready.sem, 1)

            split_w1(0)
            turn_rows(0)
            experts(dve, one)

        @block.tensor
        def _(pe):
            y_made.grant(pe)

            def turn_rows(e):
                pe.wait_ge(rows_loaded.sem, rows_loaded.at(e, 16))
                for n, tiles in enumerate(TURNS):
                    for at, r in enumerate(tiles):
                        for c in range(DC):
                            last = pe.transpose(b_t[n][:, (at * DC + c) * P:(at * DC + c + 1) * P], row[:, r, c * P:(c + 1) * P], ident)
                    last.then_inc(rT_made.sem, 1)

            def one(e, more):
                pe.wait_ge(rT_low.sem, rT_low.at(e, len(TURNS)))
                pe.wait_ge(w1_low.sem, w1_low.at(e, 1))
                for m in range(STEPS):
                    f, part = m // 2, slice((m % 2) * HALF, (m % 2 + 1) * HALF)
                    if more and m == STEPS - 3:
                        pe.wait_ge(y_ready.sem, y_ready.at(e, 0))
                        turn_rows(e + 1)
                    pe.wait_ge(h_relu.sem, h_relu.at(e, m - 3))
                    product(pe, b_h[m % 4][:, 0:HALF], w1, rT, range(DC), lambda a, k: a[:, k, f * P:(f + 1) * P],
                            lambda a, k: a[:, k, part]).then_inc(h_made.sem, 1)
                pe.wait_ge(w2_low.sem, w2_low.at(e, 1))
                for r in range(CT):
                    pe.wait_ge(y_ready.sem, y_ready.at(e, r - 1))
                    if more and r == 1:
                        pe.wait_ge(rT_low.sem, rT_low.at(e + 1, 1))
                    for k in range(FC):
                        if r == 0:
                            pe.wait_ge(h_ready.sem, h_ready.at(e, 2 * k + 1))
                        if r == 2 and k == 0:
                            pe.wait_ge(h_ready.sem, h_ready.at(e, STEPS))
                        last = product(pe, b_y[r % 2][:, 0:D], h, w2, [k], lambda a, kk: a[:, kk, r * P:(r + 1) * P],
                                       lambda a, kk: a[:, kk, :], start=(k == 0), stop=(k == FC - 1))
                    last.then_inc(y_made.sem, 1)

            turn_rows(0)
            experts(pe, one)


class ChosenInputs:

    def __init__(self, sb, sems, io, x):
        self.io, self.x = io, x
        self.w = sb("c_w_raw", [P, W1TAB, DC, D])
        self.ids, self.bias, self.gate = sb("c_ids", [W1TAB, SEQS], I32), sb("c_bias_raw", [W1TAB, D]), sb("c_gate_raw", [P, DC, E1])
        self.w_loaded, self.small_loaded, self.x_loaded = (Signal(sems.new("c_" + n)) for n in ("w_loaded", "small_loaded", "x_loaded"))

    def load(self, sp):
        io = self.io
        sp.dma_start(self.w[:], io["L1_cond_W"].rearrange("w (c p) e -> p w c e", p=P)).then_inc(self.w_loaded.sem, 16)
        sp.dma_start(self.ids[:], io["itok_B_0_15"].partition_broadcast(W1TAB)).then_inc(self.small_loaded.sem, 16)
        sp.dma_start(self.bias[:], io["L1_cond_b"]).then_inc(self.small_loaded.sem, 16)
        sp.dma_start(self.gate[:], io["gate1"].rearrange("(c p) e -> p c e", p=P)).then_inc(self.small_loaded.sem, 16)
        sp.dma_start(self.x[:], io["x"].rearrange("(n p) d -> p n d", p=P)).then_inc(self.x_loaded.sem, 16)


def chosen_layer_phase(nc, sems, io, psum, consts, raws, slots, weights_eff, rows_out, x, xT, combineT, load_next):
    PAIRS, J = TILES // 2, 2
    with ExitStack() as ctx:
        def sb(name, shape, dt=F32):
            return ctx.enter_context(nc.sbuf_tensor("c_" + name, shape, dt))

        def sem(name):
            return sems.new("c_" + name)

        def sig(name, per=1, free=0):
            return Signal(sem(name), per, free)

        PIECE = 4
        PIECES = W1TAB // PIECE
        w = Split(sb, "w", [P, W1TAB, DC, D], low=raws.w)
        ids, w_loaded, small_loaded, x_loaded = raws.ids, raws.w_loaded, raws.small_loaded, raws.x_loaded
        bias_raw, bias = raws.bias, Split(sb, "bias", [W1TAB, D])
        gate_raw, gate = raws.gate, Split(sb, "gate", [P, DC, E1])
        ids_f = sb("ids_f", [W1TAB, SEQS])
        is_id = sb("is_id", [W1TAB, J, TSEQ, SEQ], F32R)
        sim = sb("sim", [P, 4, E1])
        got = sb("got", [P, TILES, 2, D])
        part = sb("part", [P, J, D])
        x_now = sb("x_now", [P, J, D])
        x_nowT = Split(sb, "x_nowT", [P, J, DC, P])
        c = sb("c", [P, J, D])
        cT = Split(sb, "cT", [P, J, DC, P])
        r_peak = sb("r_peak", [P, J])
        r_prob = sb("r_prob", [P, J, E1])
        r_sum = sb("r_sum", [P, J])
        top = sb("top", [P, J, K1])
        top_at = sb("top_at", [P, J, K1], U32)
        top_e = sb("top_e", [P, J, K1])
        t_sum = sb("t_sum", [P, J])
        route = sb("route", [P, J, K1])
        hot = sb("hot", [P, J, K1, E1])
        hotT = sb("hotT", [P, J, P])
        pairs = sb("pairs", [P, J, 4, PRIM1, E1])
        likeness = sb("likeness", [P, J, 4, PRIM1])
        best = sb("best", [P, J, 4])
        keep = sb("keep", [P, J, 4])
        stays = sb("stays", [P, J, 4])
        leaves = sb("leaves", [P, J, 4])
        first = sb("first", [P, J, 4, PRIM1])
        first_of = sb("first_of", [P, J, 4])
        more_w = sb("more_w", [P, J, PRIM1])
        spread_w = sb("spread_w", [P, J, K1, E1])
        comb = sb("comb", [P, 2 * J, E1])
        combT = sb("combT", [J * E1, P])

        sim_cleared = sig("sim_cleared")
        sim_loaded = sig("sim_loaded")
        sim_ready = sig("sim_ready")
        w_high = sig("w_high")
        w_low = sig("w_low")
        got_pair = [sem(f"got_pair{n}") for n in range(PAIRS)]
        small_ready = sig("small_ready")
        weighted, part_ready = sig("weighted"), sig("part_ready")
        x_ready = sig("x_ready", 1, 1)
        x_kept = sig("x_kept", 1, 1)
        xT_made = sig("xT_made", 1, 1)
        xT_high = sig("xT_high")
        xT_low = sig("xT_low", 1, 1)
        is_id_ready = sig("is_id_ready")
        c_made = sig("c_made", J, 2)
        c_ready = sig("c_ready", J, 2)
        cT_made = sig("cT_made", 1, 1)
        cT_high = sig("cT_high")
        cT_low = sig("cT_low", 1, 1)
        cT_kept = sig("cT_kept", 1, 1)
        logits_made = sig("logits_made", 1, 1)
        r_shifted = sig("r_shifted")
        r_exp = sig("r_exp")
        hot_ready = sig("hot_ready")
        hotT_made = sig("hotT_made")
        hotT_ready = sig("hotT_ready")
        sim_made = sig("sim_made")
        sim_read = sig("sim_read", 1, 1)
        comb_ready = sig("comb_ready")
        combT_made = sig("combT_made")
        combT_ready = sig("combT_ready", 1, 1)
        combT_stored = sig("combT_stored", 2 * 16, 16)
        steps = sig("steps")
        dve_passed, sp_passed = sig("dve_passed"), sig("sp_passed")
        block = ctx.enter_context(nc.Block())
        ident, count = const(consts, "ident"), const(consts, "count")
        banks = [psum[:, n, :] for n in range(8)]
        b_xT, b_cT, b_g, b_sim, b_hotT, b_combT = banks[4], banks[5], banks[6], banks[6][:, P:3 * P], banks[7], banks[7]

        def skewed(engine, step):
            step(-1, True, False, False)
            step(0, True, True, False)
            with engine.Fori(1, PAIRS - 1) as i:
                step(i, True, True, True)
            step(PAIRS - 1, False, True, True)
            step(PAIRS, False, False, True)

        @block.sync
        def _(sp):
            sp.sem_inc(combT_stored.sem, 16)
            sp.wait_ge(sim_cleared.sem, sim_cleared.at(0, 1))
            for n in range(4):
                sp.dma_start(sim[n * E1:(n + 1) * E1, n, :], io["L1_ffn_similarity"]).then_inc(sim_loaded.sem, 16)
            load_next(sp)

            def one(i, ahead, front, back):
                if back:
                    sp.wait_ge(combT_ready.sem, combT_ready.at(i, 0))
                    sp.sem_inc(sp_passed.sem, 1)
                    for j in range(J):
                        at = (i - 1) * (J * P) + j * P
                        sp.dma_start(combineT[:, bass.ds(at, P)], combT[j * E1:(j + 1) * E1, :]).then_inc(combT_stored.sem, 16)

            skewed(sp, one)
            sp.wait_ge(combT_stored.sem, combT_stored.at(PAIRS, 0))

        @block.gpsimd
        def _(pool):
            pool.memset(sim[:], 0.0).then_inc(sim_cleared.sem, 1)

            pool.sem_inc(x_ready.sem, x_ready.free)

            def combine(m):
                pool.wait_ge(got_pair[m], 4 * 16)
                now = slice(m * J, (m + 1) * J)
                pool.tensor_tensor(got[:, now], got[:, now], spread(weights_eff[:, now, :], 3, D), ALU.mult).then_inc(weighted.sem, 1)
                pool.wait_ge(weighted.sem, weighted.at(m, 1))
                pool.wait_ge(x_ready.sem, x_ready.at(m, 0))
                pool.tensor_tensor(part[:], got[:, now, 0, :], got[:, now, 1, :], ALU.add).then_inc(part_ready.sem, 1)
                pool.wait_ge(part_ready.sem, part_ready.at(m, 1))
                pool.wait_ge(xT_made.sem, xT_made.at(m, 0))
                pool.wait_ge(x_kept.sem, x_kept.at(m, 0))
                pool.tensor_tensor(x_now[:], x[:, now, :], part[:], ALU.add).then_inc(x_ready.sem, 1)

            for m in range(PAIRS):
                for n in (2 * m, 2 * m + 1):
                    for k in range(2):
                        pool.indirect_dma_start(got[:, n, k, :], None, rows_out,
                                                bass.IndirectOffsetOnAxis(ap=slots[:, n, k:k + 1], axis=0)).then_inc(got_pair[m], 16)
                if m == 0:
                    pool.wait_ge(sim_loaded.sem, sim_loaded.at(0, 64))
                    flat = sim[:].rearrange("p k e -> p (k e)")
                    pool.affine_select(out=flat, in_=flat, compare_op=ALU.not_equal, fill=1.0, base=0,
                                       pattern=[[-1, P]], channel_multiplier=1).then_inc(sim_ready.sem, 1)
                    pool.wait_ge(x_loaded.sem, x_loaded.at(0, 16))
                combine(m)

        @block.scalar
        def _(act):
            for made in (x_kept, c_ready, cT_kept, combT_ready):
                made.grant(act)
            act.wait_ge(small_loaded.sem, small_loaded.at(0, 48))
            act.activation(bias.high[:], bias_raw[:], ACT.Copy).then_inc(small_ready.sem, 1)
            act.activation(gate.high[:], gate_raw[:], ACT.Copy).then_inc(small_ready.sem, 1)
            act.wait_ge(w_loaded.sem, w_loaded.at(0, 16))
            for n in range(PIECES):
                act.activation(w.high[:, n * PIECE:(n + 1) * PIECE], raws.w[:, n * PIECE:(n + 1) * PIECE], ACT.Copy).then_inc(w_high.sem, 1)

            def one(i, ahead, front, back):
                if back:
                    act.wait_ge(r_shifted.sem, r_shifted.at(i - 1, 1))
                    act.activation(r_prob[:], r_prob[:], ACT.Exp).then_inc(r_exp.sem, 1)

                def take(j):
                    act.wait_ge(c_made.sem, c_made.at(i, j + 1))
                    act.wait_ge(cT_made.sem, cT_made.at(i, 0))
                    for b in range(TSEQ):
                        quad = slice(b * SEQ, (b + 1) * SEQ)
                        last = act.activation(c[quad, j, :], banks[2 * j + b // 2][quad, (b % 2) * D:(b % 2 + 1) * D], ACT.Copy)
                    last.then_inc(c_ready.sem, 1)

                if back:
                    act.wait_ge(hotT_made.sem, hotT_made.at(i - 1, 1))
                    act.activation(hotT[:].rearrange("p j t -> p (j t)"), b_hotT[:, 0:J * P], ACT.Copy).then_inc(hotT_ready.sem, 1)
                if front:
                    take(0)
                    take(1)
                if ahead:
                    act.wait_ge(xT_made.sem, xT_made.at(i + 1, 1))
                    act.activation(x_nowT.high[:].rearrange("p j c t -> p (j c t)"), b_xT, ACT.Copy).then_inc(xT_high.sem, 1)
                    act.activation(x[:, bass.ds((i + 1) * J, J), :], x_now[:], ACT.Copy).then_inc(x_kept.sem, 1)
                if front:
                    act.wait_ge(cT_made.sem, cT_made.at(i, 1))
                    act.wait_ge(logits_made.sem, logits_made.at(i, 0))
                    act.wait_ge(cT_kept.sem, cT_kept.at(i, 0))
                    act.activation(cT.high[:].rearrange("p j c t -> p (j c t)"), b_cT, ACT.Copy).then_inc(cT_high.sem, 1)
                if back:
                    act.wait_ge(combT_made.sem, combT_made.at(i - 1, 1))
                    act.wait_ge(combT_stored.sem, combT_stored.at(i - 1, 0))
                    act.activation(combT[:], b_combT[0:J * E1, 0:P], ACT.Copy).then_inc(combT_ready.sem, 1)
                if front:
                    act.wait_ge(cT_low.sem, cT_low.at(i, 1))
                    for half in ("high", "low"):
                        src = (cT.high, cT.low)[half == "low"]
                        dst = (xT.high, xT.low)[half == "low"]
                        last = act.activation(dst[:, :, bass.ds(i * J * P, J * P)].rearrange("p c (j t) -> p j c t", j=J).bitcast(F32R),
                                              src[:].bitcast(F32), ACT.Copy)
                    last.then_inc(cT_kept.sem, 1)

            skewed(act, one)

        @block.vector
        def _(dve):
            chain = Chain(dve, steps.sem, 25)
            sim_read.grant(dve)
            cT_low.grant(dve)
            xT_low.grant(dve)
            dve.memset(comb[:], 0.0).then_inc(small_ready.sem, 1)
            dve.wait_ge(small_ready.sem, small_ready.at(0, 3))
            dve.tensor_tensor(bias.low[:], bias_raw[:], bias.high_read, ALU.subtract).then_inc(small_ready.sem, 1)
            dve.tensor_tensor(gate.low[:], gate_raw[:], gate.high_read, ALU.subtract).then_inc(small_ready.sem, 1)
            dve.tensor_copy(ids_f[:], ids[:]).then_inc(small_ready.sem, 1)
            for n in range(PIECES):
                dve.wait_ge(w_high.sem, w_high.at(0, n + 1))
                dve.tensor_tensor(w.low[:, n * PIECE:(n + 1) * PIECE], raws.w[:, n * PIECE:(n + 1) * PIECE],
                                  w.high[:, n * PIECE:(n + 1) * PIECE].bitcast(F32), ALU.subtract).then_inc(w_low.sem, 1)
            dve.wait_ge(small_ready.sem, small_ready.at(0, 6))

            def select(i):
                dve.wait_ge(c_made.sem, c_made.at(i, 0))
                dve.tensor_scalar(is_id[:], spread(ids_f[:, bass.ds(i * J * TSEQ, J * TSEQ)].rearrange("p (j b) -> p j b", j=J), 3, SEQ),
                                  consts[0:W1TAB, CONST["position"][0]:CONST["position"][1]], None, ALU.is_equal).then_inc(is_id_ready.sem, 1)

            def low(dst, bank):
                return dve.tensor_tensor(dst.low[:].rearrange("p j c t -> p (j c t)"), bank,
                                         dst.high[:].rearrange("p j c t -> p (j c t)").bitcast(F32), ALU.subtract)

            def choose(i):
                logits = b_g[:, 0:J * E1].rearrange("p (j e) -> p j e", e=E1)
                chain.start(i)
                dve.wait_ge(logits_made.sem, logits_made.at(i, 1))
                dve.tensor_reduce(r_peak[:], logits, AX, ALU.max).then_inc(chain.next(), 1)
                dve.wait_ge(chain.sem, chain.count())
                dve.tensor_tensor(r_prob[:], logits, spread(r_peak[:], 2, E1), ALU.subtract).then_inc(r_shifted.sem, 1)
                dve.wait_ge(r_exp.sem, r_exp.at(i, 1))
                dve.tensor_reduce(r_sum[:], r_prob[:], AX, ALU.add).then_inc(chain.next(), 1)
                dve.wait_ge(chain.sem, chain.count())
                dve.reciprocal(r_sum[:], r_sum[:]).then_inc(chain.next(), 1)
                dve.wait_ge(chain.sem, chain.count())
                dve.tensor_tensor(r_prob[:], r_prob[:], spread(r_sum[:], 2, E1), ALU.mult).then_inc(chain.next(), 1)
                dve.wait_ge(chain.sem, chain.count())
                dve.sem_inc(dve_passed.sem, 1)
                for j in range(J):
                    last = dve.max(top[:, j, :], r_prob[:, j, :])
                last.then_inc(chain.next(), 1)
                dve.wait_ge(chain.sem, chain.count())
                dve.sem_inc(dve_passed.sem, 1)
                for j in range(J):
                    last = dve.max_index(top_at[:, j, :], top[:, j, :], r_prob[:, j, :])
                last.then_inc(chain.next(), 1)
                dve.wait_ge(chain.sem, chain.count())
                dve.tensor_copy(top_e[:], top_at[:]).then_inc(chain.next(), 1)
                dve.tensor_reduce(t_sum[:], top[:], AX, ALU.add).then_inc(chain.next(), 1)
                dve.wait_ge(chain.sem, chain.count())
                dve.tensor_scalar(t_sum[:], t_sum[:], 1e-12, None, ALU.max).then_inc(chain.next(), 1)
                dve.tensor_tensor(hot[:].rearrange("p j k e -> p (j k) e"), spread(count, 1, J * K1),
                                  spread(top_e[:].rearrange("p j k -> p (j k)"), 2, E1), ALU.is_equal).then_inc(hot_ready.sem, 1)
                dve.wait_ge(chain.sem, chain.count())
                dve.reciprocal(t_sum[:], t_sum[:]).then_inc(chain.next(), 1)
                dve.wait_ge(chain.sem, chain.count())
                dve.tensor_tensor(route[:], top[:], spread(t_sum[:], 2, K1), ALU.mult).then_inc(chain.next(), 1)

            def likenesses(i):
                dve.wait_ge(sim_made.sem, sim_made.at(i, 1))
                dve.wait_ge(hot_ready.sem, hot_ready.at(i, 1))
                for j in range(J):
                    last = dve.tensor_tensor(pairs[:, j], spread(b_sim[:, j * P:(j + 1) * P].rearrange("p (k e) -> p k e", e=E1), 2, PRIM1),
                                             spread(hot[:, j, 0:PRIM1, :], 1, 4), ALU.mult)
                last.then_inc(sim_read.sem, 1)
                dve.wait_ge(sim_read.sem, sim_read.at(i, 1))
                dve.tensor_reduce(likeness[:].rearrange("p j s m -> p (j s m)"),
                                            pairs[:].rearrange("p j s m e -> p (j s m) e"), AX, ALU.add).then_inc(chain.next(), 1)

            def reroute(i):
                dve.wait_ge(chain.sem, chain.count())
                dve.tensor_reduce(best[:], likeness[:], AX, ALU.max).then_inc(chain.next(), 1)
                dve.wait_ge(chain.sem, chain.count())
                dve.tensor_scalar(keep[:], best[:], 0.5, None, ALU.is_lt).then_inc(chain.next(), 1)
                dve.tensor_tensor(first[:].rearrange("p j s m -> p (j s) m"), likeness[:].rearrange("p j s m -> p (j s) m"),
                                            spread(best[:].rearrange("p j s -> p (j s)"), 2, PRIM1), ALU.is_equal).then_inc(chain.next(), 1)
                dve.wait_ge(chain.sem, chain.count())
                dve.scalar_tensor_tensor(first[:].rearrange("p j s m -> p (j s) m"),
                                                   spread(count[:, 0:PRIM1], 1, J * 4), -8.0,
                                                   first[:].rearrange("p j s m -> p (j s) m"), ALU.add, ALU.mult).then_inc(chain.next(), 1)
                dve.tensor_tensor(stays[:], route[:, :, PRIM1:K1], keep[:], ALU.mult).then_inc(chain.next(), 1)
                dve.wait_ge(chain.sem, chain.count())
                dve.tensor_reduce(first_of[:], first[:], AX, ALU.min).then_inc(chain.next(), 1)
                dve.wait_ge(chain.sem, chain.count())
                dve.tensor_tensor(first[:].rearrange("p j s m -> p (j s) m"), first[:].rearrange("p j s m -> p (j s) m"),
                                            spread(first_of[:].rearrange("p j s -> p (j s)"), 2, PRIM1), ALU.is_equal).then_inc(chain.next(), 1)
                dve.tensor_tensor(leaves[:], route[:, :, PRIM1:K1], stays[:], ALU.subtract).then_inc(chain.next(), 1)
                dve.wait_ge(chain.sem, chain.count())
                dve.tensor_copy(route[:, :, PRIM1:K1], stays[:]).then_inc(chain.next(), 1)
                dve.tensor_tensor(first[:].rearrange("p j s m -> p (j s) m"), first[:].rearrange("p j s m -> p (j s) m"),
                                            spread(leaves[:].rearrange("p j s -> p (j s)"), 2, PRIM1), ALU.mult).then_inc(chain.next(), 1)
                dve.wait_ge(chain.sem, chain.count())
                dve.tensor_reduce(more_w[:], first[:].rearrange("p j s m -> p j m s"), AX, ALU.add).then_inc(chain.next(), 1)
                dve.wait_ge(chain.sem, chain.count())
                dve.tensor_tensor(route[:, :, 0:PRIM1], route[:, :, 0:PRIM1], more_w[:], ALU.add).then_inc(chain.next(), 1)
                dve.wait_ge(chain.sem, chain.count())
                dve.tensor_tensor(spread_w[:].rearrange("p j k e -> p (j k) e"), hot[:].rearrange("p j k e -> p (j k) e"),
                                            spread(route[:].rearrange("p j k -> p (j k)"), 2, E1), ALU.mult).then_inc(chain.next(), 1)
                dve.wait_ge(chain.sem, chain.count())
                dve.tensor_reduce(comb[:, 0:J, :], spread_w[:].rearrange("p j k e -> p j e k"), AX, ALU.add).then_inc(comb_ready.sem, 1)
                dve.wait_ge(comb_ready.sem, comb_ready.at(i, 1))
                chain.end()

            def one(i, ahead, front, back):
                if back:
                    choose(i - 1)
                    likenesses(i - 1)
                    reroute(i - 1)
                if ahead:
                    dve.wait_ge(xT_high.sem, xT_high.at(i + 1, 1))
                    low(x_nowT, b_xT).then_inc(xT_low.sem, 1)
                    select(i + 1)
                if front:
                    dve.wait_ge(cT_high.sem, cT_high.at(i, 1))
                    low(cT, b_cT).then_inc(cT_low.sem, 1)

            skewed(dve, one)

        @block.tensor
        def _(pe):
            for made in (xT_made, c_made, cT_made, logits_made):
                made.grant(pe)
            pe.wait_ge(small_ready.sem, small_ready.at(0, 6))
            pe.wait_ge(w_low.sem, w_low.at(0, PIECES))
            pe.wait_ge(sim_ready.sem, sim_ready.at(0, 1))

            def turn_x(i):
                pe.wait_ge(x_ready.sem, x_ready.at(i, 1))
                pe.wait_ge(xT_low.sem, xT_low.at(i, 0))
                for j in range(J):
                    for k in range(DC):
                        last = pe.transpose(b_xT[:, (j * DC + k) * P:(j * DC + k + 1) * P], x_now[:, j, k * P:(k + 1) * P], ident)
                last.then_inc(xT_made.sem, 1)

            def chosen_by(i, j, b):
                return pe.value_load(ids[0:1, bass.ds(i * J * TSEQ + j * TSEQ + b, 1)], min_val=0, max_val=W1TAB - 1)

            def layer(i, j, own=None):
                pe.wait_ge(xT_low.sem, xT_low.at(i, 1))
                pe.wait_ge(is_id_ready.sem, is_id_ready.at(i, 1))
                pe.wait_ge(c_ready.sem, c_ready.at(i, j - 1))
                for pair in range(2):
                    out = banks[2 * j + pair]
                    which = is_id[:, j].rearrange("p b t -> p (b t)")
                    for n, half in enumerate((bias.high, bias.low)):
                        pe.matmul(out, which, spread(half[:], 1, 2), start=(n == 0), stop=False, skip_group_check=True)
                    for b in (2 * pair, 2 * pair + 1):
                        w_at = own[b] if own else chosen_by(i, j, b)
                        last = product(pe, out[:, (b % 2) * D:(b % 2 + 1) * D], x_nowT, w, range(DC), lambda a, k: a[:, j, k, :],
                                       lambda a, k: a[:, bass.ds(w_at, 1), k, :].rearrange("p o e -> p (o e)"), start=False)
                last.then_inc(c_made.sem, 1)

            def one(i, ahead, front, back):
                if front:
                    layer(i, 0)
                    own = [chosen_by(i, 1, b) for b in range(TSEQ)]
                if back:
                    pe.wait_ge(hot_ready.sem, hot_ready.at(i - 1, 1))
                    pe.wait_ge(combT_ready.sem, combT_ready.at(i - 1, 0))
                    for j in range(J):
                        last = pe.transpose(b_hotT[:, j * P:(j + 1) * P], hot[:, j, PRIM1:K1, :].rearrange("p k e -> p (k e)"), ident)
                    last.then_inc(hotT_made.sem, 1)
                if ahead:
                    turn_x(i + 1)
                if back:
                    pe.wait_ge(hotT_ready.sem, hotT_ready.at(i - 1, 1))
                    for j in range(J):
                        last = pe.matmul(b_sim[:, j * P:(j + 1) * P], hotT[:, j, :], sim[:].rearrange("p k e -> p (k e)"),
                                         start=True, stop=True, skip_group_check=True)
                    last.then_inc(sim_made.sem, 1)
                if front:
                    layer(i, 1, own)
                if front:
                    pe.wait_ge(c_ready.sem, c_ready.at(i, J))
                    pe.wait_ge(cT_low.sem, cT_low.at(i, 0))
                    for j in range(J):
                        for k in range(DC):
                            last = pe.transpose(b_cT[:, (j * DC + k) * P:(j * DC + k + 1) * P], c[:, j, k * P:(k + 1) * P], ident)
                    last.then_inc(cT_made.sem, 1)
                if back:
                    pe.wait_ge(comb_ready.sem, comb_ready.at(i - 1, 1))
                    pe.transpose(b_combT[:, 0:P], comb[:].rearrange("p j e -> p (j e)"), ident).then_inc(combT_made.sem, 1)
                if front:
                    pe.wait_ge(cT_low.sem, cT_low.at(i, 1))
                    pe.wait_ge(sim_read.sem, sim_read.at(i, 0))
                    for j in range(J):
                        last = product(pe, b_g[:, j * E1:(j + 1) * E1], cT, gate, range(DC), lambda a, k: a[:, j, k, :],
                                       lambda a, k: a[:, k, :])
                    last.then_inc(logits_made.sem, 1)

            skewed(pe, one)


class ExpertWeights:

    def __init__(self, sb, sems, name, gate_w, up_w, down_w, chunks):
        self.gate_w, self.up_w, self.down_w, self.chunks = gate_w, up_w, down_w, chunks
        self.gu = sb(name + "_gu_raw", [P, chunks, 2, DC, P])
        self.down = sb(name + "_down_raw", [P, chunks, D])
        self.gu_loaded = [Signal(sems.new(f"{name}_gu_loaded{c}"), 32) for c in range(chunks)]
        self.down_loaded = Signal(sems.new(name + "_down_loaded"), 16)

    def load_gate_up(self, sp, g, c):
        for n, w in enumerate((self.gate_w, self.up_w)):
            src = w[:, bass.ds((g * self.chunks + c) * P, P)].rearrange("(k p) f -> p k f", p=P)
            sp.dma_start(self.gu[:, c, n], src).then_inc(self.gu_loaded[c].sem, 16)

    def load_down(self, sp, g):
        src = self.down_w[bass.ds(g * (self.chunks * P), self.chunks * P), :].rearrange("(c p) d -> p c d", p=P)
        sp.dma_start(self.down[:], src).then_inc(self.down_loaded.sem, 16)

    def load(self, sp):
        for c in range(self.chunks):
            self.load_gate_up(sp, 0, c)
        self.load_down(sp, 0)


def gated_experts_phase(nc, sems, name, psum, raws, combineT, width, experts, x, xT, load_next=None, out=None):
    chunks, gu_loaded, down_loaded = raws.chunks, raws.gu_loaded, raws.down_loaded
    gu_raw, down_raw = raws.gu, raws.down
    group = chunks * P // width
    GROUPS = experts // group
    STEPS = BLOCKS * chunks
    with ExitStack() as ctx:
        def sb(n, shape, dt=F32):
            return ctx.enter_context(nc.sbuf_tensor(f"{name}_{n}", shape, dt))

        def sig(n, per=1, free=0):
            return Signal(sems.new(f"{name}_{n}"), per, free)

        gu, down = Split(sb, "gu", [P, chunks, 2, DC, P]), Split(sb, "down", [P, chunks, D])
        weight = sb("weight", [P, chunks, T])
        silu = sb("silu", [P, 2, BLOCK])
        prod = sb("prod", [P, 2, BLOCK])
        hw = sb("hw", [P, 2, BLOCK])
        h = Split(sb, "h", [P, 2, chunks, BLOCK])

        weight_loaded = [[sig(f"weight_loaded{c}_{half}", 16 * len(pieces(c, width))) for half in range(2)] for c in range(chunks)]
        gu_high, gu_low = sig("gu_high", chunks), sig("gu_low", chunks)
        down_high, down_low = sig("down_high"), sig("down_low")
        gu_made = sig("gu_made", STEPS)
        silu_ready = sig("silu_ready", STEPS)
        prod_ready = sig("prod_ready", STEPS, 2)
        hw_ready = sig("hw_ready", STEPS, 2)
        h_high = sig("h_high", STEPS)
        h_low = sig("h_low", STEPS, 2)
        y_made = sig("y_made", BLOCKS, 2)
        y_added = sig("y_added", BLOCKS, 2)
        sp_passed = sig("sp_passed")
        stored = sig("stored")
        block = ctx.enter_context(nc.Block())
        banks = [psum[:, n, :] for n in range(8)]

        def groups(engine, one):
            one(0, False, True)
            with engine.Fori(1, GROUPS - 1) as g:
                one(g, True, True)
            one(GROUPS - 1, True, False)

        @block.sync
        def _(sp):
            def load_weight(g, c, half):
                cols = slice(half * T // 2, (half + 1) * T // 2)
                for a, b, e in pieces(c, width):
                    src = combineT[bass.ds(g * group + e, 1), cols].rearrange("o t -> (o t)").partition_broadcast(b - a)
                    sp.dma_start(weight[a:b, c, cols], src).then_inc(weight_loaded[c][half].sem, 16)

            for half in range(2):
                for c in range(chunks):
                    load_weight(0, c, half)
            if load_next:
                load_next(sp)

            def one(g, before, more):
                if more:
                    for c in range(chunks):
                        sp.wait_ge(gu_low.sem, gu_low.at(g, c + 1))
                        sp.sem_inc(sp_passed.sem, 1)
                        raws.load_gate_up(sp, g + 1, c)
                    sp.wait_ge(down_low.sem, down_low.at(g, 1))
                    sp.sem_inc(sp_passed.sem, 1)
                    raws.load_down(sp, g + 1)
                    for half in range(2):
                        for c in range(chunks):
                            last = (half + 1) * BLOCKS // 2 - 1
                            sp.wait_ge(hw_ready.sem, hw_ready.at(g, last * chunks + c + 1))
                            sp.sem_inc(sp_passed.sem, 1)
                            load_weight(g + 1, c, half)
                elif out is not None:
                    for b in range(BLOCKS):
                        sp.wait_ge(y_added.sem, y_added.at(g, b + 1))
                        tiles = slice(b * BTILES, (b + 1) * BTILES)
                        sp.dma_start(out.rearrange("(n p) d -> p n d", p=P)[:, tiles, :], x[:, tiles, :]).then_inc(stored.sem, 16)
                    sp.wait_ge(stored.sem, stored.at(0, 16 * BLOCKS))

            groups(sp, one)

        @block.gpsimd
        def _(pool):
            hw_ready.grant(pool)

            def one(g, before, more):
                for m in range(STEPS):
                    b, c = divmod(m, chunks)
                    if b % (BLOCKS // 2) == 0:
                        loaded = weight_loaded[c][b // (BLOCKS // 2)]
                        pool.wait_ge(loaded.sem, loaded.at(g, loaded.per))
                    pool.wait_ge(prod_ready.sem, prod_ready.at(g, m + 1))
                    pool.wait_ge(h_low.sem, h_low.at(g, m - 1))
                    pool.tensor_tensor(hw[:, m % 2], prod[:, m % 2], weight[:, c, b * BLOCK:(b + 1) * BLOCK],
                                       ALU.mult).then_inc(hw_ready.sem, 1)

            groups(pool, one)

        @block.scalar
        def _(act):
            def split_gu(g, c):
                act.wait_ge(gu_loaded[c].sem, gu_loaded[c].at(g, 32))
                act.activation(gu.high[:, c], gu_raw[:, c], ACT.Copy).then_inc(gu_high.sem, 1)

            for c in range(chunks):
                split_gu(0, c)

            def one(g, before, more):
                for m in range(STEPS):
                    b, c = divmod(m, chunks)
                    act.wait_ge(gu_made.sem, gu_made.at(g, m + 1))
                    act.wait_ge(prod_ready.sem, prod_ready.at(g, m - 1))
                    act.activation(silu[:, m % 2], banks[m % 2], ACT.Silu).then_inc(silu_ready.sem, 1)
                    if m == chunks:
                        act.wait_ge(down_loaded.sem, down_loaded.at(g, 16))
                        act.wait_ge(y_made.sem, y_made.at(g, 0))
                        act.activation(down.high[:], down_raw[:], ACT.Copy).then_inc(down_high.sem, 1)
                    if more and b == BLOCKS - 1:
                        split_gu(g + 1, c)
                    act.wait_ge(hw_ready.sem, hw_ready.at(g, m + 1))
                    act.wait_ge(y_made.sem, y_made.at(g, b - 1))
                    act.activation(h.high[:, b % 2, c], hw[:, m % 2], ACT.Copy).then_inc(h_high.sem, 1)

            groups(act, one)

        @block.vector
        def _(dve):
            for made in (prod_ready, h_low, y_added):
                made.grant(dve)

            def split_gu(g, c):
                dve.wait_ge(gu_high.sem, gu_high.at(g, c + 1))
                dve.tensor_tensor(gu.low[:, c], gu_raw[:, c], gu.high[:, c].bitcast(F32), ALU.subtract).then_inc(gu_low.sem, 1)

            for c in range(chunks):
                split_gu(0, c)

            def add(g, b):
                dve.wait_ge(y_made.sem, y_made.at(g, b + 1))
                dve.wait_ge(y_added.sem, y_added.at(g, b))
                for half in range(2):
                    out = x[:, b * BTILES + 2 * half:b * BTILES + 2 * half + 2, :].rearrange("p n d -> p (n d)")
                    last = dve.tensor_tensor(out, banks[4 + 2 * (b % 2) + half], out, ALU.add)
                last.then_inc(y_added.sem, 1)

            def one(g, before, more):
                for m in range(STEPS):
                    b, c = divmod(m, chunks)
                    dve.wait_ge(silu_ready.sem, silu_ready.at(g, m + 1))
                    dve.wait_ge(hw_ready.sem, hw_ready.at(g, m - 1))
                    dve.tensor_tensor(prod[:, m % 2], banks[2 + m % 2], silu[:, m % 2], ALU.mult).then_inc(prod_ready.sem, 1)
                    if m == chunks:
                        dve.wait_ge(down_high.sem, down_high.at(g, 1))
                        dve.tensor_tensor(down.low[:], down_raw[:], down.high_read, ALU.subtract).then_inc(down_low.sem, 1)
                    if more and b == BLOCKS - 1:
                        split_gu(g + 1, c)
                    dve.wait_ge(h_high.sem, h_high.at(g, m + 1))
                    dve.tensor_tensor(h.low[:, b % 2, c], hw[:, m % 2], h.high[:, b % 2, c].bitcast(F32),
                                      ALU.subtract).then_inc(h_low.sem, 1)
                    if c == chunks - 1:
                        if b > 0:
                            add(g, b - 1)
                        elif before:
                            add(g - 1, BLOCKS - 1)
                if not more:
                    add(g, BLOCKS - 1)

            groups(dve, one)

        @block.tensor
        def _(pe):
            y_made.grant(pe)

            def hidden(g, b, c):
                m = b * chunks + c
                if b == 0:
                    pe.wait_ge(gu_low.sem, gu_low.at(g, c + 1))
                pe.wait_ge(prod_ready.sem, prod_ready.at(g, m - 1))
                for n in range(2):
                    last = product(pe, banks[2 * n + m % 2], gu, xT, range(DC), lambda a, k: a[:, c, n, k, :],
                                   lambda a, k: a[:, k, b * BLOCK:(b + 1) * BLOCK])
                last.then_inc(gu_made.sem, 1)

            def result(g, b):
                if b == 0:
                    pe.wait_ge(down_low.sem, down_low.at(g, 1))
                pe.wait_ge(y_added.sem, y_added.at(g, b - 1))
                for c in range(chunks):
                    pe.wait_ge(h_low.sem, h_low.at(g, b * chunks + c + 1))
                    for r in range(BTILES):
                        last = product(pe, banks[4 + 2 * (b % 2) + r // 2][:, (r % 2) * D:(r % 2 + 1) * D], h, down, [c],
                                       lambda a, k: a[:, b % 2, k, r * P:(r + 1) * P], lambda a, k: a[:, k, :],
                                       start=(c == 0 and r % 2 == 0), stop=(c == chunks - 1))
                last.then_inc(y_made.sem, 1)

            def one(g, before, more):
                for b in range(BLOCKS):
                    for c in range(chunks):
                        hidden(g, b, c)
                    if b > 0:
                        result(g, b - 1)
                    elif before:
                        result(g - 1, BLOCKS - 1)
                if not more:
                    result(g, BLOCKS - 1)

            groups(pe, one)


def pieces(c, width):
    out, at = [], c * P
    while at < (c + 1) * P:
        e = at // width
        end = min((e + 1) * width, (c + 1) * P)
        out.append((at - c * P, end - c * P, e))
        at = end
    return out


class QuantisedInputs:

    def __init__(self, sb, sems, io):
        self.io = io
        self.cond, self.down, self.up = sb("q_cond_raw", [P, DC, D]), sb("q_down_raw", [P, DC, P]), sb("q_up_raw", [P, 1, D])
        self.ids, self.scaling = sb("q_ids", [P, SEQS], I32), sb("q_scaling", [P, 1])
        self.g1, self.g2 = sb("q_g1", [P, D]), sb("q_g2", [P, F2])
        self.w1, self.w2 = sb("q_w1_raw", [P, DC, F2]), sb("q_w2_raw", [P, F2 // P, D])
        self.loaded = Signal(sems.new("q_loaded"))
        self.all_loaded = 16 * (8 + A2)

    def load(self, sp):
        def load(dst, src):
            sp.dma_start(dst, src).then_inc(self.loaded.sem, 16)

        io = self.io
        load(self.cond[:], io["cond2"].rearrange("(c p) e -> p c e", p=P))
        load(self.down[:], io["adapter_down"].rearrange("(c p) r -> p c r", p=P))
        load(self.up[:, 0, :], io["adapter_up"])
        load(self.w1[:], io["quant_w1"].rearrange("(c p) f -> p c f", p=P))
        load(self.w2[:], io["quant_w2"].rearrange("(c p) d -> p c d", p=P))
        load(self.ids[:], io["itok_B_0_6"].partition_broadcast(P))
        load(self.g1[:], io["L2_ffn_g1"].partition_broadcast(P))
        load(self.g2[:], io["L2_ffn_g2"].partition_broadcast(P))
        for a in range(A2):
            load(self.scaling[a * R2:(a + 1) * R2, :], io["L2_cond_scalings"][a:a + 1].partition_broadcast(R2))


def quantised_phase(nc, sems, psum, consts, raws, x):
    FC, J = F2 // P, BTILES
    with ExitStack() as ctx:
        def sb(name, shape, dt=F32):
            return ctx.enter_context(nc.sbuf_tensor("q_" + name, shape, dt))

        def sig(name, per=1, free=0):
            return Signal(sems.new("q_" + name), per, free)

        loaded, g1, g2, w1_raw, w2_raw = raws.loaded, raws.g1, raws.g2, raws.w1, raws.w2
        cond = Split(sb, "cond", [P, DC, D])
        down = Split(sb, "down", [P, DC, P])
        up = Split(sb, "up", [P, 1, D])
        ids_f = sb("ids_f", [P, SEQS])
        own = sb("own", [P, SEQS])
        w1_q = sb("w1_q", [P, DC, F2], BF16)
        w2_q = sb("w2_q", [P, FC, D], BF16)
        w_abs = sb("w_abs", [P, 2])
        w_mean = sb("w_mean", [P, 2])
        w_scale = sb("w_scale", [P, 2])
        magic = sb("magic", [P, 1])
        magic_off = sb("magic_off", [P, 1])
        eps = sb("eps", [P, 1])
        x_now = sb("x_now", [P, J, D])
        x_T = Split(sb, "x_T", [P, J, DC, P])
        low_rank = sb("low_rank", [P, BLOCK])
        lr = Split(sb, "lr", [P, 1, BLOCK])
        c = sb("c", [P, J, D])
        v = sb("v", [P, J, D])
        q1 = sb("q1", [P, J, DC, P], BF16)
        square = sb("square", [P, 2, F2])
        square1 = sb("square1", [P, J, D])
        r = sb("r", [P, 2, F2])
        r2 = sb("r2", [P, 2, F2])
        v2 = sb("v2", [P, J, F2])
        t2 = sb("t2", [P, 2, F2])
        q2 = sb("q2", [P, 2, FC, P], BF16)
        sums, rms, inv, peak, to_q, back = (sb(n, [P, 2, J]) for n in ("sums", "rms", "inv", "peak", "to_q", "back"))

        constants_set = sig("constants_set")
        split_high, split_low = sig("split_high"), sig("split_low")
        own_ready = sig("own_ready")
        abs_ready = sig("abs_ready")
        w_scale_ready = sig("w_scale_ready")
        w_scaled, w_clipped, w_ready = sig("w_scaled"), sig("w_clipped"), sig("w_ready")
        abs_summed = sig("abs_summed")
        x_copied = sig("x_copied")
        xT_made = sig("xT_made", 2, 1)
        xT_high = sig("xT_high", 2)
        xT_low = sig("xT_low", 2)
        lr_made = sig("lr_made")
        lr_masked = sig("lr_masked")
        lr_high = sig("lr_high")
        lr_low = sig("lr_low")
        c_made = sig("c_made", 2, 1)
        c_copied = sig("c_copied", 2)
        v_ready = sig("v_ready", 2)
        rms_ready = sig("rms_ready", 2)
        sqrt1, sqrt2 = sig("sqrt1"), sig("sqrt2")
        back1_ready, back2_ready = sig("back1_ready"), sig("back2_ready")
        t_ready = sig("t_ready")
        t_made = sig("t_made", 2)
        q1_ready = sig("q1_ready", 2, 2)
        h_made = sig("h_made", J, 1)
        r_ready = sig("r_ready", J, 2)
        r2_ready = sig("r2_ready", J, 2)
        v2_ready = sig("v2_ready", J, 2)
        sums2_ready = sig("sums2_ready", J, 2)
        to_q2_ready = sig("to_q2_ready")
        t2_ready = sig("t2_ready", J, 1)
        t2_clipped = sig("t2_clipped", J)
        t2_made = sig("t2_made", J, 2)
        q2_act = sig("q2_act", J, 2)
        q2_dve = sig("q2_dve", J, 2)
        y_made = sig("y_made", J, 2)
        y_added = sig("y_added", J, J + 1)
        steps1, steps2 = sig("steps1"), sig("steps2")
        block = ctx.enter_context(nc.Block())
        ident = const(consts, "ident")
        banks = [psum[:, n, :] for n in range(8)]
        b_lr, b_c = banks[2], banks[3]
        b_abs = banks[4][:, 0:2]
        b_y = (banks[2], banks[3])

        def b_h(j):
            first = 4 + 2 * (j % 2)
            return psum[:, first:first + 2, :].rearrange("p n f -> p (n f)")

        def b_t2(j, half):
            return banks[4 + 2 * (j % 2) + half]

        def skewed(engine, step):
            step(-1, True, False)
            with engine.Fori(0, BLOCKS - 1) as i:
                step(i, True, True)
            step(BLOCKS - 1, False, True)

        @block.gpsimd
        def _(pool):
            v2_ready.grant(pool)
            pool.wait_ge(loaded.sem, loaded.at(0, raws.all_loaded))

            def step(i, ahead, now):
                if ahead:
                    pool.wait_ge(xT_made.sem, xT_made.at(i + 1, 0))
                    pool.tensor_copy(x_now[:], x[:, bass.ds((i + 1) * J, J), :]).then_inc(x_copied.sem, 1)
                if now:
                    for j in range(J):
                        pool.wait_ge(r2_ready.sem, r2_ready.at(i, j + 1))
                        pool.wait_ge(t2_ready.sem, t2_ready.at(i, 0))
                        pool.tensor_tensor(v2[:, j, :], r2[:, j % 2], g2[:], ALU.mult).then_inc(v2_ready.sem, 1)

            skewed(pool, step)

        @block.scalar
        def _(act):
            for made in (r_ready, sums2_ready, t2_ready, q2_act):
                made.grant(act)
            act.wait_ge(loaded.sem, loaded.at(0, raws.all_loaded))
            for raw, split in ((raws.cond, cond), (raws.down, down), (raws.up, up)):
                act.activation(split.high[:], raw[:], ACT.Copy).then_inc(split_high.sem, 1)
            act.wait_ge(constants_set.sem, constants_set.at(0, 3))

            def x_high(i):
                for half in range(2):
                    act.wait_ge(xT_made.sem, xT_made.at(i, half + 1))
                    act.activation(x_T.high[:, 2 * half:2 * half + 2].rearrange("p j c t -> p (j c t)"), banks[half],
                                   ACT.Copy).then_inc(xT_high.sem, 1)

            def low_rank_high(i):
                act.wait_ge(lr_masked.sem, lr_masked.at(i, 1))
                act.activation(lr.high[:, 0, :], low_rank[:], ACT.Copy).then_inc(lr_high.sem, 1)

            def dense(i, half):
                act.wait_ge(c_made.sem, c_made.at(i, half + 1))
                act.activation(c[:, 2 * half:2 * half + 2, :].rearrange("p j d -> p (j d)"), b_c, ACT.Copy).then_inc(c_copied.sem, 1)
                act.wait_ge(c_copied.sem, c_copied.at(i, half + 1))
                for j in (2 * half, 2 * half + 1):
                    last = act.activation(square1[:, j, :], c[:, j, :], ACT.Square, accum_out=sums[:, 0, j:j + 1])
                last.then_inc(rms_ready.sem, 1)

            def root(i):
                act.wait_ge(rms_ready.sem, rms_ready.at(i, 2))
                act.activation(rms[:, 0, :], sums[:, 0, :], ACT.Sqrt, bias=eps[:], scale=1.0 / D).then_inc(sqrt1.sem, 1)

            def relu(i, j):
                act.wait_ge(h_made.sem, h_made.at(i, j + 1))
                act.wait_ge(back1_ready.sem, back1_ready.at(i, 1))
                act.wait_ge(r2_ready.sem, r2_ready.at(i, j - 1))
                act.activation(r[:, j % 2], b_h(j), ACT.Relu, scale=back[:, 0, j:j + 1]).then_inc(r_ready.sem, 1)

            def sum_squares(i, j):
                act.wait_ge(r2_ready.sem, r2_ready.at(i, j + 1))
                act.activation(square[:, j % 2], r2[:, j % 2], ACT.Square, accum_out=sums[:, 1, j:j + 1]).then_inc(sums2_ready.sem, 1)

            def take(i, j):
                act.wait_ge(t2_made.sem, t2_made.at(i, j + 1))
                act.wait_ge(y_made.sem, y_made.at(i, j - 1))
                act.activation(q2[:, j % 2, 0:4, :].rearrange("p f t -> p (f t)"), b_t2(j, 0), ACT.Identity,
                               bias=magic_off[:]).then_inc(q2_act.sem, 1)

            def second(i):
                act.wait_ge(sums2_ready.sem, sums2_ready.at(i, J))
                act.activation(rms[:, 1, :], sums[:, 1, :], ACT.Sqrt, bias=eps[:], scale=1.0 / F2).then_inc(sqrt2.sem, 1)
                act.wait_ge(to_q2_ready.sem, to_q2_ready.at(i, 1))
                for j in range(J):
                    act.wait_ge(t2_made.sem, t2_made.at(i, j - 1))
                    act.activation(t2[:, j % 2], v2[:, j, :], ACT.Identity, bias=magic[:], scale=to_q[:, 1, j:j + 1])\
                        .then_inc(t2_ready.sem, 1)
                    if j > 0:
                        take(i, j - 1)
                take(i, J - 1)

            def whole_weights():
                act.wait_ge(w_scale_ready.sem, w_scale_ready.at(0, 2))
                for n, raw in enumerate((w1_raw, w2_raw)):
                    act.activation(raw[:], raw[:], ACT.Identity, bias=magic[:], scale=w_scale[:, n:n + 1]).then_inc(w_scaled.sem, 1)
                for n, (raw, whole) in enumerate(((w1_raw, w1_q), (w2_raw, w2_q))):
                    act.wait_ge(w_clipped.sem, w_clipped.at(0, n + 1))
                    act.activation(whole[:], raw[:], ACT.Identity, bias=magic_off[:]).then_inc(w_ready.sem, 1)

            def step(i, ahead, now):
                if now:
                    relu(i, 0)
                if ahead:
                    x_high(i + 1)
                if now:
                    relu(i, 1)
                    sum_squares(i, 0)
                if ahead:
                    low_rank_high(i + 1)
                if now:
                    relu(i, 2)
                if ahead:
                    dense(i + 1, 0)
                if now:
                    sum_squares(i, 1)
                    relu(i, 3)
                if ahead:
                    dense(i + 1, 1)
                    root(i + 1)
                if not now:
                    whole_weights()
                if now:
                    sum_squares(i, 2)
                    sum_squares(i, 3)
                    second(i)

            skewed(act, step)

        @block.vector
        def _(dve):
            first, second = Chain(dve, steps1.sem, 7), Chain(dve, steps2.sem, 5)
            for made in (r2_ready, q2_dve, q1_ready, y_added):
                made.grant(dve)
            dve.memset(magic[:], MAGIC).then_inc(constants_set.sem, 1)
            dve.memset(magic_off[:], -MAGIC).then_inc(constants_set.sem, 1)
            dve.memset(eps[:], 1e-6).then_inc(constants_set.sem, 1)
            dve.wait_ge(loaded.sem, loaded.at(0, raws.all_loaded))
            for n, (raw, split) in enumerate(((raws.cond, cond), (raws.down, down), (raws.up, up))):
                dve.wait_ge(split_high.sem, split_high.at(0, n + 1))
                dve.tensor_tensor(split.low[:], raw[:], split.high_read, ALU.subtract).then_inc(split_low.sem, 1)
            dve.tensor_copy(ids_f[:], raws.ids[:]).then_inc(own_ready.sem, 1)
            dve.wait_ge(own_ready.sem, own_ready.at(0, 1))
            dve.tensor_scalar(own[:], ids_f[:], const(consts, "adapter"), raws.scaling[:], ALU.is_equal, ALU.mult).then_inc(own_ready.sem, 1)
            dve.wait_ge(own_ready.sem, own_ready.at(0, 2))

            def absolute(n):
                dve.tensor_reduce(w_abs[:, n:n + 1], (w1_raw, w2_raw)[n][:].rearrange("p c f -> p (c f)"), AX, ALU.add,
                                  apply_absolute_value=True).then_inc(abs_ready.sem, 1)

            def weight_scales():
                dve.wait_ge(abs_summed.sem, abs_summed.at(0, 1))
                dve.tensor_scalar(w_mean[:], b_abs, 1.0 / (D * F2), 1e-5, ALU.mult, ALU.max).then_inc(w_scale_ready.sem, 1)
                dve.wait_ge(w_scale_ready.sem, w_scale_ready.at(0, 1))
                dve.reciprocal(w_scale[:], w_mean[:]).then_inc(w_scale_ready.sem, 1)

            def clip_weights():
                for n, raw in enumerate((w1_raw, w2_raw)):
                    dve.wait_ge(w_scaled.sem, w_scaled.at(0, n + 1))
                    dve.tensor_scalar(raw[:], raw[:], MAGIC + 1, MAGIC - 1, ALU.min, ALU.max).then_inc(w_clipped.sem, 1)

            def scales(i, n, chain, sqrt, back_ready):
                dve.wait_ge(sqrt.sem, sqrt.at(i, 1))
                dve.reciprocal(inv[:, n, :], rms[:, n, :]).then_inc(chain.next(), 1)
                dve.wait_ge(chain.sem, chain.count())
                dve.tensor_tensor(peak[:, n, :], peak[:, n, :], inv[:, n, :], ALU.mult).then_inc(chain.next(), 1)
                dve.wait_ge(chain.sem, chain.count())
                dve.tensor_scalar(peak[:, n, :], peak[:, n, :], 1e-5, None, ALU.max).then_inc(chain.next(), 1)
                dve.wait_ge(chain.sem, chain.count())
                dve.reciprocal(to_q[:, n, :], peak[:, n, :]).then_inc(chain.next(), 1)
                dve.tensor_scalar(back[:, n, :], peak[:, n, :], w_mean[:, n:n + 1], 1.0 / 127, ALU.mult, ALU.mult).then_inc(back_ready.sem, 1)
                dve.wait_ge(chain.sem, chain.count())
                return dve.scalar_tensor_tensor(to_q[:, n, :], to_q[:, n, :], 127.0, inv[:, n, :], ALU.mult, ALU.mult)

            def x_low(i):
                for half in range(2):
                    dve.wait_ge(xT_high.sem, xT_high.at(i, half + 1))
                    out = slice(2 * half, 2 * half + 2)
                    dve.tensor_tensor(x_T.low[:, out].rearrange("p j c t -> p (j c t)"), banks[half],
                                      x_T.high[:, out].rearrange("p j c t -> p (j c t)").bitcast(F32), ALU.subtract).then_inc(xT_low.sem, 1)

            def low_rank_own(i):
                dve.wait_ge(lr_made.sem, lr_made.at(i, 1))
                dve.tensor_tensor(low_rank[:].rearrange("p (b t) -> p b t", t=SEQ), b_lr.rearrange("p (b t) -> p b t", t=SEQ),
                                  spread(own[:, bass.ds(i * BSEQ, BSEQ)], 2, SEQ), ALU.mult).then_inc(lr_masked.sem, 1)

            def low_rank_low(i):
                dve.wait_ge(lr_high.sem, lr_high.at(i, 1))
                dve.tensor_tensor(lr.low[:, 0, :], low_rank[:], lr.high[:, 0, :].bitcast(F32), ALU.subtract).then_inc(lr_low.sem, 1)

            def gain(i, half):
                dve.wait_ge(c_copied.sem, c_copied.at(i, half + 1))
                out = slice(2 * half, 2 * half + 2)
                dve.tensor_tensor(v[:, out, :], c[:, out, :], spread(g1[:], 1, 2), ALU.mult).then_inc(v_ready.sem, 1)

            def peaks(i):
                first.start(i)
                dve.wait_ge(v_ready.sem, v_ready.at(i, 2))
                dve.tensor_reduce(peak[:, 0, :], v[:], AX, ALU.max, apply_absolute_value=True).then_inc(first.next(), 1)
                dve.wait_ge(first.sem, first.count())

            def quantise(i):
                scales(i, 0, first, sqrt1, back1_ready).then_inc(first.next(), 1)
                dve.wait_ge(first.sem, first.count())
                for j in range(J):
                    last = dve.tensor_scalar(v[:, j, :], v[:, j, :], to_q[:, 0, j:j + 1], MAGIC, ALU.mult, ALU.add)
                last.then_inc(first.next(), 1)
                dve.wait_ge(first.sem, first.count())
                dve.tensor_scalar(v[:], v[:], MAGIC + 127, MAGIC - 128, ALU.min, ALU.max).then_inc(t_ready.sem, 1)
                first.end()

            def integers(i):
                for half in range(2):
                    dve.wait_ge(t_made.sem, t_made.at(i, half + 1))
                    dve.tensor_scalar(q1[:, 2 * half:2 * half + 2].rearrange("p j c t -> p (j c t)"), banks[half], -MAGIC, None,
                                      ALU.add).then_inc(q1_ready.sem, 1)

            def square_relu(i, j):
                dve.wait_ge(r_ready.sem, r_ready.at(i, j + 1))
                dve.wait_ge(v2_ready.sem, v2_ready.at(i, j - 1))
                dve.wait_ge(sums2_ready.sem, sums2_ready.at(i, j - 1))
                dve.tensor_tensor(r2[:, j % 2], r[:, j % 2], r[:, j % 2], ALU.mult).then_inc(r2_ready.sem, 1)

            def peak2(i, j):
                dve.wait_ge(v2_ready.sem, v2_ready.at(i, j + 1))
                return dve.tensor_reduce(peak[:, 1, j:j + 1], v2[:, j, :], AX, ALU.max, apply_absolute_value=True)

            def take(i, j):
                dve.wait_ge(t2_made.sem, t2_made.at(i, j + 1))
                dve.tensor_scalar(q2[:, j % 2, 4:8, :].rearrange("p f t -> p (f t)"), b_t2(j, 1), -MAGIC, None,
                                  ALU.add).then_inc(q2_dve.sem, 1)

            def add(i, j):
                dve.wait_ge(y_made.sem, y_made.at(i, j + 1))
                dve.wait_ge(back2_ready.sem, back2_ready.at(i, 1))
                out = x[:, bass.ds(i * J + j, 1), :].rearrange("p o d -> p (o d)")
                dve.scalar_tensor_tensor(out, b_y[j % 2][:, 0:D], back[:, 1, j:j + 1], out, ALU.mult, ALU.add).then_inc(y_added.sem, 1)

            def step(i, ahead, now):
                if now:
                    square_relu(i, 0)
                if ahead:
                    x_low(i + 1)
                if now:
                    square_relu(i, 1)
                if ahead:
                    low_rank_own(i + 1)
                if now:
                    second.start(i)
                    peak2(i, 0)
                if not now:
                    absolute(0)
                if ahead:
                    low_rank_low(i + 1)
                if not now:
                    absolute(1)
                if now:
                    square_relu(i, 2)
                    peak2(i, 1)
                if ahead:
                    gain(i + 1, 0)
                if now:
                    square_relu(i, 3)
                if ahead:
                    gain(i + 1, 1)
                    peaks(i + 1)
                if not now:
                    weight_scales()
                if now:
                    peak2(i, 2)
                if ahead:
                    quantise(i + 1)
                if now:
                    peak2(i, 3).then_inc(second.next(), 1)
                    dve.wait_ge(second.sem, second.count())
                    scales(i, 1, second, sqrt2, back2_ready).then_inc(to_q2_ready.sem, 1)
                if ahead:
                    integers(i + 1)
                if not now:
                    clip_weights()
                if now:
                    for j in range(J + 2):
                        if j < J:
                            dve.wait_ge(t2_ready.sem, t2_ready.at(i, j + 1))
                            dve.tensor_scalar(t2[:, j % 2], t2[:, j % 2], MAGIC + 127, MAGIC - 128, ALU.min, ALU.max).then_inc(t2_clipped.sem, 1)
                        if 1 <= j <= J:
                            take(i, j - 1)
                        if j >= 2:
                            add(i, j - 2)
                    second.end()

            skewed(dve, step)

        @block.tensor
        def _(pe):
            for made in (xT_made, c_made, h_made, t2_made, y_made):
                made.grant(pe)
            pe.wait_ge(split_low.sem, split_low.at(0, 3))

            def turn_x(i):
                pe.wait_ge(x_copied.sem, x_copied.at(i, 1))
                pe.wait_ge(q1_ready.sem, q1_ready.at(i, 0))
                for half in range(2):
                    for n in range(2 * DC):
                        j, k = 2 * half + n // DC, n % DC
                        last = pe.transpose(banks[half][:, n * P:(n + 1) * P], x_now[:, j, k * P:(k + 1) * P], ident)
                    last.then_inc(xT_made.sem, 1)

            def adapters_down(i):
                pe.wait_ge(xT_low.sem, xT_low.at(i, 2))
                pe.wait_ge(y_added.sem, y_added.at(i - 1, 0))
                product(pe, b_lr, down, x_T, range(DC), lambda a, k: a[:, k, :], lambda a, k: a[:, :, k, :]).then_inc(lr_made.sem, 1)

            def dense(i, half):
                if half:
                    pe.wait_ge(c_copied.sem, c_copied.at(i, half))
                for n in range(2):
                    out, j = b_c[:, n * D:(n + 1) * D], 2 * half + n
                    product(pe, out, x_T, cond, range(DC), lambda a, k: a[:, j, k, :], lambda a, k: a[:, k, :], stop=False)
                    pe.wait_ge(lr_low.sem, lr_low.at(i, 1))
                    last = product(pe, out, lr, up, [0], lambda a, k: a[:, k, j * P:(j + 1) * P], lambda a, k: a[:, k, :], start=False)
                last.then_inc(c_made.sem, 1)

            def turn_v(i):
                pe.wait_ge(t_ready.sem, t_ready.at(i, 1))
                for half in range(2):
                    for n in range(2 * DC):
                        j, k = 2 * half + n // DC, n % DC
                        last = pe.transpose(banks[half][:, n * P:(n + 1) * P], v[:, j, k * P:(k + 1) * P], ident)
                    last.then_inc(t_made.sem, 1)

            def hidden(i, j):
                pe.wait_ge(q1_ready.sem, q1_ready.at(i, j // 2 + 1))
                pe.wait_ge(r_ready.sem, r_ready.at(i, j - 1))
                pe.wait_ge(q2_act.sem, q2_act.at(i, 0))
                pe.wait_ge(q2_dve.sem, q2_dve.at(i, 0))
                for half in range(2):
                    for k in range(DC):
                        last = pe.matmul(b_h(j)[:, half * 512:(half + 1) * 512], q1[:, j, k, :], w1_q[:, k, half * 512:(half + 1) * 512],
                                         start=(k == 0), stop=(k == DC - 1))
                last.then_inc(h_made.sem, 1)

            def turn_t2(i, j):
                pe.wait_ge(t2_clipped.sem, t2_clipped.at(i, j + 1))
                pe.wait_ge(q2_act.sem, q2_act.at(i, j - 1))
                pe.wait_ge(q2_dve.sem, q2_dve.at(i, j - 1))
                for f in range(FC):
                    last = pe.transpose(b_t2(j, f // 4)[:, (f % 4) * P:(f % 4 + 1) * P], t2[:, j % 2, f * P:(f + 1) * P], ident)
                last.then_inc(t2_made.sem, 1)

            def result(i, j):
                pe.wait_ge(q2_act.sem, q2_act.at(i, j + 1))
                pe.wait_ge(q2_dve.sem, q2_dve.at(i, j + 1))
                pe.wait_ge(y_added.sem, y_added.at(i, j - 1))
                for f in range(FC):
                    last = pe.matmul(b_y[j % 2][:, 0:D], q2[:, j % 2, f, :], w2_q[:, f, :], start=(f == 0), stop=(f == FC - 1))
                last.then_inc(y_made.sem, 1)

            def step(i, ahead, now):
                if now:
                    hidden(i, 0)
                    hidden(i, 1)
                if ahead:
                    turn_x(i + 1)
                if now:
                    hidden(i, 2)
                if ahead:
                    adapters_down(i + 1)
                if now:
                    hidden(i, 3)
                if ahead:
                    dense(i + 1, 0)
                    dense(i + 1, 1)
                if not now:
                    pe.wait_ge(abs_ready.sem, abs_ready.at(0, 2))
                    pe.matmul(b_abs, const(consts, "ones"), w_abs[:], start=True, stop=True).then_inc(abs_summed.sem, 1)
                if ahead:
                    turn_v(i + 1)
                    pe.wait_ge(c_copied.sem, c_copied.at(i + 1, 2))
                if not now:
                    pe.wait_ge(w_ready.sem, w_ready.at(0, 2))
                if now:
                    for j in range(J + 1):
                        if j < J:
                            turn_t2(i, j)
                        if j > 0:
                            result(i, j - 1)

            skewed(pe, step)


def position_mix_phase(nc, sems, io, psum, consts, mixes, x, xT, combineT, load_next):
    J = BTILES
    with ExitStack() as ctx:
        def sb(name, shape, dt=F32):
            return ctx.enter_context(nc.sbuf_tensor("m_" + name, shape, dt))

        def sig(name, per=1, free=0):
            return Signal(sems.new("m_" + name), per, free)

        mix_wide = sb("mix_wide", [P, TILES, TSEQ, SEQ])
        mix = [Split(sb, f"mix{u}", [P, J, P]) for u in range(2)]
        x_now = [Split(sb, f"x_now{u}", [P, J, D]) for u in range(2)]
        gate_raw, gate = sb("gate_raw", [P, DC, E3 + 1]), Split(sb, "gate", [P, DC, E3 + 1])
        gate_b, biases = sb("gate_b", [P, E3]), sb("biases", [P, E3])
        logitsT = sb("logitsT", [E3 + 1, T])
        logits = sb("logits", [P, TILES, E3])
        peak = sb("peak", [P, TILES])
        total = sb("total", [P, TILES])
        prob = sb("prob", [P, TILES, E3 + 1])
        biased = sb("biased", [P, TILES, E3 + 1])
        top = sb("top", [P, TILES, 8])
        top_at = sb("top_at", [P, TILES, 8], U32)
        top_e = sb("top_e", [P, TILES, K3])
        hot = sb("hot", [P, TILES, K3, E3 + 1])
        hot_prob = sb("hot_prob", [P, TILES, K3, E3 + 1])
        top_prob = sb("top_prob", [P, TILES, K3])
        comb = sb("comb", [P, E3 + 1, TILES])
        combT = sb("combT", [P, P])

        loaded = sig("loaded")
        set_ = sig("set")
        gate_high = sig("gate_high")
        mix_ready = sig("mix_ready")
        mix_high, mix_low = sig("mix_high", 2), sig("mix_low", 2)
        x_high, x_low = sig("x_high", 2), sig("x_low", 2)
        c_made = sig("c_made", 4, 4)
        c_high, c_low = sig("c_high", 4), sig("c_low", 4, 4)
        logitsT_made, logitsT_ready, logits_made = sig("logitsT_made", 2), sig("logitsT_ready", 2, 2), sig("logits_made")
        act_passed = sig("act_passed")
        shifted, exped = sig("shifted"), sig("exped")
        comb_ready, combT_made, combT_ready, stored = sig("comb_ready"), sig("combT_made"), sig("combT_ready"), sig("stored")
        steps = sig("steps")
        dve_passed = sig("dve_passed")
        block = ctx.enter_context(nc.Block())
        ident, quad, count = (const(consts, n) for n in ("ident", "quad", "count"))
        banks = [psum[:, n, :] for n in range(8)]
        b_gT, b_g, b_t = banks[4:6], banks[6], banks[7]

        @block.sync
        def _(sp):
            sp.wait_ge(set_.sem, set_.at(0, 1))
            sp.dma_start(gate_raw[:, :, 0:E3], io["L3_ffn_gate_w"].rearrange("(c p) e -> p c e", p=P)).then_inc(loaded.sem, 16)
            sp.dma_start(gate_b[:], io["L3_ffn_gate_b"].partition_broadcast(P)).then_inc(loaded.sem, 16)
            sp.dma_start(biases[:], io["L3_ffn_biases"].partition_broadcast(P)).then_inc(loaded.sem, 16)
            load_next(sp)
            sp.wait_ge(combT_ready.sem, combT_ready.at(0, 1))
            sp.dma_start(combineT.rearrange("e (n t) -> (e n) t", t=P), combT[:]).then_inc(stored.sem, 16)
            sp.wait_ge(stored.sem, stored.at(0, 16))

        @block.scalar
        def _(act):
            act.wait_ge(loaded.sem, loaded.at(0, 48))
            act.activation(gate.high[:], gate_raw[:], ACT.Copy).then_inc(gate_high.sem, 1)
            act.wait_ge(mix_ready.sem, mix_ready.at(0, 1))
            logitsT_ready.grant(act)
            def split(i, u):
                act.wait_ge(c_made.sem, c_made.at(i, 2 * u - 2))
                act.sem_inc(act_passed.sem, 1)
                act.activation(x_now[u].high[:], x[:, bass.ds(i * 2 * J + u * J, J), :], ACT.Copy).then_inc(x_high.sem, 1)
                act.activation(mix[u].high[:], mix_wide[:, bass.ds(i * 2 * J + u * J, J)].rearrange("p n b t -> p n (b t)"),
                               ACT.Copy).then_inc(mix_high.sem, 1)

            def keep(i, u):
                for k in range(DC):
                    act.wait_ge(c_made.sem, c_made.at(i, 2 * u + k + 1))
                    act.sem_inc(act_passed.sem, 1)
                    act.activation(xT.high[:, k, bass.ds(i * 2 * BLOCK + u * BLOCK, BLOCK)], banks[2 * u + k], ACT.Copy).then_inc(c_high.sem, 1)

            def keep_logits(i, u):
                act.wait_ge(logitsT_made.sem, logitsT_made.at(i, u + 1))
                act.sem_inc(act_passed.sem, 1)
                act.activation(logitsT[:, bass.ds(i * 2 * BLOCK + u * BLOCK, BLOCK)], b_gT[u][0:E3 + 1, :], ACT.Copy).then_inc(logitsT_ready.sem, 1)

            with act.Fori(0, BLOCKS // 2) as i:
                split(i, 0)
                split(i, 1)
                keep(i, 0)
                keep(i, 1)
                keep_logits(i, 0)
                keep_logits(i, 1)
            act.wait_ge(shifted.sem, shifted.at(0, 1))
            act.activation(logits[:], logits[:], ACT.Exp).then_inc(exped.sem, 1)
            act.wait_ge(combT_made.sem, combT_made.at(0, 1))
            act.activation(combT[:], b_t[:, 0:P], ACT.Copy).then_inc(combT_ready.sem, 1)

        @block.vector
        def _(dve):
            c_low.grant(dve)
            dve.memset(gate_raw[:], 0.0).then_inc(set_.sem, 1)
            dve.memset(prob[:], 0.0).then_inc(set_.sem, 1)
            dve.memset(biased[:], -1e30).then_inc(set_.sem, 1)
            dve.memset(comb[:], 1.0).then_inc(set_.sem, 1)
            dve.tensor_tensor(mix_wide[:], spread(mixes[:], 2, TSEQ), spread(spread(quad, 2, SEQ), 1, TILES), ALU.mult).then_inc(mix_ready.sem, 1)
            dve.wait_ge(gate_high.sem, gate_high.at(0, 1))
            dve.tensor_tensor(gate.low[:], gate_raw[:], gate.high_read, ALU.subtract).then_inc(gate_high.sem, 1)
            dve.wait_ge(mix_ready.sem, mix_ready.at(0, 1))
            def split(i, u):
                dve.wait_ge(x_high.sem, x_high.at(i, u + 1))
                dve.tensor_tensor(x_now[u].low[:], x[:, bass.ds(i * 2 * J + u * J, J), :], x_now[u].high_read, ALU.subtract).then_inc(x_low.sem, 1)
                dve.wait_ge(mix_high.sem, mix_high.at(i, u + 1))
                dve.tensor_tensor(mix[u].low[:], mix_wide[:, bass.ds(i * 2 * J + u * J, J)].rearrange("p n b t -> p n (b t)"),
                                  mix[u].high_read, ALU.subtract).then_inc(mix_low.sem, 1)

            def keep(i, u):
                for k in range(DC):
                    at = bass.ds(i * 2 * BLOCK + u * BLOCK, BLOCK)
                    dve.wait_ge(c_high.sem, c_high.at(i, 2 * u + k + 1))
                    dve.tensor_tensor(xT.low[:, k, at], banks[2 * u + k], xT.high[:, k, at].bitcast(F32), ALU.subtract).then_inc(c_low.sem, 1)

            with dve.Fori(0, BLOCKS // 2) as i:
                split(i, 0)
                split(i, 1)
                keep(i, 0)
                keep(i, 1)

            chain = Chain(dve, steps.sem, 0)
            dve.wait_ge(logits_made.sem, logits_made.at(0, 1))
            dve.wait_ge(set_.sem, set_.at(0, 4))
            dve.tensor_tensor(logits[:], b_g[:, 0:TILES * (E3 + 1)].rearrange("p (n e) -> p n e", e=E3 + 1)[:, :, 0:E3],
                                        spread(gate_b[:], 1, TILES), ALU.add).then_inc(chain.next(), 1)
            dve.wait_ge(chain.sem, chain.count())
            dve.tensor_reduce(peak[:], logits[:], AX, ALU.max).then_inc(chain.next(), 1)
            dve.wait_ge(chain.sem, chain.count())
            dve.tensor_tensor(logits[:], logits[:], spread(peak[:], 2, E3), ALU.subtract).then_inc(shifted.sem, 1)
            dve.wait_ge(exped.sem, exped.at(0, 1))
            dve.tensor_reduce(total[:], logits[:], AX, ALU.add).then_inc(chain.next(), 1)
            dve.wait_ge(chain.sem, chain.count())
            dve.reciprocal(total[:], total[:]).then_inc(chain.next(), 1)
            dve.wait_ge(chain.sem, chain.count())
            dve.tensor_tensor(prob[:, :, 0:E3], logits[:], spread(total[:], 2, E3), ALU.mult).then_inc(chain.next(), 1)
            dve.wait_ge(chain.sem, chain.count())
            dve.tensor_tensor(biased[:, :, 0:E3], prob[:, :, 0:E3], spread(biases[:], 1, TILES), ALU.add).then_inc(chain.next(), 1)
            dve.wait_ge(chain.sem, chain.count())
            for n in range(TILES):
                last = dve.max(top[:, n, :], biased[:, n, :])
            last.then_inc(chain.next(), 1)
            dve.wait_ge(chain.sem, chain.count())
            for n in range(TILES):
                last = dve.max_index(top_at[:, n, :], top[:, n, :], biased[:, n, :])
            last.then_inc(chain.next(), 1)
            dve.wait_ge(chain.sem, chain.count())
            dve.tensor_copy(top_e[:], top_at[:, :, 0:K3]).then_inc(chain.next(), 1)
            dve.wait_ge(chain.sem, chain.count())
            dve.tensor_tensor(hot[:].rearrange("p n k e -> p (n k) e"), spread(count[:, 0:E3 + 1], 1, TILES * K3),
                                        spread(top_e[:].rearrange("p n k -> p (n k)"), 2, E3 + 1), ALU.is_equal).then_inc(chain.next(), 1)
            dve.wait_ge(chain.sem, chain.count())
            dve.tensor_tensor(hot_prob[:], hot[:], spread(prob[:], 2, K3), ALU.mult).then_inc(chain.next(), 1)
            dve.wait_ge(chain.sem, chain.count())
            dve.tensor_reduce(top_prob[:], hot_prob[:], AX, ALU.add).then_inc(chain.next(), 1)
            dve.wait_ge(chain.sem, chain.count())
            dve.tensor_reduce(total[:], top_prob[:], AX, ALU.add).then_inc(chain.next(), 1)
            dve.wait_ge(chain.sem, chain.count())
            dve.reciprocal(total[:], total[:]).then_inc(chain.next(), 1)
            dve.wait_ge(chain.sem, chain.count())
            dve.tensor_tensor(top_prob[:], top_prob[:], spread(total[:], 2, K3), ALU.mult).then_inc(chain.next(), 1)
            dve.wait_ge(chain.sem, chain.count())
            dve.tensor_tensor(hot_prob[:].rearrange("p n k e -> p (n k) e"), hot[:].rearrange("p n k e -> p (n k) e"),
                                        spread(top_prob[:].rearrange("p n k -> p (n k)"), 2, E3 + 1), ALU.mult).then_inc(chain.next(), 1)
            dve.wait_ge(chain.sem, chain.count())
            dve.tensor_reduce(comb[:, 0:E3, :].rearrange("p e n -> p n e"), hot_prob[:, :, :, 0:E3].rearrange("p n k e -> p n e k"),
                              AX, ALU.add).then_inc(comb_ready.sem, 1)

        @block.tensor
        def _(pe):
            c_made.grant(pe)
            pe.wait_ge(gate_high.sem, gate_high.at(0, 2))

            def mixed(i, u):
                pe.wait_ge(x_low.sem, x_low.at(i, u + 1))
                pe.wait_ge(mix_low.sem, mix_low.at(i, u + 1))
                pe.wait_ge(c_low.sem, c_low.at(i, 2 * u - 2))
                for k in range(DC):
                    for j in range(J):
                        last = product(pe, banks[2 * u + k][:, j * P:(j + 1) * P], x_now[u], mix[u], [j],
                                       lambda a, jj: a[:, jj, k * P:(k + 1) * P], lambda a, jj: a[:, jj, :])
                    last.then_inc(c_made.sem, 1)

            def router(i, u):
                pe.wait_ge(c_low.sem, c_low.at(i, 2 * u + 2))
                pe.wait_ge(logitsT_ready.sem, logitsT_ready.at(i, u - 1))
                product(pe, b_gT[u][0:E3 + 1, :], gate, xT, range(DC), lambda a, k: a[:, k, :],
                        lambda a, k: a[:, k, bass.ds(i * 2 * BLOCK + u * BLOCK, BLOCK)]).then_inc(logitsT_made.sem, 1)

            with pe.Fori(0, BLOCKS // 2) as i:
                mixed(i, 0)
                mixed(i, 1)
                router(i, 0)
                router(i, 1)
            pe.wait_ge(logitsT_ready.sem, logitsT_ready.at(BLOCKS // 2, 0))
            for n in range(TILES):
                last = pe.transpose(b_g[:, n * (E3 + 1):(n + 1) * (E3 + 1)], logitsT[:, n * P:(n + 1) * P], ident[0:E3 + 1, 0:E3 + 1])
            last.then_inc(logits_made.sem, 1)
            pe.wait_ge(comb_ready.sem, comb_ready.at(0, 1))
            pe.transpose(b_t[:, 0:P], comb[:].rearrange("p e n -> p (e n)"), ident).then_inc(combT_made.sem, 1)


def build_program(nc, names, args, out):
    io = dict(zip(names, args))
    with ExitStack() as ctx:
        def sb(name, shape, dt=F32):
            return ctx.enter_context(nc.sbuf_tensor(name, shape, dt))

        def dram(name, shape):
            return nc.dram_tensor(name, shape, F32, kind="Internal").ap()

        rows, rows_out = dram("expert_rows", [E0 * CAP, D]), dram("expert_results", [E0 * CAP, D])
        combine1T, combine3T = dram("combine1T", [E1, T]), dram("combine3T", [E3 + 1, T])
        psum = ctx.enter_context(nc.psum_tensor("psum", [P, 8, 512], F32))
        consts = sb("consts", [P, CONSTANTS.shape[1]])
        mixes = sb("mixes", [P, TILES, SEQ])
        slots, weights_eff = sb("slots", [P, TILES, 2], U32), sb("weights_eff", [P, TILES, 2])
        sems, held = Semaphores(nc), Semaphores(nc)
        x = sb("residual", [P, TILES, D])

        def right(stack):
            return lambda name, shape, dt=F32: stack.enter_context(nc.sbuf_tensor(name, shape, dt, side="right"))

        def left(stack):
            return lambda name, shape, dt=F32: stack.enter_context(nc.sbuf_tensor(name, shape, dt))

        with ExitStack() as for_chosen:
            with ExitStack() as for_capacity:
                capacity = CapacityWeights(right(for_capacity), sems, io)
                attention_phase(nc, sems, io, psum, consts, slots, weights_eff, mixes, rows, capacity.load)
                chosen = ChosenInputs(left(for_chosen), held, io, x)
                capacity_experts_phase(nc, sems, psum, consts, capacity, rows, rows_out, chosen.load)
            sems.clear()
            xT = Split(right(ctx), "inputs", [P, DC, T])
            experts1 = ExpertWeights(right(ctx), held, "g", io["gate_1"], io["up_1"], io["down_1"], 3)
            chosen_layer_phase(nc, sems, io, psum, consts, chosen, slots, weights_eff, rows_out, x, xT, combine1T, experts1.load)
        sems.clear()
        quantised = QuantisedInputs(sb, sems, io)
        gated_experts_phase(nc, sems, "g", psum, experts1, combine1T, F1, E1, x, xT, quantised.load)
        quantised_phase(nc, sems, psum, consts, quantised, x)
        experts3 = ExpertWeights(sb, sems, "s", io["gate_3"], io["up_3"], io["down_3"], 2)
        position_mix_phase(nc, sems, io, psum, consts, mixes, x, xT, combine3T, experts3.load)
        gated_experts_phase(nc, sems, "s", psum, experts3, combine3T, F3, E3 + 1, x, xT,
                            out=out.rearrange("s t d -> (s t) d"))


def laid_out(inputs):
    take = {k: np.asarray(v) for k, v in inputs.items()}
    x = take["x"].reshape(T, D)
    swap = {
        "constants": CONSTANTS,
        "x": x,
        "xT": x.T,
        "w_attention": np.stack([take["L0_cond_W" + n].T for n in "qkvo"]),
        "b1": take["L0_ffn_b1"].reshape(E0, F0 // P, P).transpose(2, 0, 1).reshape(P, -1),
        "gate1": take["L1_ffn_gate_weight"].T,
        "gate_1": take["L1_ffn_gate_up_proj"][:, :F1].transpose(2, 0, 1).reshape(D, -1),
        "up_1": take["L1_ffn_gate_up_proj"][:, F1:].transpose(2, 0, 1).reshape(D, -1),
        "down_1": take["L1_ffn_down_proj"].transpose(0, 2, 1).reshape(-1, D),
        "quant_w1": take["L2_ffn_w1"].T,
        "quant_w2": take["L2_ffn_w2"].T,
        "cond2": take["L2_cond_W"].T,
        "adapter_down": take["L2_cond_A"].reshape(P, D).T,
        "adapter_up": take["L2_cond_Bm"].transpose(0, 2, 1).reshape(P, D),
        "mix_rows": take["L3_cond_weights"].reshape(S3 * SEQ, SEQ),
        "gate_3": np.concatenate([take["L3_ffn_W1"], take["L3_ffn_Ws1"][None]]).transpose(1, 0, 2).reshape(D, -1),
        "up_3": np.concatenate([take["L3_ffn_Wg"], take["L3_ffn_Wsg"][None]]).transpose(1, 0, 2).reshape(D, -1),
        "down_3": np.concatenate([take["L3_ffn_W2"], take["L3_ffn_Ws2"][None]]).reshape(-1, D),
    }
    same = ("cond_1", "L0_ffn_gating_w", "L0_ffn_w1", "L0_ffn_w2", "L0_ffn_b2", "itok_B_0_15", "itok_B_0_6", "itok_B_1_198",
            "L1_cond_W", "L1_cond_b", "L1_ffn_similarity", "L2_ffn_g1", "L2_ffn_g2", "L2_cond_scalings",
            "L3_ffn_gate_w", "L3_ffn_gate_b", "L3_ffn_biases")
    swap.update({name: take[name] for name in same})
    return {name: np.ascontiguousarray(a) for name, a in swap.items()}


def kernel(**inputs):
    import concourse.bacc as bacc
    from concourse.bass_utils import run_bass_kernel_spmd

    nc = bacc.Bacc("TRN2", target_bir_lowering=False, num_devices=1)
    arrays = laid_out(inputs)
    args = [nc.dram_tensor(name, a.shape, mybir.dt.from_np(a.dtype), kind="ExternalInput").ap() for name, a in arrays.items()]
    out = nc.dram_tensor("out", (SEQS, SEQ, D), F32, kind="ExternalOutput").ap()
    build_program(nc, list(arrays), args, out)
    result = run_bass_kernel_spmd(nc, [arrays], core_ids=[0])
    return result.results[0]["out"]
```
